# Optimizing a Trainium2 kernel written in Bass

```python
import numpy as np
import jax
import jax.numpy as jnp

def _softmax(x, axis=-1):
    return jax.nn.softmax(x, axis=axis)

def _gelu(x):
    return jax.nn.gelu(x, approximate=True)

def _silu(x):
    return jax.nn.silu(x)

def _sigmoid(x):
    return jax.nn.sigmoid(x)

def _layernorm(x, axis=-1, eps=1e-05):
    m = jnp.mean(x, axis=axis, keepdims=True)
    v = jnp.var(x, axis=axis, keepdims=True)
    return (x - m) / jnp.sqrt(v + eps)

def _scatter_add(tgt, idx, src, axis=0):
    return tgt.at[idx].add(src)

def _segment_sum(src, seg, n):
    return jax.ops.segment_sum(src, seg, n)
kernel_name = 'mk_decoder_postln_d1_seqx_r8_a974d6'

def setup_inputs(seed: int=0):
    np.random.seed(seed)
    _w = jnp.asarray

    def _rec_inputs():
        import jax
        import jax.numpy as jnp
        _rk = jax.random.key(seed)
        x = 4.136e-05 + 0.9999 * jax.random.normal(jax.random.fold_in(_rk, 1), (4, 256, 256), jnp.float32)
        _lenS = 256 - jax.random.randint(jax.random.fold_in(_rk, 7), (4,), 0, max(1, 256 // 4) + 1, jnp.int32)
        _lenS2 = 256 - jax.random.randint(jax.random.fold_in(_rk, 8), (4,), 0, max(1, 256 // 4) + 1, jnp.int32)
        _ctx_1024P = jax.random.normal(jax.random.fold_in(_rk, 11), (4, 16, 128), jnp.float32)
        _ctx_1024c = jax.random.dirichlet(jax.random.fold_in(_rk, 511), 0.3 * jnp.ones((16,), jnp.float32), (4, 256))
        _ctx_1024t = jnp.einsum('bsk,bkd->bsd', _ctx_1024c, _ctx_1024P)
        _ctx_1024t = _ctx_1024t * jax.lax.rsqrt(jnp.mean(jnp.square(_ctx_1024t)) + 1e-12) * 0.953939
        ctx_1024 = -0.000292821 + 1.00034 * (_ctx_1024t + 0.3 * jax.random.normal(jax.random.fold_in(_rk, 611), (4, 256, 128), jnp.float32))
        return (x, ctx_1024)
    x, ctx_1024 = _rec_inputs()

    def _L0_attn_setup():
        import jax, jax.numpy as jnp
        import numpy as np
        B, L, D, H = (2, 256, 256, 16)
        DH = D // H
        EPS = 1e-05

        def _delta_rule(q, k, v, beta):

            def step(S, inp):
                qt, kt, vt, bt = inp
                v_pred = jnp.einsum('bhk,bhkv->bhv', kt, S)
                delta = (vt - v_pred) * bt[..., None]
                S = S + kt[..., None] * delta[:, :, None, :]
                ot = jnp.einsum('bhk,bhkv->bhv', qt, S)
                return (S, ot)
            xs = (q.transpose(2, 0, 1, 3), k.transpose(2, 0, 1, 3), v.transpose(2, 0, 1, 3), beta.transpose(2, 0, 1))
            S0 = jnp.zeros(q.shape[:2] + (q.shape[-1], v.shape[-1]), q.dtype)
            _, o = jax.lax.scan(step, S0, xs)
            return o.transpose(1, 2, 0, 3)
        key = jax.random.key(seed)
        ks = jax.random.split(key, 6)
        s = 0.02
        return {'hidden_states': jax.random.normal(ks[0], (B, L, D), jnp.float32), 'Wq': jax.random.normal(ks[1], (D, D), jnp.float32) * s, 'Wk': jax.random.normal(ks[2], (D, D), jnp.float32) * s, 'Wv': jax.random.normal(ks[3], (D, D), jnp.float32) * s, 'Wb': jax.random.normal(ks[4], (D, H), jnp.float32) * s, 'o_norm_weight': jnp.ones((DH,), jnp.float32), 'Wo': jax.random.normal(ks[5], (D, D), jnp.float32) * s}
    _L0_attn_all = _L0_attn_setup()
    _L0_attn_in = {k: v for k, v in _L0_attn_all.items() if k in ('Wq', 'Wk', 'Wv', 'Wb', 'o_norm_weight', 'Wo')}
    del _L0_attn_all

    def _L0_xattn_setup():
        import jax, jax.numpy as jnp
        import numpy as np
        import math
        B, L, DM = (2, 256, 128)
        DS, DC, EXP = (16, 4, 2)
        DI = EXP * DM
        DR = math.ceil(DM / 16)
        DT_MIN, DT_MAX, DT_FLOOR = (0.001, 0.1, 0.0001)

        def _ssm_forward(hidden_states, z, in_proj_w, conv_w, conv_b, x_proj_w, dt_proj_w, dt_proj_b, A_log, D):
            b = hidden_states.shape[0]
            x = jnp.einsum('ed,bld->bel', in_proj_w, hidden_states)
            xp = jnp.pad(x, ((0, 0), (0, 0), (DC - 1, 0)))
            xc = jax.lax.conv_general_dilated(xp, conv_w[:, None, :], window_strides=(1,), padding='VALID', dimension_numbers=('NCH', 'OIH', 'NCH'), feature_group_count=DI)
            u = jax.nn.silu(xc + conv_b[None, :, None])
            x_dbl = jnp.einsum('ke,bel->bkl', x_proj_w, u)
            dt_lo = x_dbl[:, :DR]
            Bm = x_dbl[:, DR:DR + DS]
            Cm = x_dbl[:, DR + DS:]
            delta = jax.nn.softplus(jnp.einsum('er,brl->bel', dt_proj_w, dt_lo) + dt_proj_b[None, :, None])
            A = -jnp.exp(A_log)

            def step(state, xs):
                d_t, B_t, C_t, u_t = xs
                dA = jnp.exp(d_t[..., None] * A)
                state = state * dA + (d_t * u_t)[..., None] * B_t[:, None, :]
                y_t = jnp.einsum('ben,bn->be', state, C_t)
                return (state, y_t)
            xs = (jnp.moveaxis(delta, -1, 0), jnp.moveaxis(Bm, -1, 0), jnp.moveaxis(Cm, -1, 0), jnp.moveaxis(u, -1, 0))
            state0 = jnp.zeros((b, DI, DS), delta.dtype)
            _, ys = jax.lax.scan(step, state0, xs)
            y = jnp.moveaxis(ys, 0, -1)
            y = y + D[None, :, None] * u
            y = y * jax.nn.silu(z)
            return jnp.swapaxes(y, 1, 2)
        key = jax.random.key(seed)
        ks = jax.random.split(key, 8)
        hidden_states = jax.random.normal(ks[0], (B, L, DM), jnp.float32)
        z = jax.random.normal(ks[1], (B, DI, L), jnp.float32)
        in_proj_w = jax.random.normal(ks[2], (DI, DM), jnp.float32) * DM ** (-0.5)
        conv_w = jax.random.normal(ks[3], (DI, DC), jnp.float32) * DC ** (-0.5)
        conv_b = jnp.zeros((DI,), jnp.float32)
        x_proj_w = jax.random.normal(ks[4], (DR + 2 * DS, DI), jnp.float32) * DI ** (-0.5)
        dt_std = DR ** (-0.5)
        dt_proj_w = jax.random.uniform(ks[5], (DI, DR), jnp.float32, -dt_std, dt_std)
        dt = jnp.exp(jax.random.uniform(ks[6], (DI,), jnp.float32) * (math.log(DT_MAX) - math.log(DT_MIN)) + math.log(DT_MIN))
        dt = jnp.clip(dt, DT_FLOOR)
        dt_proj_b = dt + jnp.log(-jnp.expm1(-dt))
        A_log = jnp.log(jnp.broadcast_to(jnp.arange(1, DS + 1, dtype=jnp.float32), (DI, DS)))
        D = jnp.ones((DI,), jnp.float32)
        return dict(hidden_states=hidden_states, z=z, in_proj_w=in_proj_w, conv_w=conv_w, conv_b=conv_b, x_proj_w=x_proj_w, dt_proj_w=dt_proj_w, dt_proj_b=dt_proj_b, A_log=A_log, D=D)
    _L0_xattn_all = _L0_xattn_setup()
    _L0_xattn_in = {k: v for k, v in _L0_xattn_all.items() if k in ('in_proj_w', 'conv_w', 'conv_b', 'x_proj_w', 'dt_proj_w', 'dt_proj_b', 'A_log', 'D')}
    del _L0_xattn_all

    def _L0_ffn_setup():
        import jax, jax.numpy as jnp
        import numpy as np
        D_MODEL, D_FF, NS, NR, KR = (256, 176, 2, 16, 4)
        B, S = (4, 256)

        def _moe_forward(u, shared_w1, shared_b1, shared_w2, shared_b2, routed_w1, routed_b1, routed_w2, routed_b2, centroids, bias):
            b, s, d = u.shape
            flat = u.reshape(-1, d)
            T = flat.shape[0]
            h = jax.nn.relu(jnp.einsum('td,ndf->ntf', flat, shared_w1) + shared_b1[:, None, :])
            shared_out = jnp.einsum('ntf,nfd->td', h, shared_w2) + shared_b2.sum(0)
            out = flat + shared_out
            scores = jax.nn.sigmoid(flat @ centroids.T) + bias
            vals, idx = jax.lax.top_k(scores, KR)
            gating = jnp.zeros_like(scores).at[jnp.arange(T)[:, None], idx].set(vals)
            gating = gating / jnp.clip(gating.sum(-1, keepdims=True), 1e-08)

            def step(acc, ew):
                w1, b1, w2, b2, g = ew
                hj = jax.nn.relu(flat @ w1 + b1)
                yj = hj @ w2 + b2
                return (acc + yj * g[:, None], None)
            rout0 = jnp.zeros_like(flat)
            rout, _ = jax.lax.scan(step, rout0, (routed_w1, routed_b1, routed_w2, routed_b2, gating.T))
            return (out + rout).reshape(b, s, d)
        key = jax.random.key(seed)
        ks = jax.random.split(key, 10)
        s1 = 1.0 / np.sqrt(D_MODEL)
        s2 = 1.0 / np.sqrt(D_FF)
        return {'u': jax.random.normal(ks[0], (B, S, D_MODEL), dtype=jnp.float32), 'shared_w1': jax.random.normal(ks[1], (NS, D_MODEL, D_FF), dtype=jnp.float32) * s1, 'shared_b1': jnp.zeros((NS, D_FF), dtype=jnp.float32), 'shared_w2': jax.random.normal(ks[2], (NS, D_FF, D_MODEL), dtype=jnp.float32) * s2, 'shared_b2': jnp.zeros((NS, D_MODEL), dtype=jnp.float32), 'routed_w1': jax.random.normal(ks[3], (NR, D_MODEL, D_FF), dtype=jnp.float32) * s1, 'routed_b1': jnp.zeros((NR, D_FF), dtype=jnp.float32), 'routed_w2': jax.random.normal(ks[4], (NR, D_FF, D_MODEL), dtype=jnp.float32) * s2, 'routed_b2': jnp.zeros((NR, D_MODEL), dtype=jnp.float32), 'centroids': jax.random.normal(ks[5], (NR, D_MODEL), dtype=jnp.float32) * s1, 'bias': jnp.zeros((NR,), dtype=jnp.float32)}
    _L0_ffn_all = _L0_ffn_setup()
    _L0_ffn_in = {k: v for k, v in _L0_ffn_all.items() if k in ('shared_w1', 'shared_b1', 'shared_w2', 'shared_b2', 'routed_w1', 'routed_b1', 'routed_w2', 'routed_b2', 'centroids', 'bias')}
    del _L0_ffn_all
    return {'x': x, 'ctx_1024': ctx_1024, 'L0_attn_Wq': _L0_attn_in['Wq'], 'L0_attn_Wk': _L0_attn_in['Wk'], 'L0_attn_Wv': _L0_attn_in['Wv'], 'L0_attn_Wb': _L0_attn_in['Wb'], 'L0_attn_o_norm_weight': _L0_attn_in['o_norm_weight'], 'L0_attn_Wo': _L0_attn_in['Wo'], 'L0_xattn_in_proj_w': _L0_xattn_in['in_proj_w'], 'L0_xattn_conv_w': _L0_xattn_in['conv_w'], 'L0_xattn_conv_b': _L0_xattn_in['conv_b'], 'L0_xattn_x_proj_w': _L0_xattn_in['x_proj_w'], 'L0_xattn_dt_proj_w': _L0_xattn_in['dt_proj_w'], 'L0_xattn_dt_proj_b': _L0_xattn_in['dt_proj_b'], 'L0_xattn_A_log': _L0_xattn_in['A_log'], 'L0_xattn_D': _L0_xattn_in['D'], 'L0_ffn_shared_w1': _L0_ffn_in['shared_w1'], 'L0_ffn_shared_b1': _L0_ffn_in['shared_b1'], 'L0_ffn_shared_w2': _L0_ffn_in['shared_w2'], 'L0_ffn_shared_b2': _L0_ffn_in['shared_b2'], 'L0_ffn_routed_w1': _L0_ffn_in['routed_w1'], 'L0_ffn_routed_b1': _L0_ffn_in['routed_b1'], 'L0_ffn_routed_w2': _L0_ffn_in['routed_w2'], 'L0_ffn_routed_b2': _L0_ffn_in['routed_b2'], 'L0_ffn_centroids': _L0_ffn_in['centroids'], 'L0_ffn_bias': _L0_ffn_in['bias']}

def reference(x, ctx_1024, L0_attn_Wq, L0_attn_Wk, L0_attn_Wv, L0_attn_Wb, L0_attn_o_norm_weight, L0_attn_Wo, L0_xattn_in_proj_w, L0_xattn_conv_w, L0_xattn_conv_b, L0_xattn_x_proj_w, L0_xattn_dt_proj_w, L0_xattn_dt_proj_b, L0_xattn_A_log, L0_xattn_D, L0_ffn_shared_w1, L0_ffn_shared_b1, L0_ffn_shared_w2, L0_ffn_shared_b2, L0_ffn_routed_w1, L0_ffn_routed_b1, L0_ffn_routed_w2, L0_ffn_routed_b2, L0_ffn_centroids, L0_ffn_bias):
    import jax
    import jax.numpy as jnp

    def _L0_attn_ref(hidden_states, Wq, Wk, Wv, Wb, o_norm_weight, Wo):
        import jax, jax.numpy as jnp
        import numpy as np
        B, L, D, H = (2, 256, 256, 16)
        DH = D // H
        EPS = 1e-05

        def _delta_rule(q, k, v, beta):

            def step(S, inp):
                qt, kt, vt, bt = inp
                v_pred = jnp.einsum('bhk,bhkv->bhv', kt, S)
                delta = (vt - v_pred) * bt[..., None]
                S = S + kt[..., None] * delta[:, :, None, :]
                ot = jnp.einsum('bhk,bhkv->bhv', qt, S)
                return (S, ot)
            xs = (q.transpose(2, 0, 1, 3), k.transpose(2, 0, 1, 3), v.transpose(2, 0, 1, 3), beta.transpose(2, 0, 1))
            S0 = jnp.zeros(q.shape[:2] + (q.shape[-1], v.shape[-1]), q.dtype)
            _, o = jax.lax.scan(step, S0, xs)
            return o.transpose(1, 2, 0, 3)
        b, l, d = hidden_states.shape
        h = Wb.shape[1]
        dh = d // h
        q = hidden_states @ Wq
        k = hidden_states @ Wk
        v = jax.nn.silu(hidden_states @ Wv)

        def heads(x):
            return x.reshape(b, l, h, dh).transpose(0, 2, 1, 3)
        q, k, v = (heads(q), heads(k), heads(v))

        def l2n(x):
            n = jnp.sqrt(jnp.sum(x * x, axis=-1, keepdims=True))
            return x / jnp.maximum(n, 1e-12)
        q, k = (l2n(q), l2n(k))
        q = q * dh ** (-0.5)
        beta = jax.nn.sigmoid(hidden_states @ Wb).transpose(0, 2, 1)
        o = _delta_rule(q, k, v, beta)
        o = o.transpose(0, 2, 1, 3)
        o = o * jax.lax.rsqrt(jnp.mean(o * o, axis=-1, keepdims=True) + EPS)
        o = o * o_norm_weight
        return o.reshape(b, l, d) @ Wo

    def _L0_xattn_ref(hidden_states, z, in_proj_w, conv_w, conv_b, x_proj_w, dt_proj_w, dt_proj_b, A_log, D):
        import jax, jax.numpy as jnp
        import numpy as np
        import math
        B, L, DM = (2, 256, 128)
        DS, DC, EXP = (16, 4, 2)
        DI = EXP * DM
        DR = math.ceil(DM / 16)
        DT_MIN, DT_MAX, DT_FLOOR = (0.001, 0.1, 0.0001)

        def _ssm_forward(hidden_states, z, in_proj_w, conv_w, conv_b, x_proj_w, dt_proj_w, dt_proj_b, A_log, D):
            b = hidden_states.shape[0]
            x = jnp.einsum('ed,bld->bel', in_proj_w, hidden_states)
            xp = jnp.pad(x, ((0, 0), (0, 0), (DC - 1, 0)))
            xc = jax.lax.conv_general_dilated(xp, conv_w[:, None, :], window_strides=(1,), padding='VALID', dimension_numbers=('NCH', 'OIH', 'NCH'), feature_group_count=DI)
            u = jax.nn.silu(xc + conv_b[None, :, None])
            x_dbl = jnp.einsum('ke,bel->bkl', x_proj_w, u)
            dt_lo = x_dbl[:, :DR]
            Bm = x_dbl[:, DR:DR + DS]
            Cm = x_dbl[:, DR + DS:]
            delta = jax.nn.softplus(jnp.einsum('er,brl->bel', dt_proj_w, dt_lo) + dt_proj_b[None, :, None])
            A = -jnp.exp(A_log)

            def step(state, xs):
                d_t, B_t, C_t, u_t = xs
                dA = jnp.exp(d_t[..., None] * A)
                state = state * dA + (d_t * u_t)[..., None] * B_t[:, None, :]
                y_t = jnp.einsum('ben,bn->be', state, C_t)
                return (state, y_t)
            xs = (jnp.moveaxis(delta, -1, 0), jnp.moveaxis(Bm, -1, 0), jnp.moveaxis(Cm, -1, 0), jnp.moveaxis(u, -1, 0))
            state0 = jnp.zeros((b, DI, DS), delta.dtype)
            _, ys = jax.lax.scan(step, state0, xs)
            y = jnp.moveaxis(ys, 0, -1)
            y = y + D[None, :, None] * u
            y = y * jax.nn.silu(z)
            return jnp.swapaxes(y, 1, 2)
        return _ssm_forward(hidden_states, z, in_proj_w, conv_w, conv_b, x_proj_w, dt_proj_w, dt_proj_b, A_log, D)

    def _L0_ffn_ref(u, shared_w1, shared_b1, shared_w2, shared_b2, routed_w1, routed_b1, routed_w2, routed_b2, centroids, bias):
        import jax, jax.numpy as jnp
        import numpy as np
        D_MODEL, D_FF, NS, NR, KR = (256, 176, 2, 16, 4)
        B, S = (4, 256)

        def _moe_forward(u, shared_w1, shared_b1, shared_w2, shared_b2, routed_w1, routed_b1, routed_w2, routed_b2, centroids, bias):
            b, s, d = u.shape
            flat = u.reshape(-1, d)
            T = flat.shape[0]
            h = jax.nn.relu(jnp.einsum('td,ndf->ntf', flat, shared_w1) + shared_b1[:, None, :])
            shared_out = jnp.einsum('ntf,nfd->td', h, shared_w2) + shared_b2.sum(0)
            out = flat + shared_out
            scores = jax.nn.sigmoid(flat @ centroids.T) + bias
            vals, idx = jax.lax.top_k(scores, KR)
            gating = jnp.zeros_like(scores).at[jnp.arange(T)[:, None], idx].set(vals)
            gating = gating / jnp.clip(gating.sum(-1, keepdims=True), 1e-08)

            def step(acc, ew):
                w1, b1, w2, b2, g = ew
                hj = jax.nn.relu(flat @ w1 + b1)
                yj = hj @ w2 + b2
                return (acc + yj * g[:, None], None)
            rout0 = jnp.zeros_like(flat)
            rout, _ = jax.lax.scan(step, rout0, (routed_w1, routed_b1, routed_w2, routed_b2, gating.T))
            return (out + rout).reshape(b, s, d)
        return _moe_forward(u, shared_w1, shared_b1, shared_w2, shared_b2, routed_w1, routed_b1, routed_w2, routed_b2, centroids, bias)
    x = _layernorm(x + _L0_attn_ref(x, L0_attn_Wq, L0_attn_Wk, L0_attn_Wv, L0_attn_Wb, L0_attn_o_norm_weight, L0_attn_Wo), axis=-1)
    x = _layernorm(x + _L0_xattn_ref(ctx_1024, x, L0_xattn_in_proj_w, L0_xattn_conv_w, L0_xattn_conv_b, L0_xattn_x_proj_w, L0_xattn_dt_proj_w, L0_xattn_dt_proj_b, L0_xattn_A_log, L0_xattn_D), axis=-1)
    x = _layernorm(x + _L0_ffn_ref(x, L0_ffn_shared_w1, L0_ffn_shared_b1, L0_ffn_shared_w2, L0_ffn_shared_b2, L0_ffn_routed_w1, L0_ffn_routed_b1, L0_ffn_routed_w2, L0_ffn_routed_b2, L0_ffn_centroids, L0_ffn_bias), axis=-1)
    return x

_drawn_inputs = setup_inputs


def setup_inputs(seed=0):
    import zlib

    import numpy as np

    out = dict(_drawn_inputs(seed))
    spreads = {'L0_attn_o_norm_weight': (1.0, 0.2),
     'L0_xattn_conv_b': (0.0, 0.1),
     'L0_xattn_D': (1.0, 0.2),
     'L0_ffn_shared_b1': (0.0, 0.1),
     'L0_ffn_shared_b2': (0.0, 0.1),
     'L0_ffn_routed_b1': (0.0, 0.541),
     'L0_ffn_routed_b2': (0.0, 0.369),
     'L0_ffn_bias': (0.0, 0.1)}
    factors = {'L0_xattn_dt_proj_w': 4.355}
    for name, (base, spread) in spreads.items():
        noise = np.random.default_rng([zlib.crc32(name.encode()), seed]).standard_normal(out[name].shape)
        drawn = base * np.exp(spread * noise) if base else spread * noise
        out[name] = jnp.asarray(drawn.astype(out[name].dtype))
    for name, factor in factors.items():
        out[name] = (out[name] * factor).astype(out[name].dtype)
    return out
```

```python
from contextlib import ExitStack

import concourse.bass as bass
from concourse import mybir

F32 = mybir.dt.float32
BF16 = mybir.dt.bfloat16
ALU = mybir.AluOpType
ACT = mybir.ActivationFunctionType
AX_X = mybir.AxisListType.X

P = 128
B, L, D = 4, 256, 256
T = B * L
KT = D // P
H, DH = 16, 16
HH = P // DH
C = 16
GB = 2
GT_ = GB * L
NG = B // GB
NU = 2 * GB
NC = L // C
CLO = 4
DM, DS, DC, DR = 128, 16, 4, 8
DI = 2 * DM
LP = L + DC - 1
NE, NSH, KR, DFF = 16, 2, 4, 176
NX = NE + NSH
FT = -(-NX * DFF // P)
FP = FT * P
EPS = 1e-5
LN2 = 0.6931471805599453
SCALE_LOG2 = 20

C_ID, C_BLK, C_E, C_MS, C_MP, C_BIAS = 0, 128, 256, 272, 288, 304
BI_ONE, BI_EPS, BI_K, BI_Q = range(4)
C_ALL = C_BIAS + 4


def bank_turns():
    used = [0] * 8
    turns = {}

    def take(key, bank):
        turns[key] = (bank, used[bank])
        used[bank] += 1

    for et in range(2):
        for th in range(NG):
            take(("xe", et, th), 2 * et + th)
    for th in range(NG):
        take(("xdbl", th), 4 + th)
    for et in range(2):
        for th in range(NG):
            take(("dt", et, th), 6 + th)
    for g in range(NG):
        n = 0

        def ring(key):
            nonlocal n
            take((*key, g), 4 + n % 4)
            n += 1

        for kind in "vbqk":
            for half in range(2):
                ring((kind, half))
                if kind in "qk":
                    ring(("ss" + kind, half))
        for u in range(NU):
            ring(("A", u))
        for u in range(NU):
            ring(("P", u))
        for u in range(NU):
            ring(("V", u))
        for u in range(NU):
            ring(("UW", u))
        for u in range(NU):
            ring(("GQ", u))
        for u in range(NU):
            ring(("H", u))
        for c in range(1, NC - 1):
            ring(("S", c))
        for u in range(NU):
            ring(("O", u))
        for half in range(2):
            ring(("ms", half))
        for tt in range(4):
            ring(("wo", tt))
    for th in range(NG):
        for bb in range(GB):
            for lt in range(2):
                take(("yT", th, bb, lt), 4 + (2 * bb + lt) % 4)
    for th in range(NG):
        for k in range(4):
            take(("x3T", th, k), 4 + k)
        take(("score", th), 4)
        take(("gT", th), 5)
        for ft in range(FT):
            take(("h", th, ft), 4 + ft % 2)
            take(("G", th, ft), 6 + ft % 2)
    return turns


def decoder_layer(nc, x_tok_d, x_t_d, ctx_t_d, wqkvb_d, onorm_d, wo_d, inproj_d, convw_d, convb_d, xproj_d,
                  dtproj_d, dtb_d, alog_d, dskip_d, w1_d, b1_d, w2_d, b2_d, cent_d, ebias_d, const_d, eye3_d,
                  sel_d, lmask_d, out_d):
    turns = bank_turns()
    scr_a = nc.dram_tensor("scr_a", (NG, P, NU * L), F32).ap()
    scr_t = nc.dram_tensor("scr_t", (NG, P, C * CLO * C), F32).ap()

    with ExitStack() as ctx:
        def sb(name, shape, dt=F32):
            return ctx.enter_context(nc.sbuf_tensor(name, shape, dt))

        def sem(name):
            return ctx.enter_context(nc.semaphore(name))

        bank = [ctx.enter_context(nc.psum_tensor(f"bank{i}", [P, 512], F32)) for i in range(8)]
        bank_b, bank_c, bank_y = bank[0], bank[1], bank[2:4]

        xT = sb("xT", [P, KT, T])
        xres = sb("xres", [P, 8, D])
        wqkvb = sb("wqkvb", [P, KT, 3 * D + H])
        wo = sb("wo", [P, 2, D])
        onorm = sb("onorm", [P, 1])
        const = sb("const", [P, C_ALL])
        eye3 = sb("eye3", [96, 2 * DS], BF16)
        inproj = sb("inproj", [P, DI])
        convw = sb("convw", [P, 2, DC])
        convb = sb("convb", [P, 2])
        xproj = sb("xproj", [P, 2, 104])
        dtproj = sb("dtproj", [P, DI])
        dtb = sb("dtb", [P, 2])
        alog = sb("alog", [P, 2, DS])
        dskip = sb("dskip", [P, 2])
        ident = const[:, C_ID:C_ID + P]
        blk = const[:, C_BLK:C_BLK + P]
        eye16 = const[:, C_E:C_E + C]
        mask_s = const[:, C_MS:C_MS + C]
        mask_p = const[:, C_MP:C_MP + C]

        def bias_col(i, n=P):
            return const[0:n, C_BIAS + i:C_BIAS + i + 1]

        arena_s = sb("arena_s", [P, 2 * B * LP + T])
        xpad = arena_s[:, 0:2 * B * LP].rearrange("p (e b l) -> p e b l", e=2, b=B)
        ctxT = arena_s[:, 2 * B * LP:2 * B * LP + T]
        dA = arena_s[:, 0:2 * 2 * GT_].rearrange("p (k n) -> p k n", k=2)
        dBu = arena_s[:, 4 * GT_:6 * GT_]
        arena_h = sb("arena_h", [P, 3 * 2 * GT_])
        sp_z = arena_h[:, 0:T]
        sp_w = arena_h[:, T:2 * T]
        sp_l = arena_h[:, 2 * T:3 * T]
        hst = arena_h[:, 0:2 * GT_]
        hC = arena_h[:, 2 * GT_:6 * GT_].rearrange("p (k n) -> p k n", k=2)
        u = sb("u", [P, 2, T])
        delta = sb("delta", [P, 2, T])
        du = sb("du", [P, 2, T])
        stk = sb("stk", [96, T], BF16)
        negA = sb("negA", [P, 2, DS])

        bd = [sb(f"bd{k}", [P, P, NU * NC]) for k in range(2)]
        qE = sb("qE", [P, NU, NC, 2 * C])
        kE = sb("kE", [P, NU, NC, 2 * C])
        k_uv = sb("k_uv", [P, NU * L])
        kb_a_w = sb("kb_a_w", [P, NU * L])
        vk_hs = sb("vk_hs", [P, NU, NC, 2 * C])
        KP = sb("KP", [P, NU, NC, 2 * C])
        ain_g = sb("ain_g", [P, NU * L])
        tt_ = sb("tt_", [P, C * CLO * C])
        tmp_o = sb("tmp_o", [P, NU * L])
        vb = sb("vb", [P, NU * L])
        beta_kc = sb("beta_kc", [P, NU * L])
        dtlo = beta = kc = beta_kc
        sq = sb("sq", [P, GT_])
        ln_st = sb("ln_st", [P, 4, 6])
        ln_mv = sb("ln_mv", [P, 4, 2])
        ln_r = sb("ln_r", [P, 4])
        H_ = vk_hs[:, :, :, :].rearrange("p u c n -> p (u c n)")[:, 0:NU * L]
        S_ = vk_hs[:, :, :, :].rearrange("p u c n -> p (u c n)")[:, NU * L:2 * NU * L]

        def ucn(t):
            return t.rearrange("p (u c n) -> p u c n", u=NU, c=NC)

        def nuc(t):
            return t.rearrange("p (n u c) -> p u c n", u=NU, c=NC)

        bdf = [b_[:, :, :].rearrange("p m n -> p (m n)") for b_ in bd]
        w1 = bdf[0][:, 0:KT * FP].rearrange("p (k f) -> p k f", k=KT)
        w2 = bdf[1][:, 0:FT * D].rearrange("p (f d) -> p f d", f=FT)
        sel = bdf[0][:, KT * FP:KT * FP + FP // 2].bitcast(BF16)
        b1 = sb("b1", [P, FT])
        b2 = bdf[1][0:NX, FT * D:FT * D + D]
        lmask = bdf[1][:, FT * D + D:FT * D + D + NE * NE]
        cent = sb("cent", [P, KT, NE])
        ebias = sb("ebias", [P, NE])
        x3T = xT[:, :, :]
        sig = sb("sig", [P, 4, NE])
        sc = sb("sc", [P, 4, NE])
        rk0 = qE[:, :, :, :].rearrange("p u c n -> p (u c n)")[:, 0:4 * NE * NE]
        rk1 = qE[:, :, :, :].rearrange("p u c n -> p (u c n)")[:, 4 * NE * NE:8 * NE * NE]
        rank = sb("rank", [P, 4, NE])
        gsum = sb("gsum", [P, 4])
        g96 = kE[:, :, :, :].rearrange("p u c n -> p (u c n)")[:, 2 * GT_:2 * GT_ + 4 * 96].rearrange("p (t n) -> p t n", t=4)
        gstk = sb("gstk", [96, GT_], BF16)
        gT = vb[0:32, 0:GT_]
        gr1 = sq[0:96, :]
        gm16 = beta_kc[0:96, 0:GT_ // 2].bitcast(BF16)
        hrel = kE[:, :, :, :].rearrange("p u c n -> p (u c n)")[:, 0:2 * GT_].rearrange("p (k n) -> p k n", k=2)
        hg = KP[:, :, :, :].rearrange("p u c n -> p (u c n)")[:, 0:2 * GT_].rearrange("p (k n) -> p k n", k=2)

        s_ld_ssm = sem("s_ld_ssm")
        s_ld_att = sem("s_ld_att")
        s_ld_ffn = sem("s_ld_ffn")
        s_ld_small = sem("s_ld_small")
        s_full = [sem(f"s_full{i}") for i in range(8)]
        s_free = [sem(f"s_free{i}") for i in range(8)]
        s_pad = sem("s_pad")
        s_xpad = sem("s_xpad")
        s_conv = sem("s_conv")
        s_u = sem("s_u")
        s_dtlo = sem("s_dtlo")
        s_stk = sem("s_stk")
        s_negA = sem("s_negA")
        s_nA = sem("s_nA")
        s_sp = sem("s_sp")
        s_delta = sem("s_delta")
        s_spf = sem("s_spf")
        s_act = sem("s_act")
        s_dve = sem("s_dve")
        s_pool = sem("s_pool")
        s_dA0 = sem("s_dA0")
        s_dA = sem("s_dA")
        s_dAuse = sem("s_dAuse")
        s_bb = sem("s_bb")
        s_cc = sem("s_cc")
        s_bfree = sem("s_bfree")
        s_hc = sem("s_hc")
        s_hcuse = sem("s_hcuse")
        s_y = sem("s_y")
        s_yfree = sem("s_yfree")
        s_zero = sem("s_zero")
        s_att = sem("s_att")
        s_sq = sem("s_sq")
        s_clamp = sem("s_clamp")
        s_rs = sem("s_rs")
        s_qk = sem("s_qk")
        s_vb = sem("s_vb")
        s_ke = sem("s_ke")
        s_exp = [sem(f"s_exp{i}") for i in range(2)]
        s_acp = sem("s_acp")
        s_kbc = sem("s_kbc")
        s_adram = sem("s_adram")
        s_ain = sem("s_ain")
        s_kp = sem("s_kp")
        s_kca = sem("s_kca")
        s_vc = sem("s_vc")
        s_tt = sem("s_tt")
        s_tdram = sem("s_tdram")
        s_wb = sem("s_wb")
        s_tcp = sem("s_tcp")
        s_tperm = sem("s_tperm")
        s_uv = sem("s_uv")
        s_w = sem("s_w")
        s_gt = sem("s_gt")
        s_qp = sem("s_qp")
        s_h = sem("s_h")
        s_s = sem("s_s")
        s_ot = sem("s_ot")
        s_osq = sem("s_osq")
        s_or = sem("s_or")
        s_on = sem("s_on")
        s_var = sem("s_var")
        s_rstd = sem("s_rstd")
        s_x2 = sem("s_x2")
        s_yd = sem("s_yd")
        s_z = sem("s_z")
        s_ys = sem("s_ys")
        s_x3 = sem("s_x3")
        s_x3T = sem("s_x3T")
        s_sige = sem("s_sige")
        s_g96 = sem("s_g96")
        s_gT = sem("s_gT")
        s_gstk = sem("s_gstk")
        s_rel = sem("s_rel")
        s_hg = sem("s_hg")
        s_hguse = sem("s_hguse")
        s_yacc = sem("s_yacc")
        s_yaccfree = sem("s_yaccfree")
        s_last = sem("s_last")
        s_out = sem("s_out")

        block = ctx.enter_context(nc.Block())

        LD_SSM, LD_ATT, LD_FFN = 9 * 16, 7 * 16, 5 * 16

        @block.sync
        def _(sp):
            def load(dst, src, s):
                sp.dma_start(dst, src).then_inc(s, 16)

            load(ctxT, ctx_t_d, s_ld_ssm)
            load(inproj[:, :], inproj_d, s_ld_ssm)
            load(convw[:, :, :], convw_d.rearrange("(e p) k -> p e k", p=P), s_ld_ssm)
            load(convb[:, :], convb_d, s_ld_ssm)
            load(xproj[:, :, :], xproj_d.rearrange("(e p) k -> p e k", p=P), s_ld_ssm)
            load(dtproj[96:96 + DR, :], dtproj_d, s_ld_ssm)
            load(dtb[:, :], dtb_d, s_ld_ssm)
            load(alog[:, :, :], alog_d.rearrange("(e p) n -> p e n", p=P), s_ld_ssm)
            load(dskip[:, :], dskip_d, s_ld_ssm)
            load(const[:, :], const_d, s_ld_att)
            load(onorm[:, :], onorm_d, s_ld_att)
            load(eye3[:, :], eye3_d, s_ld_att)
            load(xT[:, :, :], x_t_d.rearrange("(k p) t -> p k t", p=P), s_ld_att)
            load(wqkvb[:, :, :], wqkvb_d.rearrange("(k p) n -> p k n", p=P), s_ld_att)
            load(xres[:, :, :], x_tok_d.rearrange("(n p) d -> p n d", p=P), s_ld_att)
            load(wo[:, :, :], wo_d.rearrange("(k p) n -> p k n", p=P), s_ld_att)

            def read(key):
                b_, n = turns[key]
                sp.wait_ge(s_full[b_], n + 1)

            def expand(k, src):
                for h in range(HH):
                    r = slice(DH * h, DH * h + DH)
                    sp.dma_start(bd[k][r, r, :].rearrange("p m n -> p (m n)"), src[r, :]).then_inc(s_exp[k], 16)

            for g in range(NG):
                sp.wait_ge(s_zero, 2)
                sp.wait_ge(s_qk, 2 * g + 2)
                if g:
                    read(("O", NU - 1, g - 1))
                expand(0, kb_a_w)
                expand(1, k_uv)
                sp.wait_ge(s_acp, NU * (g + 1))
                sp.dma_start(scr_a[g], kb_a_w[:, :]).then_inc(s_adram, 16)
                read(("A", NU - 1, g))
                sp.wait_ge(s_vb, g + 1)
                expand(0, vb)
                sp.wait_ge(s_adram, 16 * (g + 1))
                for h in range(HH):
                    r = slice(DH * h, DH * h + DH)
                    sp.dma_start(ain_g[r, :].rearrange("i (t e) -> i t e", t=C),
                                 scr_a[g, r, :].rearrange("t (i e) -> i t e", i=16)).then_inc(s_ain, 16)
                sp.wait_ge(s_tt, g + 1)
                sp.dma_start(scr_t[g], tt_[:, :]).then_inc(s_tdram, 16)
                sp.wait_ge(s_tdram, 16 * (g + 1))
                for h in range(HH):
                    r = slice(DH * h, DH * h + DH)
                    sp.dma_start(ain_g[r, :].rearrange("p (i e) -> p i e", i=16),
                                 scr_t[g, r, :].rearrange("i (j e) -> j i e", j=C)).then_inc(s_tcp, 16)
                sp.wait_ge(s_tperm, g + 1)
                read(("P", NU - 1, g))
                expand(1, tt_)
                sp.wait_ge(s_w, NU * (g + 1))
                read(("V", NU - 1, g))
                expand(0, kb_a_w)
                sp.wait_ge(s_kca, NU * (g + 1))
                read(("UW", NU - 1, g))
                expand(1, kc)
                read(("GQ", NU - 1, g))
                sp.wait_ge(s_uv, NU * (g + 1))
                expand(0, k_uv)
                sp.wait_ge(s_gt, NU * (g + 1))
                read(("H", NU - 1, g))
                expand(1, ain_g)
                sp.wait_ge(s_s, (NC - 1) * (g + 1))
                read(("S", NC - 2, g))
                expand(1, S_)
            read(("O", NU - 1, NG - 1))
            load(w1, w1_d.rearrange("(k p) f -> p k f", p=P), s_ld_ffn)
            load(w2, w2_d.rearrange("(f p) d -> p f d", p=P), s_ld_ffn)
            load(sel[0:96, :], sel_d, s_ld_ffn)
            load(b2, b2_d, s_ld_ffn)
            load(lmask, lmask_d, s_ld_ffn)
            for th in range(NG):
                for tt in range(4):
                    sp.wait_ge(s_last, 4 * th + tt + 1)
                    n = 4 * th + tt
                    sp.dma_start(out_d[P * n:P * (n + 1), :], xres[:, n, :]).then_inc(s_out, 16)
            sp.wait_ge(s_out, 16 * 8)

        @block.gpsimd
        def _(pool):
            pool.memset(xpad[:, :, :, 0:DC - 1], 0.0).then_inc(s_pad, 1)
            pool.dma_start(b1[:, :], b1_d).then_inc(s_ld_small, 16)
            pool.dma_start(cent[:, :, :], cent_d.rearrange("(k p) e -> p k e", p=P)).then_inc(s_ld_small, 16)
            pool.dma_start(ebias[:, :], ebias_d.rearrange("(a e) -> a e", a=1).partition_broadcast(P)).then_inc(s_ld_small, 16)
            for k in range(2):
                pool.memset(bdf[k], 0.0).then_inc(s_zero, 1)

        @block.tensor
        def _(pe):
            def fill(key):
                b_, n = turns[key]
                if n:
                    pe.wait_ge(s_free[b_], n)
                return bank[b_]

            def filled(key, mm):
                mm.then_inc(s_full[turns[key][0]], 1)

            def prelude():
                pe.wait_ge(s_ld_ssm, LD_SSM)
                for et in range(2):
                    for th in range(NG):
                        k = ("xe", et, th)
                        filled(k, pe.matmul(fill(k)[:, :], inproj[:, P * et:P * et + P],
                                            ctxT[:, GT_ * th:GT_ * th + GT_], start=True, stop=True))
                pe.wait_ge(s_u, 2)
                for th in range(NG):
                    k = ("xdbl", th)
                    o = fill(k)
                    for et in range(2):
                        mm = pe.matmul(o[0:104, :], xproj[:, et, :], u[:, et, GT_ * th:GT_ * th + GT_],
                                       start=(et == 0), stop=(et == 1))
                    filled(k, mm)
                pe.wait_ge(s_dtlo, NG)
                for et in range(2):
                    for th in range(NG):
                        k = ("dt", et, th)
                        filled(k, pe.matmul(fill(k)[:, :], dtproj[96:96 + DR, P * et:P * et + P],
                                            dtlo[96:96 + DR, GT_ * th:GT_ * th + GT_], start=True, stop=True))

            def broadcasts(i):
                th, n = divmod(i, DS)
                cols = slice(GT_ * th, GT_ * th + GT_)
                if i:
                    pe.wait_ge(s_bfree, 2 * i)
                for o, r, s in ((bank_b, n, s_bb), (bank_c, DS + n, s_cc)):
                    pe.matmul(o[:, :], eye3[:, r:r + 1].broadcast_to([96, P]), stk[:, cols],
                              start=True, stop=True).then_inc(s, 1)

            def reduce_states(i):
                th, n = divmod(i, DS)
                pe.wait_ge(s_hc, i + 1)
                if n == 0 and th:
                    pe.wait_ge(s_yfree, 2 * th)
                for et in range(2):
                    mm = pe.matmul(bank_y[et][:, :], ident, hC[:, i % 2, GT_ * et:GT_ * et + GT_],
                                   start=(n == 0), stop=(n == DS - 1))
                mm.then_inc(s_hcuse, 1)

            def blocks(k, un, c):
                return bd[k][:, :, NC * un + c]

            def att(g, n):
                cols = slice(GT_ * g, GT_ * g + GT_)
                if n == 0:
                    pe.wait_ge(s_ld_att, LD_ATT)
                    pe.wait_ge(s_wb, g + 1)
                    for j, kind in enumerate("vbqk"):
                        for half in range(2):
                            k = (kind, half, g)
                            o = fill(k)
                            for kt in range(KT):
                                if kind == "b":
                                    w = sq[:, D * kt + P * half:D * kt + P * half + P]
                                else:
                                    at = {"q": 0, "k": D, "v": 2 * D}[kind] + P * half
                                    w = wqkvb[:, kt, at:at + P]
                                mm = pe.matmul(o[:, :], w, xT[:, kt, cols], start=(kt == 0), stop=(kt == KT - 1))
                            filled(k, mm)
                            if kind in "qk":
                                k = ("ss" + kind, half, g)
                                o = fill(k)
                                pe.wait_ge(s_sq, 4 * g + 2 * (kind == "k") + half + 1)
                                filled(k, pe.matmul(o[:, :], blk, sq[:, :], start=True, stop=True))
                if n == 2:
                    pe.wait_ge(s_exp[0], 128 * (4 * g + 1))
                    pe.wait_ge(s_ke, 2 * (g + 1))
                    for un in range(NU):
                        k = ("A", un, g)
                        o = fill(k)
                        for c in range(NC):
                            mm = pe.matmul(o[:, 32 * c:32 * c + 32], blocks(0, un, c), kE[:, un, c, :], start=True, stop=True)
                        filled(k, mm)
                if n == 3:
                    pe.wait_ge(s_exp[1], 128 * (5 * g + 1))
                    for un in range(NU):
                        k = ("P", un, g)
                        o = fill(k)
                        for c in range(NC):
                            mm = pe.matmul(o[:, 32 * c:32 * c + 32], blocks(1, un, c), qE[:, un, c, :], start=True, stop=True)
                        filled(k, mm)
                if n == 4:
                    pe.wait_ge(s_exp[0], 128 * (4 * g + 2))
                    for un in range(NU):
                        k = ("V", un, g)
                        o = fill(k)
                        for c in range(NC):
                            mm = pe.matmul(o[:, 16 * c:16 * c + 16], blocks(0, un, c), eye16, start=True, stop=True)
                        filled(k, mm)
                if n == 8:
                    pe.wait_ge(s_exp[1], 128 * (5 * g + 2))
                    pe.wait_ge(s_vc, NU * (g + 1))
                    pe.wait_ge(s_kbc, NU * (g + 1))
                    for un in range(NU):
                        k = ("UW", un, g)
                        o = fill(k)
                        for c in range(NC):
                            mm = pe.matmul(o[:, 32 * c:32 * c + 32], blocks(1, un, c), vk_hs[:, un, c, :], start=True, stop=True)
                        filled(k, mm)
                if n == 9:
                    pe.wait_ge(s_exp[0], 128 * (4 * g + 3))
                    pe.wait_ge(s_kp, NU * (g + 1))
                    pe.wait_ge(s_kca, NU * (g + 1))
                    for un in range(NU):
                        k = ("GQ", un, g)
                        o = fill(k)
                        for c in range(NC):
                            mm = pe.matmul(o[:, 32 * c:32 * c + 32], blocks(0, un, c), KP[:, un, c, :], start=True, stop=True)
                        filled(k, mm)
                if n == 10:
                    pe.wait_ge(s_exp[1], 128 * (5 * g + 3))
                    for un in range(NU):
                        k = ("H", un, g)
                        o = fill(k)
                        for c in range(NC):
                            mm = pe.matmul(o[:, 16 * c:16 * c + 16], blocks(1, un, c), nuc(k_uv[:, :])[:, un, c, :], start=True, stop=True)
                        filled(k, mm)
                if n == 12:
                    pe.wait_ge(s_exp[1], 128 * (5 * g + 4))
                    for c in range(1, NC - 1):
                        k = ("S", c, g)
                        o = fill(k)
                        pe.wait_ge(s_s, (NC - 1) * g + c)
                        for un in range(NU):
                            mm = pe.matmul(o[:, 16 * un:16 * un + 16], blocks(1, un, c), nuc(S_)[:, un, c, :], start=True, stop=True)
                        filled(k, mm)
                if n == 14:
                    pe.wait_ge(s_exp[0], 128 * (4 * g + 4))
                    pe.wait_ge(s_exp[1], 128 * (5 * g + 5))
                    pe.wait_ge(s_qp, NU * (g + 1))
                    for un in range(NU):
                        k = ("O", un, g)
                        o = fill(k)
                        for c in range(NC):
                            cc = slice(16 * c, 16 * c + 16)
                            mm = pe.matmul(o[:, cc], blocks(0, un, c), KP[:, un, c, C:2 * C], start=True, stop=(c == 0))
                            if c:
                                mm = pe.matmul(o[:, cc], blocks(1, un, c), qE[:, un, c, 0:C], start=False, stop=True)
                        filled(k, mm)
                if n == 15:
                    for half in range(2):
                        k = ("ms", half, g)
                        o = fill(k)
                        pe.wait_ge(s_osq, 2 * g + half + 1)
                        filled(k, pe.matmul(o[:, :], blk, sq[:, :], start=True, stop=True))
                    pe.wait_ge(s_on, 2 * (g + 1))
                    for tt in range(4):
                        k = ("wo", tt, g)
                        o = fill(k)
                        for half in range(2):
                            at = GT_ * half + P * tt
                            mm = pe.matmul(o[:, 0:D], tmp_o[:, at:at + P], wo[:, half, :], start=(half == 0), stop=(half == 1))
                        filled(k, mm)

            def moe(th):
                for k4 in range(4):
                    k = ("x3T", th, k4)
                    o = fill(k)
                    pe.wait_ge(s_x3, 4 * th + k4 + 1)
                    for kt in range(KT):
                        mm = pe.transpose(o[:, P * kt:P * kt + P], xres[:, 4 * th + k4, P * kt:P * kt + P], ident)
                    filled(k, mm)
                pe.wait_ge(s_x3T, 4 * (th + 1))
                if th == 0:
                    pe.wait_ge(s_ld_ffn, LD_FFN)
                    pe.wait_ge(s_ld_small, 48)
                k = ("score", th)
                o = fill(k)
                for tt in range(4):
                    for kt in range(KT):
                        mm = pe.matmul(o[:, NE * tt:NE * tt + NE], x3T[:, kt, GT_ * th + P * tt:GT_ * th + P * tt + P],
                                       cent[:, kt, :], start=(kt == 0), stop=(kt == KT - 1))
                filled(k, mm)
                k = ("gT", th)
                o = fill(k)
                pe.wait_ge(s_g96, th + 1)
                for tt in range(4):
                    mm = pe.transpose(o[0:96, P * tt:P * tt + P], g96[:, tt, :], ident)
                filled(k, mm)

                def hidden(ft):
                    k = ("h", th, ft)
                    o = fill(k)
                    for kt in range(KT):
                        mm = pe.matmul(o[:, :], w1[:, kt, P * ft:P * ft + P], x3T[:, kt, GT_ * th:GT_ * th + GT_],
                                       start=(kt == 0), stop=(kt == KT - 1))
                    filled(k, mm)
                    k = ("G", th, ft)
                    o = fill(k)
                    if ft == 0:
                        pe.wait_ge(s_gstk, th + 1)
                    filled(k, pe.matmul(o[:, :], sel[0:96, P * ft:P * ft + P], gstk[:, :], start=True, stop=True))

                def outputs(ft):
                    pe.wait_ge(s_hg, FT * th + ft + 1)
                    for tt in range(4):
                        o = bank_y[tt // 2][:, D * (tt % 2):D * (tt % 2) + D]
                        mm = pe.matmul(o, hg[:, ft % 2, P * tt:P * tt + P], w2[:, ft, :],
                                       start=(ft == 0 and tt % 2 == 0), stop=False, skip_group_check=True)
                    mm.then_inc(s_hguse, 1)

                hidden(0)
                for ft in range(FT):
                    if ft + 1 < FT:
                        hidden(ft + 1)
                    if ft == 0:
                        pe.wait_ge(s_yfree, 2 * NG)
                        if th:
                            pe.wait_ge(s_yaccfree, 4 * th)
                    outputs(ft)
                for tt in range(4):
                    o = bank_y[tt // 2][:, D * (tt % 2):D * (tt % 2) + D]
                    pe.matmul(o, gT[0:NX, P * tt:P * tt + P], b2, start=False, stop=True,
                              skip_group_check=True).then_inc(s_yacc, 1)

            prelude()
            for i in range(NG * DS):
                if i == 0:
                    pe.wait_ge(s_stk, NG)
                    pe.wait_ge(s_ld_att, LD_ATT)
                broadcasts(i)
                att(i // DS, i % DS)
                reduce_states(i)
                if i % DS == DS - 1:
                    pe.wait_ge(s_hcuse, i + 1)
                    pe.nop().then_inc(s_y, 1)
            for th in range(NG):
                for bb in range(GB):
                    for lt in range(2):
                        k = ("yT", th, bb, lt)
                        o = fill(k)
                        pe.wait_ge(s_ys, 2 * (2 * th + bb) + 2)
                        for et in range(2):
                            at = GT_ * th + L * bb + P * lt
                            mm = pe.transpose(o[:, P * et:P * et + P], u[:, et, at:at + P], ident)
                        filled(k, mm)
            for th in range(NG):
                moe(th)

        @block.scalar
        def _(act):
            chain = [0]

            def link(ins):
                chain[0] += 1
                ins.then_inc(s_act, 1)
                act.wait_ge(s_act, chain[0])

            def take(key):
                b_, n = turns[key]
                act.wait_ge(s_full[b_], n + 1)
                return bank[b_]

            def freed(key, ins):
                ins.then_inc(s_free[turns[key][0]], 1)

            def prelude():
                for et in range(2):
                    for th in range(NG):
                        k = ("xe", et, th)
                        o = take(k)
                        ins = act.activation(xpad[:, et, GB * th:GB * th + GB, DC - 1:LP],
                                             o[:, :].rearrange("p (b l) -> p b l", b=GB), ACT.Copy)
                        link(ins)
                        act.nop().then_inc(s_free[turns[k][0]], 1)
                        act.nop().then_inc(s_xpad, 1)
                for et in range(2):
                    act.wait_ge(s_conv, et + 1)
                    act.activation(u[:, et, :], u[:, et, :], ACT.Silu).then_inc(s_u, 1)
                link(act.activation(negA[:, :, :], alog[:, :, :], ACT.Exp))
                link(act.activation(negA[:, :, :], negA[:, :, :], ACT.Copy, scale=-1.0))
                for th in range(NG):
                    o = take(("xdbl", th))
                    act.activation(dtlo[96:96 + DR, GT_ * th:GT_ * th + GT_], o[96:96 + DR, :], ACT.Copy).then_inc(s_dtlo, 1)
                act.wait_ge(s_ld_att, LD_ATT)
                for et in range(2):
                    if et:
                        act.wait_ge(s_spf, et)
                    for th in range(NG):
                        k = ("dt", et, th)
                        o = take(k)
                        c_ = slice(GT_ * th, GT_ * th + GT_)
                        act.activation(delta[:, et, c_], o[:, :], ACT.Identity, bias=dtb[:, et:et + 1])
                        link(act.activation(sp_z[:, c_], o[:, :], ACT.Abs, bias=dtb[:, et:et + 1]))
                        act.nop().then_inc(s_free[turns[k][0]], 1)
                    link(act.activation(sp_z, sp_z, ACT.Exp, scale=-1.0))
                    link(act.activation(sp_w, sp_z, ACT.Identity, bias=bias_col(BI_ONE)))
                    act.activation(sp_l, sp_w, ACT.Ln).then_inc(s_sp, 1)

            def decays(i):
                th, n = divmod(i, DS)
                if i == 0:
                    act.wait_ge(s_delta, 2)
                    act.wait_ge(s_dA0, 2)
                if i >= 2:
                    act.wait_ge(s_dAuse, i - 1)
                for et in range(2):
                    o = dA[:, i % 2, GT_ * et:GT_ * et + GT_].rearrange("p (b l) -> p b l", b=GB)[:, :, 1:L]
                    src = delta[:, et, GT_ * th:GT_ * th + GT_].rearrange("p (b l) -> p b l", b=GB)[:, :, 1:L]
                    act.activation(o, src, ACT.Exp, scale=negA[:, et, n:n + 1]).then_inc(s_dA, 1)

            def att(g, n):
                if n == 0:
                    if g:
                        act.wait_ge(s_vb, g)
                        act.wait_ge(s_exp[0], 128 * (4 * (g - 1) + 2))
                        act.wait_ge(s_qk, 2 * g)
                    for kind, f, dst in (("v", ACT.Silu, tt_), ("b", ACT.Sigmoid, beta)):
                        for half in range(2):
                            k = (kind, half, g)
                            o = take(k)
                            ins = act.activation(dst[:, GT_ * half:GT_ * half + GT_], o[:, :], f)
                            link(ins)
                            act.nop().then_inc(s_free[turns[k][0]], 1)
                    act.nop().then_inc(s_att, 1)
                    for j, kind in enumerate("qk"):
                        for half in range(2):
                            w = 4 * g + 2 * j + half
                            o = take((kind, half, g))
                            if w:
                                act.wait_ge(s_clamp, w)
                            act.activation(sq[:, :], o[:, :], ACT.Square).then_inc(s_sq, 1)
                            act.wait_ge(s_clamp, w + 1)
                            r = tmp_o[:, GT_ * (half):GT_ * (half) + GT_]
                            link(act.activation(r, r, ACT.Ln, scale=float(2 ** SCALE_LOG2)))
                            act.activation(r, r, ACT.Exp, scale=-0.5,
                                           bias=bias_col(BI_Q if kind == "q" else BI_K)).then_inc(s_rs, 1)
                if n == 2:
                    for un in range(NU):
                        k = ("A", un, g)
                        o = take(k)
                        act.wait_ge(s_acp, NU * g + un + 1)
                        ins = act.activation(vk_hs[:, un, :, C:2 * C], o[:, :].rearrange("p (c n) -> p c n", c=NC)[:, :, C:2 * C], ACT.Copy)
                        link(ins)
                        act.nop().then_inc(s_free[turns[k][0]], 1)
                        act.nop().then_inc(s_kbc, 1)
                if n == 3:
                    for un in range(NU):
                        k = ("P", un, g)
                        o = take(k)[:, :].rearrange("p (c n) -> p c n", c=NC)[:, :, C:2 * C]
                        act.wait_ge(s_kp, NU * g + un + 1)
                        link(act.activation(KP[:, un, :, 0:C], o, ACT.Copy))
                        ins = act.activation(nuc(kc[:, :])[:, un, :, :], o, ACT.Copy)
                        link(ins)
                        act.nop().then_inc(s_free[turns[k][0]], 1)
                        act.nop().then_inc(s_kca, 1)
                if n == 4:
                    for un in range(NU):
                        k = ("V", un, g)
                        o = take(k)[:, 0:L].rearrange("p (c n) -> p c n", c=NC)
                        link(act.activation(vk_hs[:, un, :, 0:C], o, ACT.Copy))
                        act.nop().then_inc(s_free[turns[k][0]], 1)
                        act.nop().then_inc(s_vc, 1)
                if n == 8:
                    act.wait_ge(s_tcp, 128 * (g + 1))
                    act.activation(tt_[:, :].rearrange("p (n a) -> p a n", n=C),
                                   ain_g[:, :].rearrange("p (a n) -> p a n", n=C), ACT.Copy).then_inc(s_tperm, 1)
                    for un in range(NU):
                        k = ("UW", un, g)
                        o = take(k)[:, :].rearrange("p (c n) -> p c n", c=NC)[:, :, 0:C]
                        act.wait_ge(s_w, NU * g + un + 1)
                        link(act.activation(nuc(k_uv[:, :])[:, un, :, :], o, ACT.Copy))
                        act.nop().then_inc(s_free[turns[k][0]], 1)
                        act.nop().then_inc(s_uv, 1)
                if n == 10:
                    for un in range(NU):
                        k = ("H", un, g)
                        o = take(k)[:, 0:L]
                        link(act.activation(H_[:, L * un:L * un + L], o, ACT.Copy))
                        act.nop().then_inc(s_free[turns[k][0]], 1)
                        act.nop().then_inc(s_h, 1)
                if n == 14:
                    for un in range(NU):
                        k = ("O", un, g)
                        o = take(k)[:, 0:L]
                        link(act.activation(tmp_o[:, L * un:L * un + L], o, ACT.Copy))
                        act.nop().then_inc(s_free[turns[k][0]], 1)
                if n == 15:
                    for half in range(2):
                        r = sq[:, :]
                        act.activation(r, tmp_o[:, GT_ * half:GT_ * half + GT_], ACT.Square).then_inc(s_osq, 1)
                        k = ("ms", half, g)
                        o = take(k)
                        rr = vb[:, GT_ * half:GT_ * half + GT_]
                        link(act.activation(rr, o[:, :], ACT.Ln, scale=1.0 / DH, bias=bias_col(BI_EPS)))
                        act.nop().then_inc(s_free[turns[k][0]], 1)
                        act.activation(rr, rr, ACT.Exp, scale=-0.5).then_inc(s_or, 1)
                    rstd(g)

            def rstd(n):
                act.wait_ge(s_var, n + 1)
                link(act.activation(ln_r[:, :], ln_mv[:, :, 1], ACT.Ln, bias=bias_col(BI_EPS)))
                act.activation(ln_r[:, :], ln_r[:, :], ACT.Exp, scale=-0.5).then_inc(s_rstd, 1)

            def moe(th):
                act.wait_ge(s_ld_small, 48)
                for k4 in range(4):
                    k = ("x3T", th, k4)
                    o = take(k)[:, 0:D].rearrange("p (k t) -> p k t", k=KT)
                    at = GT_ * th + P * k4
                    link(act.activation(x3T[:, :, at:at + P], o, ACT.Copy))
                    act.nop().then_inc(s_free[turns[k][0]], 1)
                    act.nop().then_inc(s_x3T, 1)
                k = ("score", th)
                o = take(k)
                link(act.activation(sig[:, :, :], o[:, 0:4 * NE].rearrange("p (t e) -> p t e", t=4), ACT.Sigmoid))
                act.nop().then_inc(s_free[turns[k][0]], 1)
                act.nop().then_inc(s_sige, 1)
                k = ("gT", th)
                o = take(k)
                act.activation(gT[0:32, :], o[0:32, :], ACT.Copy).then_inc(s_gT, 1)
                for ft in range(FT):
                    k = ("h", th, ft)
                    i = FT * th + ft
                    o = take(k)
                    if i >= 2:
                        act.wait_ge(s_hg, i - 1)
                    link(act.activation(hrel[:, ft % 2, :], o[:, :], ACT.Relu, bias=b1[:, ft:ft + 1]))
                    act.nop().then_inc(s_free[turns[k][0]], 1)
                    act.nop().then_inc(s_rel, 1)
                rstd(2 * NG + th)

            prelude()
            for i in range(NG * DS):
                decays(i)
                att(i // DS, i % DS)
            for n in range(B):
                act.wait_ge(s_x2, 2 * n + 2)
                if n:
                    act.wait_ge(s_ys, 2 * n)
                act.activation(delta[:, 0, 0:2 * L].rearrange("p (e l) -> p e l", e=2), xres[:, 2 * n:2 * n + 2, :], ACT.Silu).then_inc(s_z, 1)
            for th in range(NG):
                rstd(NG + th)
            for th in range(NG):
                moe(th)

        @block.vector
        def _(dve):
            chain = [0]

            def link(ins):
                chain[0] += 1
                ins.then_inc(s_dve, 1)
                dve.wait_ge(s_dve, chain[0])

            def take(key):
                b_, n = turns[key]
                dve.wait_ge(s_full[b_], n + 1)
                return bank[b_]

            def freed(key, ins):
                ins.then_inc(s_free[turns[key][0]], 1)

            def layer_norm(first, done):
                for tt in range(4):
                    dve.bn_stats(ln_st[:, tt, :], xres[:, first + tt, :]).then_inc(s_dve, 1)
                chain[0] += 4
                dve.wait_ge(s_dve, chain[0])
                for tt in range(4):
                    ins = dve.bn_aggr(ln_mv[:, tt, :], ln_st[:, tt, :])
                    ins.then_inc(s_dve, 1)
                chain[0] += 4
                dve.wait_ge(s_dve, chain[0])
                norms[0] += 1
                dve.nop().then_inc(s_var, 1)
                dve.wait_ge(s_rstd, norms[0])
                for tt in range(4):
                    ins = dve.tensor_scalar(xres[:, first + tt, :], xres[:, first + tt, :], ln_mv[:, tt, 0:1],
                                            ln_r[:, tt:tt + 1], ALU.subtract, ALU.mult)
                    ins.then_inc(done, 1)

            norms = [0]

            def prelude():
                dve.wait_ge(s_ld_ssm, LD_SSM)
                dve.wait_ge(s_pad, 1)
                for et in range(2):
                    dve.wait_ge(s_xpad, 2 * et + 2)
                    v = u[:, et, :].rearrange("p (b l) -> p b l", b=B)
                    link(dve.tensor_scalar(v, xpad[:, et, :, 0:L], convw[:, et, 0:1], convb[:, et:et + 1], ALU.mult, ALU.add))
                    for k in range(1, DC):
                        ins = dve.scalar_tensor_tensor(out=v, in0=xpad[:, et, :, k:k + L], scalar=convw[:, et, k:k + 1],
                                                       in1=v, op0=ALU.mult, op1=ALU.add)
                        if k < DC - 1:
                            link(ins)
                    ins.then_inc(s_conv, 1)
                dve.wait_ge(s_u, 2)
                hi, r1, mid = (gm16[:, :], gr1[:, :], gstk[:, :])
                for th in range(NG):
                    k = ("xdbl", th)
                    o = take(k)
                    c_ = slice(GT_ * th, GT_ * th + GT_)
                    dve.wait_ge(s_dtlo, th + 1)
                    link(dve.tensor_copy(hi, o[0:96, :]))
                    link(dve.tensor_tensor(r1, o[0:96, :], hi, ALU.subtract))
                    dve.tensor_copy(stk[0:32, c_], hi[0:32, :])
                    link(dve.tensor_copy(mid, r1))
                    dve.nop().then_inc(s_free[turns[k][0]], 1)
                    dve.tensor_copy(stk[32:64, c_], mid[32:64, :])
                    link(dve.tensor_tensor(r1[64:96, :], r1[64:96, :], mid[64:96, :], ALU.subtract))
                    link(dve.tensor_copy(stk[64:96, c_], r1[64:96, :]))
                    dve.nop().then_inc(s_stk, 1)
                for et in range(2):
                    dve.wait_ge(s_sp, et + 1)
                    link(dve.scalar_tensor_tensor(out=sp_w, in0=sp_w, scalar=1.0, in1=sp_z, op0=ALU.subtract, op1=ALU.subtract))
                    link(dve.tensor_tensor(sp_l, sp_l, sp_w, ALU.subtract))
                    ins = dve.scalar_tensor_tensor(out=delta[:, et, :], in0=delta[:, et, :], scalar=0.0, in1=sp_l,
                                                   op0=ALU.max, op1=ALU.add)
                    link(ins)
                    dve.nop().then_inc(s_spf, 1)
                    dve.nop().then_inc(s_delta, 1)
                    link(dve.tensor_tensor(du[:, et, :], delta[:, et, :], u[:, et, :], ALU.mult))
                for k in range(2):
                    v = dA[:, k, :].rearrange("p (n l) -> p n l", l=L)[:, :, 0:1]
                    dve.memset(v, 0.0).then_inc(s_dA0, 1)
                dve.wait_ge(s_dA0, 2)

            def states(i):
                th, n = divmod(i, DS)
                c_ = slice(GT_ * th, GT_ * th + GT_)
                dve.wait_ge(s_bb, i + 1)
                ins = dve.tensor_tensor(dBu.rearrange("p (e t) -> p e t", e=2), du[:, :, c_],
                                        bank_b[:, :].unsqueeze(1).broadcast_to([P, 2, GT_]), ALU.mult)
                link(ins)
                dve.nop().then_inc(s_bfree, 1)
                dve.wait_ge(s_dA, 2 * (i + 1))
                ins = dve.tensor_tensor_scan(hst, dA[:, i % 2, :], dBu, 0.0, ALU.mult, ALU.add)
                link(ins)
                dve.nop().then_inc(s_dAuse, 1)
                dve.wait_ge(s_cc, i + 1)
                if i >= 2:
                    dve.wait_ge(s_hcuse, i - 1)
                ins = dve.tensor_tensor(hC[:, i % 2, :].rearrange("p (e t) -> p e t", e=2), hst.rearrange("p (e t) -> p e t", e=2),
                                        bank_c[:, :].unsqueeze(1).broadcast_to([P, 2, GT_]), ALU.mult)
                link(ins)
                dve.nop().then_inc(s_bfree, 1)
                dve.nop().then_inc(s_hc, 1)

            def y_out(th):
                dve.wait_ge(s_y, th + 1)
                c_ = slice(GT_ * th, GT_ * th + GT_)
                for et in range(2):
                    dve.scalar_tensor_tensor(out=u[:, et, c_], in0=u[:, et, c_], scalar=dskip[:, et:et + 1],
                                             in1=bank_y[et][:, :], op0=ALU.mult, op1=ALU.add).then_inc(s_yfree, 1)

            solve_a = ain_g[:, :].rearrange("p (t c s) -> p t c s", t=C, c=CLO)
            solve_t = tt_[:, :].rearrange("p (j c t) -> p j c t", j=C, c=CLO)

            def solve(g, rows):
                for t in rows:
                    if t == 0:
                        dve.wait_ge(s_ain, 128 * (g + 1))
                        if g:
                            dve.wait_ge(s_tdram, 16 * g)
                        link(dve.memset(tt_[:, :], 0.0))
                        flat = tt_[:, :].rearrange("p (j r) -> p j r", j=C)
                        for c in range(CLO):
                            v = tt_[:, C * c:C * c + (CLO * C + 1) * (C - 1) + 1:CLO * C + 1]
                            ins = dve.memset(v, 1.0)
                        link(ins)
                        continue
                    prod = tmp_o[:, 0:CLO * t * t].rearrange("p (c j s) -> p c j s", c=CLO, j=t)
                    a = solve_a[:, t, :, 0:t].unsqueeze(2).broadcast_to([P, CLO, t, t])
                    tv = solve_t[:, 0:t, :, 0:t].rearrange("p j c s -> p c j s")
                    link(dve.tensor_tensor(prod, a, tv, ALU.mult))
                    ov = solve_t[:, 0:t, :, t].rearrange("p j c -> p c j")
                    link(dve.tensor_reduce(ov, prod, AX_X, ALU.add, negate=True))
                    if t == C - 1:
                        dve.nop().then_inc(s_tt, 1)

            def att(g, n):
                if n == 0:
                    if g == 0:
                        dve.wait_ge(s_ld_att, LD_ATT)
                        for t_ in (qE, kE):
                            e = eye16.unsqueeze(1).broadcast_to([P, NU * NC, C])
                            dve.tensor_copy(t_[:, :, :, C:2 * C].rearrange("p u c n -> p (u c) n"), e)
                    for kt in range(KT):
                        ins = dve.tensor_copy(sq[:, D * kt:D * kt + D].rearrange("p (h r) -> p h r", h=H),
                                              wqkvb[:, kt, 3 * D:3 * D + H].unsqueeze(2).broadcast_to([P, H, DH]))
                        ins.then_inc(s_dve, 1)
                    chain[0] += KT
                    dve.wait_ge(s_dve, chain[0])
                    dve.nop().then_inc(s_wb, 1)
                    for j, kind in enumerate("qk"):
                        for half in range(2):
                            k = ("ss" + kind, half, g)
                            o = take(k)
                            r = tmp_o[:, GT_ * half:GT_ * half + GT_]
                            if j or g:
                                pass
                            link(dve.tensor_scalar(r, o[:, :], 1e-24, None, ALU.max))
                            dve.nop().then_inc(s_free[turns[k][0]], 1)
                            dve.nop().then_inc(s_clamp, 1)
                            w = 4 * g + 2 * j + half
                            dve.wait_ge(s_rs, w + 1)
                            k = (kind, half, g)
                            o = take(k)
                            us = slice(GB * half, GB * half + GB)
                            if kind == "q":
                                if g:
                                    take(("O", NU - 1, g - 1))
                                link(dve.tensor_tensor(qE[:, us, :, 0:C].rearrange("p u c n -> p (u c) n"),
                                                       o[:, :].rearrange("p (a n) -> p a n", n=C),
                                                       r.rearrange("p (a n) -> p a n", n=C), ALU.mult))
                                dve.nop().then_inc(s_free[turns[k][0]], 1)
                            else:
                                cs = slice(GT_ * half, GT_ * half + GT_)
                                kh = nuc(k_uv[:, :])[:, us, :, :].rearrange("p u c n -> p (u c) n")
                                link(dve.tensor_tensor(kh, o[:, :].rearrange("p (a n) -> p a n", n=C),
                                                       r.rearrange("p (a n) -> p a n", n=C), ALU.mult))
                                dve.nop().then_inc(s_free[turns[k][0]], 1)
                                link(dve.tensor_copy(kE[:, us, :, 0:C].rearrange("p u c n -> p (u c) n"),
                                                     kh))
                                dve.nop().then_inc(s_ke, 1)
                                dve.wait_ge(s_att, g + 1)
                                link(dve.tensor_tensor(nuc(kb_a_w[:, :])[:, us, :, :].rearrange("p u c n -> p (u c) n"), kh,
                                                       beta[:, cs].rearrange("p (a n) -> p a n", n=C), ALU.mult))
                                dve.nop().then_inc(s_qk, 1)
                    link(dve.tensor_tensor(nuc(vb[:, :]), ucn(tt_[:, :]), ucn(beta[:, :]), ALU.mult))
                    dve.nop().then_inc(s_vb, 1)
                if n == 2:
                    dve.wait_ge(s_exp[0], 128 * (4 * g + 1))
                    for un in range(NU):
                        k = ("A", un, g)
                        o = take(k)[:, :].rearrange("p (c n) -> p c n", c=NC)[:, :, 0:C]
                        dve.tensor_tensor(ucn(kb_a_w[:, :])[:, un, :, :], o, mask_s.unsqueeze(1).broadcast_to([P, NC, C]),
                                          ALU.mult).then_inc(s_acp, 1)
                if n == 3:
                    for un in range(NU):
                        k = ("P", un, g)
                        o = take(k)[:, :].rearrange("p (c n) -> p c n", c=NC)[:, :, 0:C]
                        dve.tensor_tensor(KP[:, un, :, C:2 * C], o, mask_p.unsqueeze(1).broadcast_to([P, NC, C]),
                                          ALU.mult).then_inc(s_kp, 1)
                if 5 <= n < 8:
                    solve(g, range(0, 8) if n == 5 else range(8, 12) if n == 6 else range(12, 16))
                if n == 8:
                    dve.wait_ge(s_adram, 16 * (g + 1))
                    for un in range(NU):
                        k = ("UW", un, g)
                        o = take(k)[:, :].rearrange("p (c n) -> p c n", c=NC)[:, :, C:2 * C]
                        dve.tensor_copy(nuc(kb_a_w[:, :])[:, un, :, :], o).then_inc(s_w, 1)
                if n == 9:
                    for un in range(NU):
                        k = ("GQ", un, g)
                        o = take(k)[:, :].rearrange("p (c n) -> p c n", c=NC)
                        dve.tensor_tensor(nuc(ain_g[:, :])[:, un, :, :], eye16.unsqueeze(1).broadcast_to([P, NC, C]),
                                          o[:, :, 0:C], ALU.subtract).then_inc(s_gt, 1)
                        link(dve.tensor_tensor(qE[:, un, :, 0:C], qE[:, un, :, 0:C], o[:, :, C:2 * C], ALU.subtract))
                        dve.nop().then_inc(s_free[turns[k][0]], 1)
                        dve.nop().then_inc(s_qp, 1)
                if n == 12:
                    dve.wait_ge(s_h, NU * (g + 1))
                    dve.memset(nuc(S_)[:, :, 0, :], 0.0)
                    dve.tensor_copy(nuc(S_)[:, :, 1, :], ucn(H_)[:, :, 0, :]).then_inc(s_s, 1)
                    for c in range(1, NC - 1):
                        k = ("S", c, g)
                        o = take(k)[:, 0:NU * C].rearrange("p (u n) -> p u n", u=NU)
                        link(dve.tensor_tensor(nuc(S_)[:, :, c + 1, :], o, ucn(H_)[:, :, c, :], ALU.add))
                        dve.nop().then_inc(s_free[turns[k][0]], 1)
                        dve.nop().then_inc(s_s, 1)
                if n == 15:
                    for half in range(2):
                        dve.wait_ge(s_or, 2 * g + half + 1)
                        v = tmp_o[:, GT_ * half:GT_ * half + GT_]
                        dve.scalar_tensor_tensor(out=v, in0=v, scalar=onorm[:, 0:1], in1=vb[:, GT_ * half:GT_ * half + GT_],
                                                 op0=ALU.mult, op1=ALU.mult).then_inc(s_on, 1)
                    for tt in range(4):
                        k = ("wo", tt, g)
                        o = take(k)[:, 0:D]
                        link(dve.tensor_tensor(xres[:, 4 * g + tt, :], xres[:, 4 * g + tt, :], o, ALU.add))
                        dve.nop().then_inc(s_free[turns[k][0]], 1)
                    layer_norm(4 * g, s_x2)

            def moe(th):
                k = ("score", th)
                dve.wait_ge(s_sige, th + 1)
                if th == 0:
                    dve.wait_ge(s_ld_ffn, LD_FFN)
                    dve.wait_ge(s_ld_small, 48)
                eb = ebias[:, :].unsqueeze(1).broadcast_to([P, 4, NE])
                link(dve.tensor_tensor(sc[:, :, :], sig[:, :, :], eb, ALU.add))
                ge = rk0.rearrange("p (t e j) -> p t e j", t=4, e=NE)
                gt = rk1.rearrange("p (t e j) -> p t e j", t=4, e=NE)
                s_j = sc[:, :, :].unsqueeze(2).broadcast_to([P, 4, NE, NE])
                s_e = sc[:, :, :].unsqueeze(3).broadcast_to([P, 4, NE, NE])
                dve.tensor_tensor(gt, s_j, s_e, ALU.is_gt)
                link(dve.tensor_tensor(ge, s_j, s_e, ALU.is_ge))
                lm = lmask.unsqueeze(1).broadcast_to([P, 4, NE * NE])
                link(dve.tensor_tensor(rk0.rearrange("p (t n) -> p t n", t=4), rk0.rearrange("p (t n) -> p t n", t=4), lm, ALU.mult))
                link(dve.tensor_tensor(rk0, rk0, rk1, ALU.max))
                link(dve.tensor_reduce(rank[:, :, :], ge, AX_X, ALU.add))
                link(dve.scalar_tensor_tensor(out=sc[:, :, :], in0=rank[:, :, :], scalar=float(KR) - 0.5, in1=sc[:, :, :],
                                              op0=ALU.is_lt, op1=ALU.mult))
                link(dve.tensor_reduce(gsum[:, :], sc[:, :, :], AX_X, ALU.add))
                link(dve.tensor_scalar(gsum[:, :], gsum[:, :], 1e-8, None, ALU.max))
                link(dve.reciprocal(gsum[:, :], gsum[:, :]))
                if th == 0:
                    link(dve.memset(g96[:, :, :], 0.0))
                for r in range(3):
                    dve.memset(g96[:, :, 32 * r:32 * r + NSH], 1.0)
                    ins = dve.tensor_tensor(g96[:, :, 32 * r + NSH:32 * r + NX], sc[:, :, :],
                                            gsum[:, :].unsqueeze(2).broadcast_to([P, 4, NE]), ALU.mult)
                link(ins)
                dve.nop().then_inc(s_g96, 1)
                k = ("gT", th)
                o = take(k)
                hi, r1, mid = gm16[:, :], gr1[:, :], gm16[:, :]
                dve.wait_ge(s_gT, th + 1)
                if th:
                    b_, n_ = turns[("G", th - 1, FT - 1)]
                    dve.wait_ge(s_full[b_], n_ + 1)
                link(dve.tensor_copy(hi, o[0:96, :]))
                dve.tensor_copy(gstk[0:32, :], hi[0:32, :])
                link(dve.tensor_tensor(r1, o[0:96, :], hi, ALU.subtract))
                dve.nop().then_inc(s_free[turns[k][0]], 1)
                link(dve.tensor_copy(mid, r1))
                dve.tensor_copy(gstk[32:64, :], mid[32:64, :])
                link(dve.tensor_tensor(r1[64:96, :], r1[64:96, :], mid[64:96, :], ALU.subtract))
                link(dve.tensor_copy(gstk[64:96, :], r1[64:96, :]))
                dve.nop().then_inc(s_gstk, 1)
                for ft in range(FT):
                    i = FT * th + ft
                    k = ("G", th, ft)
                    o = take(k)
                    dve.wait_ge(s_rel, i + 1)
                    if i >= 2:
                        dve.wait_ge(s_hguse, i - 1)
                    link(dve.tensor_tensor(hg[:, ft % 2, :], hrel[:, ft % 2, :], o[:, :], ALU.mult))
                    dve.nop().then_inc(s_free[turns[k][0]], 1)
                    dve.nop().then_inc(s_hg, 1)
                for tt in range(4):
                    dve.wait_ge(s_yacc, 4 * th + 2 * (tt // 2) + 2)
                    o = bank_y[tt // 2][:, D * (tt % 2):D * (tt % 2) + D]
                    link(dve.scalar_tensor_tensor(out=xres[:, 4 * th + tt, :], in0=xres[:, 4 * th + tt, :], scalar=2.0,
                                                  in1=o, op0=ALU.mult, op1=ALU.add))
                    dve.nop().then_inc(s_yaccfree, 1)
                layer_norm(4 * th, s_last)

            prelude()
            for i in range(NG * DS):
                states(i)
                att(i // DS, i % DS)
                if i % DS == DS - 1:
                    y_out(i // DS)
            dve.wait_ge(s_yfree, 2 * NG)
            for n in range(B):
                dve.wait_ge(s_z, n + 1)
                zv = delta[:, 0, 0:2 * L].rearrange("p (e l) -> p e l", e=2)
                yv = u[:, :, L * n:L * n + L]
                link(dve.tensor_tensor(yv, yv, zv, ALU.mult))
                dve.nop().then_inc(s_ys, 2)
            for th in range(NG):
                for bb in range(GB):
                    for lt in range(2):
                        k = ("yT", th, bb, lt)
                        o = take(k)[:, 0:D]
                        n = 4 * th + 2 * bb + lt
                        link(dve.tensor_tensor(xres[:, n, :], xres[:, n, :], o, ALU.add))
                        dve.nop().then_inc(s_free[turns[k][0]], 1)
                layer_norm(4 * th, s_x3)
            for th in range(NG):
                moe(th)


_OUTS = [((4, 256, 256), "float32")]


def kernel(**inputs):
    import numpy as np
    import ml_dtypes
    import concourse.bacc as bacc
    from concourse.bass_utils import run_bass_kernel_spmd

    v = {k: np.asarray(a) for k, a in inputs.items()}
    wide = np.zeros((D, 104), np.float32)
    xp = v["L0_xattn_x_proj_w"]
    for r in range(3):
        wide[:, 32 * r:32 * r + 2 * DS] = xp[DR:].T
    wide[:, 96:96 + DR] = xp[:DR].T

    def side_by_side(shared, routed):
        return np.concatenate([shared, routed], axis=0)

    w1 = np.zeros((D, FP), np.float32)
    w1[:, :NX * DFF] = side_by_side(v["L0_ffn_shared_w1"], v["L0_ffn_routed_w1"]).transpose(1, 0, 2).reshape(D, NX * DFF)
    b1 = np.zeros((FP,), np.float32)
    b1[:NX * DFF] = side_by_side(v["L0_ffn_shared_b1"], v["L0_ffn_routed_b1"]).reshape(-1)
    w2 = np.zeros((FP, D), np.float32)
    w2[:NX * DFF] = side_by_side(v["L0_ffn_shared_w2"], v["L0_ffn_routed_w2"]).reshape(NX * DFF, D)
    b2 = side_by_side(v["L0_ffn_shared_b2"], v["L0_ffn_routed_b2"])

    const = np.zeros((P, C_ALL), np.float32)
    row, col = np.arange(P)[:, None], np.arange(P)[None, :]
    c16 = np.arange(C)[None, :]
    const[:, C_ID:C_ID + P] = row == col
    const[:, C_BLK:C_BLK + P] = row // DH == col // DH
    const[:, C_E:C_E + C] = row % C == c16
    const[:, C_MS:C_MS + C] = c16 < row % C
    const[:, C_MP:C_MP + C] = c16 >= row % C
    const[:, C_BIAS + BI_ONE] = 1.0
    const[:, C_BIAS + BI_EPS] = EPS
    const[:, C_BIAS + BI_K] = 0.5 * SCALE_LOG2 * LN2
    const[:, C_BIAS + BI_Q] = 0.5 * SCALE_LOG2 * LN2 - 2 * LN2
    lmask = np.tile((np.arange(NE)[None, :] < np.arange(NE)[:, None]).reshape(1, -1), (P, 1)).astype(np.float32)
    eye3 = (np.arange(96)[:, None] % 32 == np.arange(2 * DS)[None, :]).astype(ml_dtypes.bfloat16)
    sel = (np.arange(96)[:, None] % 32 == np.arange(FP)[None, :] // DFF).astype(ml_dtypes.bfloat16)

    arrays = {
        "x_tok": v["x"].reshape(T, D),
        "x_t": v["x"].reshape(T, D).T,
        "ctx_t": v["ctx_1024"].reshape(T, DM).T,
        "wqkvb": np.concatenate([v["L0_attn_Wq"], v["L0_attn_Wk"], v["L0_attn_Wv"], v["L0_attn_Wb"]], axis=1),
        "onorm": np.tile(v["L0_attn_o_norm_weight"], HH).reshape(P, 1),
        "wo": v["L0_attn_Wo"],
        "inproj": v["L0_xattn_in_proj_w"].T,
        "convw": v["L0_xattn_conv_w"],
        "convb": v["L0_xattn_conv_b"].reshape(2, P).T,
        "xproj": wide,
        "dtproj": v["L0_xattn_dt_proj_w"].T,
        "dtb": v["L0_xattn_dt_proj_b"].reshape(2, P).T,
        "alog": v["L0_xattn_A_log"],
        "dskip": v["L0_xattn_D"].reshape(2, P).T,
        "w1": w1,
        "b1": b1.reshape(FT, P).T,
        "w2": w2,
        "b2": b2,
        "cent": v["L0_ffn_centroids"].T,
        "ebias": v["L0_ffn_bias"],
        "const": const,
        "eye3": eye3,
        "sel": sel,
        "lmask": lmask,
    }
    arrays = {f"in_{k}": np.ascontiguousarray(a) for k, a in arrays.items()}
    nc = bacc.Bacc("TRN2", target_bir_lowering=False, num_devices=1)
    args = [nc.dram_tensor(k, a.shape, mybir.dt.from_np(a.dtype), kind="ExternalInput").ap() for k, a in arrays.items()]
    out = nc.dram_tensor("out_0", (T, D), F32, kind="ExternalOutput").ap()
    decoder_layer(nc, *args, out)
    r = run_bass_kernel_spmd(nc, [arrays], core_ids=[0])
    return r.results[0]["out_0"].reshape(B, L, D)
```

```python
from contextlib import ExitStack

import concourse.bass as bass
from concourse import mybir

F32 = mybir.dt.float32
BF16 = mybir.dt.bfloat16
F32R = mybir.dt.float32r
ALU = mybir.AluOpType
ACT = mybir.ActivationFunctionType
AX_X = mybir.AxisListType.X

P = 128
B, L, D = 4, 256, 256
T = B * L
KT = D // P
H, DH = 16, 16
HH = P // DH
C = 16
NC = L // C
W3 = 3 * C
CH = NC // 2
CLO = 2
BL = 2 * L
GB = 2
GT_ = GB * L
NG = B // GB
DM, DS, DC, DR = 128, 16, 4, 8
DI = 2 * DM
LP = L + DC - 1
NE, NSH, KR, DFF = 16, 2, 4, 176
NX = NE + NSH
FT = -(-NX * DFF // P)
FP = FT * P
EPS = 1e-5
LN2 = 0.6931471805599453
SCALE_LOG2 = 20
LN_EXP = "natural_log_exp_and_others"

C_ID, C_BLK, C_E, C_MA, C_MP, C_BIAS = 0, 128, 256, 272, 288, 304
BI_ONE, BI_EPS, BI_K, BI_Q = range(4)
C_ALL = C_BIAS + 4

NREC = NC - 2
ATTENTION = [("v", 1.7, 1.5), ("b", 1.7, 0), ("k", 2.2, 1), ("ssk", 0.9, 0), ("q", 1.7, 1), ("ssq", 0.4, 2),
             ("move_k", 0, 7),
             ("P0", 1.7, 0), ("P1", 1.7, 0), ("P2", 1.7, 0), ("P3", 1.7, 2), ("move_a", 0, 7),
             ("solve0", 0, 3), ("solve1", 0, 1), ("solve2", 0, 4), ("move_t", 0, 8), ("turn_t", 0, 2), ("expand_t", 0, 6),
             ("UW0", 3.4, 0), ("UW1", 3.4, 1), ("expand_w", 0, 0.5), ("H", 8.8, 5),
             ("GQ0", 3.4, 1), ("GQ1", 2.9, 1), ("expand_gu", 2, 6.5)]
ATTENTION += [(f"S{c}", 0.5, 1.5) for c in range(1, NREC + 1)]
ATTENTION += [("expand_s", 0, 7.5), ("O0", 7.8, 0), ("O1", 8.8, 1), ("ms", 0.9, 2), ("wo", 1.7, 0.5), ("ln", 2, 7)]
NITER = NG * DS
MIDDLE = [("gate", 0, 4), ("yT", 2, 5), ("x3T", 2, 1)]


def order():
    first = [("iter", i) for i in range(NITER)]
    chains = {x: [(n, b, pe, late) for b in range(x, B, 2) for n, pe, late in ATTENTION] for x in range(2)}
    chains[0] = chains[0][PRELUDE:]
    chains["ssm"] = [s for i in range(NITER) for s in
                     [("pre", i, .5, 0), ("run", i, .5, SSM_PERIOD)] + [("y_out", i // DS, 0, 4)] * (i % DS == DS - 1)]
    chains["mid"] = [(n, 0, pe, late) for n, pe, late in MIDDLE]
    ready = {0: 0, 1: SECOND, "ssm": 0, "mid": 0}
    done, steps, now = set(), [], 0
    while any(chains.values()):
        open_ = [c for c in chains if chains[c] and (c != "mid" or {("ln", 0), ("ln", 1), ("y_out", 0)} <= done)]
        c = min(open_, key=lambda c: (max(ready[c], now), ["mid", "ssm", 0, 1].index(c)))
        name, which, pe, late = chains[c].pop(0)
        now = max(now, ready[c]) + pe
        ready[c] = now + late
        steps.append((name, which))
        done.add((name, which))
    return steps


PRELUDE = 6
SECOND = 0
SSM_PERIOD = 8
STEPS = order()

GATE_PARTS = 8
GATE_AT = [3, 4, 5, 6, 7, 8, 10, 11]
LAST_NORM_AT = 3


def bank_turns():
    used = [0] * 8
    turns = {}
    ring = [0]
    held = set()

    def take(key, bank=None):
        if bank is None:
            while (bank := (2, 5, 6, 7)[ring[0] % 4]) in held:
                ring[0] += 1
            ring[0] += 1
        turns[key] = (bank, used[bank])
        used[bank] += 1

    def step(name, b):
        if name[0] in "vbkqPUHGSms" and name not in ("move_k", "move_a", "move_t", "solve0", "solve1", "solve2"):
            take((name, b))
        if name in ("k", "q"):
            held.add(turns[(name, b)][0])
        if name in ("ssk", "ssq"):
            held.remove(turns[(name[2], b)][0])
        if name == "O0":
            take(("O", b))
            held.add(turns[("O", b)][0])
        if name == "O1":
            held.remove(turns[("O", b)][0])
        if name == "wo":
            take((name, b))

    def mid(th):
        for n in range(4):
            take(("yT", th, n))
        for n in range(4):
            take(("x3T", th, n))

    for et in range(2):
        for th in range(NG):
            take(("xe", et, th), 1 + 2 * et + th)
    for n, _, _ in ATTENTION[:PRELUDE]:
        step(n, 0)
    for th in range(NG):
        take(("xdbl", th), 1 + th)
    for et in range(2):
        for th in range(NG):
            take(("dt", et, th), 3 + th)
    for name, b in STEPS:
        if name == "yT":
            for n in range(4):
                take(("yT", b, n))
        elif name == "x3T":
            for n in range(4):
                take(("x3T", b, n))
        elif name not in ("pre", "run", "y_out", "gate"):
            step(name, b)
    mid(1)
    for th in range(NG):
        take(("score", th), 7)
        take(("gT", th), 0)
        for ft in range(FT):
            take(("h", th, ft), 5 + ft % 2)
            take(("G", th, ft), 1 + ft % 2)
    return turns


def decoder_layer(nc, x_tok_d, x_t_d, ctx_t_d, wqkvb_d, onorm_d, wo_d, inproj_d, convw_d, convb_d, xproj_d,
                  dtproj_d, dtb_d, alog_d, dskip_d, w1_d, b1_d, w2_d, b2_d, cent_d, ebias_d, const_d, eye3_d,
                  sel_d, lmask_d, out_d):
    turns = bank_turns()
    scr_a = nc.dram_tensor("scr_a", (B, P, BL), F32).ap()
    scr_t = nc.dram_tensor("scr_t", (B, P, C * CLO * C), F32).ap()
    scr_b = nc.dram_tensor("scr_b", (B, HH, BL), F32).ap()

    with ExitStack() as ctx:
        def sb(name, shape, dt=F32):
            return ctx.enter_context(nc.sbuf_tensor(name, shape, dt))

        def sem(name):
            return ctx.enter_context(nc.semaphore(name))

        def sems(name, n=2):
            return [sem(f"{name}{i}") for i in range(n)]

        bank = [ctx.enter_context(nc.psum_tensor(f"bank{i}", [P, 512], F32)) for i in range(8)]
        bank_b, bank_c, bank_y = bank[0], bank[1], bank[3:5]

        xT = sb("xT", [P, KT, T])
        xres = sb("xres", [P, 8, D])
        wb16 = sb("wb16", [P, KT, D])
        wo = sb("wo", [P, 2, D])
        onorm = sb("onorm", [P, 1])
        const = sb("const", [P, C_ALL])
        eye3 = sb("eye3", [96, 2 * DS], BF16)
        inproj = sb("inproj", [P, DI])
        convw = sb("convw", [P, 2, DC])
        convb = sb("convb", [P, 2])
        xproj = sb("xproj", [P, 2, 104])
        dtproj = sb("dtproj", [P, DI])
        dtb = sb("dtb", [P, 2])
        alog = sb("alog", [P, 2, DS])
        dskip = sb("dskip", [P, 2])
        stk = sb("stk", [96, T], BF16)
        negA = sb("negA", [P, 2, DS])
        qke = [sb(f"qke{x}", [P, 2, NC, W3]) for x in range(2)]
        vkp = [sb(f"vkp{x}", [P, 2, NC, W3]) for x in range(2)]
        beta_kc = [sb(f"beta_kc{x}", [P, BL]) for x in range(2)]
        at_g = [sb(f"at_g{x}", [P, BL]) for x in range(2)]
        tt_s = [sb(f"tt_s{x}", [P, BL]) for x in range(2)]
        tmp_o = [sb(f"tmp_o{x}", [P, BL]) for x in range(2)]
        hh = [sb(f"hh{x}", [P, BL]) for x in range(2)]
        binst = [sb(f"binst{x}", [P, CLO * C]) for x in range(2)]
        ln_st = sb("ln_st", [P, 4, 6])
        ln_mv = sb("ln_mv", [P, 4, 2])
        ln_r = sb("ln_r", [P, 4])
        b1 = sb("b1", [P, FT])
        cent = sb("cent", [P, KT, NE])
        ebias = sb("ebias", [P, NE])
        sig = sb("sig", [P, 4, NE])
        sc = sb("sc", [P, 4, NE])
        rank = sb("rank", [P, 4, NE])
        gsum = sb("gsum", [P, 4])

        layer = ctx.enter_context(ExitStack())

        def sb_of_layer(name, shape, dt=F32):
            return layer.enter_context(nc.sbuf_tensor(name, shape, dt))

        bd_all = sb_of_layer("bd_all", [P, 2, 2, P, 2 * NC])
        arena_s = sb_of_layer("arena_s", [P, 8 * GT_])
        arena_h = sb_of_layer("arena_h", [P, 6 * GT_])
        bsb = sb_of_layer("bsb", [P, 2, GT_])
        du = sb_of_layer("du", [P, 2, T])
        delta = sb_of_layer("delta", [P, 2, T])
        u = sb_of_layer("u", [P, 2, T])
        wqkvb = sb_of_layer("wqkvb", [P, KT, 3 * D + H])
        k_uv = [sb_of_layer(f"k_uv{x}", [P, BL]) for x in range(2)]
        v_w = [sb_of_layer(f"v_w{x}", [P, BL]) for x in range(2)]
        layer.close()
        half_blocks = 2 * P * 2 * NC
        w1 = sb_of_layer("w1", [P, KT, FP])
        sel = sb_of_layer("sel", [96, FP], BF16)
        sb_of_layer("pad_b0", [P, half_blocks - KT * FP - FP // 2])
        w2 = sb_of_layer("w2", [P, FT, D])
        b2 = sb_of_layer("b2", [NX, D])
        lmask = sb_of_layer("lmask", [P, NE * NE])
        layer.close()
        spare = (half_blocks - FT * D - D - NE * NE) // D
        w1_lo = sb_of_layer("w1_lo", [P, KT, FP], F32R)
        sb_of_layer("pad_c0", [P, half_blocks - KT * FP])
        w2_lo = sb_of_layer("w2_lo", [P, FT, D], F32R)
        sb_of_layer("pad_c1", [P, half_blocks - FT * D - spare * D])
        w2_hi_a = sb_of_layer("w2_hi_a", [P, spare, D], F32R)
        w1_hi = sb_of_layer("w1_hi", [P, KT, FP], F32R)
        beside = (8 * GT_ + 6 * GT_ + 2 * GT_ + 2 * T - KT * FP) // D
        w2_hi_b = sb_of_layer("w2_hi_b", [P, beside, D], F32R)
        x_hl = [sb_of_layer(f"x_hl{th}", [P, 2, KT, GT_], F32R) for th in range(NG)]
        w2_hi_c = sb_of_layer("w2_hi_c", [P, FT - spare - beside, D], F32R)
        sb_of_layer("pad_c2", [P, KT * (3 * D + H) - (FT - spare - beside) * D])
        hg_hi = [sb_of_layer(f"hg_hi{x}", [P, GT_], F32R) for x in range(2)]
        hg_lo = [sb_of_layer(f"hg_lo{x}", [P, GT_], F32R) for x in range(2)]
        w2_runs = [(0, w2_hi_b), (beside, w2_hi_a), (beside + spare, w2_hi_c)]

        def w2_hi(ft):
            at, place = [r for r in w2_runs if r[0] <= ft][-1]
            return place[:, ft - at, :]

        ident = const[:, C_ID:C_ID + P]
        blk = const[:, C_BLK:C_BLK + P]
        eye16 = const[:, C_E:C_E + C]
        mask_a = const[:, C_MA:C_MA + C]
        mask_p = const[:, C_MP:C_MP + C]

        def bias_col(i):
            return const[:, C_BIAS + i:C_BIAS + i + 1]

        xpad = arena_s[:, 0:2 * B * LP].rearrange("p (e b l) -> p e b l", e=2, b=B)
        ctxT = arena_s[:, 2 * B * LP:2 * B * LP + T]
        dA = arena_s[:, 0:4 * GT_].rearrange("p (k n) -> p k n", k=2)
        dBu = arena_s[:, 4 * GT_:8 * GT_].rearrange("p (k n) -> p k n", k=2)
        sp_z = arena_h[:, 0:T]
        sp_w = arena_h[:, T:2 * T]
        sp_l = arena_h[:, 2 * T:3 * T]
        hst = arena_h[:, 0:2 * GT_]
        hC = arena_h[:, 2 * GT_:4 * GT_]

        sq = hh
        dtlo = arena_h[:, 0:T]

        def hcn(t):
            return t.rearrange("p (h c n) -> p h c n", h=2, c=NC)

        def nhc(t):
            return t.rearrange("p (n h c) -> p h c n", n=C, h=2)


        def flat(t):
            return t[:, :, :, :].rearrange("p h c n -> p (h c n)")

        rk0 = flat(qke[0])[:, 0:4 * NE * NE]
        rk1 = flat(qke[1])[:, 0:4 * NE * NE]
        g96 = flat(qke[0])[:, 4 * NE * NE:4 * NE * NE + 4 * 96].rearrange("p (t n) -> p t n", t=4)
        hrel = flat(vkp[0])[:, 0:2 * GT_].rearrange("p (k n) -> p k n", k=2)
        gT = [tmp_o[x][0:32, :] for x in range(2)]
        gr1 = sq[0][0:96, :]
        gm16 = at_g[0][0:96, 0:GT_ // 2].bitcast(BF16)
        gstk = [t[0:96, 0:GT_ // 2].bitcast(BF16) for t in (at_g[1], beta_kc[0])]

        s_ld_ssm = sem("s_ld_ssm")
        s_ld_c = sem("s_ld_c")
        s_ld_att = sem("s_ld_att")
        s_ld_w1 = sem("s_ld_w1")
        s_ld_w2 = sem("s_ld_w2")
        s_w1hi = sem("s_w1hi")
        s_w1lo = sem("s_w1lo")
        s_w2hi = sem("s_w2hi")
        s_w2lo = sem("s_w2lo")
        s_xhi = sem("s_xhi")
        s_xlo = sem("s_xlo")
        s_ld_small = sem("s_ld_small")
        s_full = sems("s_full", 8)
        s_free = sems("s_free", 8)
        s_pad = sem("s_pad")
        s_xpad = sem("s_xpad")
        s_conv = sem("s_conv")
        s_u = sem("s_u")
        s_dtlo = sem("s_dtlo")
        s_stk = sem("s_stk")
        s_sp = sem("s_sp")
        s_spf = sem("s_spf")
        s_delta = sem("s_delta")
        s_du = sem("s_du")
        s_act = sem("s_act")
        s_dve = sem("s_dve")
        s_dA0 = sem("s_dA0")
        s_dA = sem("s_dA")
        s_scan = sem("s_scan")
        s_bb = sem("s_bb")
        s_bcopy = sem("s_bcopy")
        s_dbu = sem("s_dbu")
        s_cc = sem("s_cc")
        s_hc = sem("s_hc")
        s_yfree = sem("s_yfree")
        s_zero = sem("s_zero")
        s_wb = sem("s_wb")
        s_eye = sem("s_eye")
        s_beta = sems("s_beta")
        s_bdram = sems("s_bdram")
        s_binst = sems("s_binst")
        s_v = sems("s_v")
        s_sq = sems("s_sq")
        s_clamp = sems("s_clamp")
        s_rs = sems("s_rs")
        s_k = sems("s_k")
        s_qk = sems("s_qk")
        s_exp = [sems(f"s_exp{x}_") for x in range(2)]
        s_at = sems("s_at")
        s_adram = sems("s_adram")
        s_ain = sems("s_ain")
        s_kc = sems("s_kc")
        s_pt = sems("s_pt")
        s_vc = sems("s_vc")
        s_tt = sems("s_tt")
        s_tdram = sems("s_tdram")
        s_tcp = sems("s_tcp")
        s_tperm = sems("s_tperm")
        s_uv = sems("s_uv")
        s_w = sems("s_w")
        s_gq = sems("s_gq")
        s_s = sems("s_s")
        s_ot = sems("s_ot")
        s_osq = sems("s_osq")
        s_or = sems("s_or")
        s_on = sems("s_on")
        s_var = sem("s_var")
        s_rstd = sem("s_rstd")
        s_x2 = sems("s_x2_", B)
        s_z = sem("s_z")
        s_ys = sem("s_ys")
        s_x3 = sem("s_x3")
        s_x3T = sem("s_x3T")
        s_sige = sem("s_sige")
        s_g96 = sem("s_g96")
        s_gT = sem("s_gT")
        s_gstk = sem("s_gstk")
        s_rel = sem("s_rel")
        s_hg = sem("s_hg")
        s_hguse = sem("s_hguse")
        s_yacc = sem("s_yacc")
        s_yaccfree = sem("s_yaccfree")
        s_last = sem("s_last")
        s_out = sem("s_out")

        block = ctx.enter_context(nc.Block())

        LD_SSM, LD_C, LD_ATT, LD_W1, LD_W2 = 8 * 16, 3 * 16, 3 * 16, 2 * 16, 3 * 16

        @block.sync
        def _(sp):
            def load(dst, src, s):
                sp.dma_start(dst, src).then_inc(s, 16)

            load(ctxT, ctx_t_d, s_ld_ssm)
            load(inproj[:, :], inproj_d, s_ld_ssm)
            load(convw[:, :, :], convw_d.rearrange("(e p) k -> p e k", p=P), s_ld_ssm)
            load(convb[:, :], convb_d, s_ld_ssm)
            load(xproj[:, :, :], xproj_d.rearrange("(e p) k -> p e k", p=P), s_ld_ssm)
            load(dtproj[96:96 + DR, :], dtproj_d, s_ld_ssm)
            load(dtb[:, :], dtb_d, s_ld_ssm)
            load(alog[:, :, :], alog_d.rearrange("(e p) n -> p e n", p=P), s_ld_ssm)
            load(const[:, :], const_d, s_ld_c)
            load(wqkvb[:, :, :], wqkvb_d.rearrange("(k p) n -> p k n", p=P), s_ld_c)
            load(xT[:, :, :], x_t_d.rearrange("(k p) t -> p k t", p=P), s_ld_c)
            load(eye3[:, :], eye3_d, s_ld_att)
            load(xres[:, :, :], x_tok_d.rearrange("(n p) d -> p n d", p=P), s_ld_att)
            load(wo[:, :, :], wo_d.rearrange("(k p) n -> p k n", p=P), s_ld_att)

            def read(key):
                b_, n = turns[key]
                sp.wait_ge(s_full[b_], n + 1)

            def heads():
                for h in range(HH):
                    yield h, slice(DH * h, DH * h + DH)

            def expand(x, k, src):
                for h, r in heads():
                    sp.dma_start(bd_all[r, x, k, r, :].rearrange("p m n -> p (m n)"), src[r, :]).then_inc(s_exp[x][k], 16)

            def step(name, b):
                x, n = b % 2, b // 2
                if name == "move_k":
                    sp.wait_ge(s_zero, 2 * x + 2)
                    sp.wait_ge(s_k[x], n + 1)
                    if n:
                        read(("O", b - 2))
                    expand(x, 1, k_uv[x])
                    sp.wait_ge(s_beta[x], n + 1)
                    sp.dma_start(scr_b[b], beta_kc[x][0:P:DH, :]).then_inc(s_bdram[x], 16)
                    sp.wait_ge(s_bdram[x], 16 * (n + 1))
                    sp.dma_start(binst[x][:, :], scr_b[b].rearrange("h (i e) -> (h i) e", i=16)).then_inc(s_binst[x], 16)
                if name == "move_a":
                    sp.wait_ge(s_at[x], 4 * (n + 1))
                    sp.dma_start(scr_a[b], at_g[x][:, :]).then_inc(s_adram[x], 16)
                    sp.wait_ge(s_adram[x], 16 * (n + 1))
                    for h, r in heads():
                        sp.dma_start(at_g[x][r, :].rearrange("i (t e) -> i t e", t=C),
                                     scr_a[b, r, :].rearrange("t (i e) -> i t e", i=16)).then_inc(s_ain[x], 16)
                    sp.wait_ge(s_kc[x], 4 * (n + 1))
                    expand(x, 0, beta_kc[x])
                if name == "move_t":
                    sp.wait_ge(s_tt[x], n + 1)
                    sp.dma_start(scr_t[b], tt_s[x][:, :]).then_inc(s_tdram[x], 16)
                    sp.wait_ge(s_tdram[x], 16 * (n + 1))
                    for h, r in heads():
                        sp.dma_start(at_g[x][r, :].rearrange("p (i e) -> p i e", i=16),
                                     scr_t[b, r, :].rearrange("i (j e) -> j i e", j=C)).then_inc(s_tcp[x], 16)
                if name == "expand_t":
                    sp.wait_ge(s_tperm[x], n + 1)
                    expand(x, 1, tt_s[x])
                if name == "expand_w":
                    sp.wait_ge(s_w[x], 2 * (n + 1))
                    expand(x, 1, v_w[x])
                if name == "expand_gu":
                    sp.wait_ge(s_gq[x], 4 * (n + 1))
                    expand(x, 0, at_g[x])
                    expand(x, 1, k_uv[x])
                if name == "expand_s":
                    sp.wait_ge(s_s[x], (NC - 1) * (n + 1))
                    expand(x, 0, tt_s[x])
                if (name, b) == ("ln", B - 2):
                    read(("O", B - 2))
                    load(w1[:, :, :], w1_d.rearrange("(k p) f -> p k f", p=P), s_ld_w1)
                    load(sel[:, :], sel_d, s_ld_w1)

            for name, which in STEPS:
                step(name, which)
            read(("O", B - 1))
            load(w2[:, :, :], w2_d.rearrange("(f p) d -> p f d", p=P), s_ld_w2)
            load(b2[:, :], b2_d, s_ld_w2)
            load(lmask[:, :], lmask_d, s_ld_w2)
            for n in range(8):
                sp.wait_ge(s_last, n + 1)
                sp.dma_start(out_d[P * n:P * (n + 1), :], xres[:, n, :]).then_inc(s_out, 16)
            sp.wait_ge(s_out, 16 * 8)

        @block.gpsimd
        def _(pool):
            pool.memset(xpad[:, :, :, 0:DC - 1], 0.0).then_inc(s_pad, 1)
            for x in range(2):
                for k in range(2):
                    pool.memset(bd_all[:, x, k, :, :], 0.0).then_inc(s_zero, 1)
            pool.dma_start(dskip[:, :], dskip_d).then_inc(s_ld_small, 16)
            pool.dma_start(onorm[:, :], onorm_d).then_inc(s_ld_small, 16)
            pool.dma_start(b1[:, :], b1_d).then_inc(s_ld_small, 16)
            pool.dma_start(cent[:, :, :], cent_d.rearrange("(k p) e -> p k e", p=P)).then_inc(s_ld_small, 16)
            pool.dma_start(ebias[:, :], ebias_d.rearrange("(a e) -> a e", a=1).partition_broadcast(P)).then_inc(s_ld_small, 16)
            pool.wait_ge(s_du, 2)
            for i in range(NITER):
                th = i // DS
                pool.wait_ge(s_bcopy, i + 1)
                if i >= 2:
                    pool.wait_ge(s_scan, i - 1)
                pool.tensor_tensor(dBu[:, i % 2, :].rearrange("p (e t) -> p e t", e=2), du[:, :, GT_ * th:GT_ * th + GT_],
                                   bsb[:, i % 2, :].unsqueeze(1).broadcast_to([P, 2, GT_]), ALU.mult).then_inc(s_dbu, 1)
            pool.wait_ge(s_yfree, 2 * NG)
            pool.wait_ge(s_ld_w1, LD_W1)
            for kt in range(KT):
                pool.tensor_copy(w1_hi[:, kt, :], w1[:, kt, :]).then_inc(s_w1hi, 1)
                pool.wait_ge(s_w1hi, kt + 1)
                pool.tensor_tensor(w1_lo[:, kt, :], w1[:, kt, :], w1_hi[:, kt, :], ALU.subtract).then_inc(s_w1lo, 1)
            b_, n_ = turns[("ssq", B - 1)]
            pool.wait_ge(s_full[b_], n_ + 1)
            pool.wait_ge(s_ld_w2, LD_W2)
            for n, (at, place) in enumerate(w2_runs):
                part = slice(at, at + place.shape[1])
                pool.tensor_copy(place[:, :, :], w2[:, part, :]).then_inc(s_w2hi, 1)
                pool.wait_ge(s_w2hi, n + 1)
                pool.tensor_tensor(w2_lo[:, part, :], w2[:, part, :], place[:, :, :], ALU.subtract).then_inc(s_w2lo, 1)

        @block.tensor
        def _(pe):
            def fill(key):
                b_, n = turns[key]
                if n:
                    pe.wait_ge(s_free[b_], n)
                return bank[b_]

            def filled(key, mm):
                mm.then_inc(s_full[turns[key][0]], 1)

            def conv_input():
                pe.wait_ge(s_ld_ssm, LD_SSM)
                for et in range(2):
                    for th in range(NG):
                        k = ("xe", et, th)
                        filled(k, pe.matmul(fill(k)[:, :], inproj[:, P * et:P * et + P],
                                            ctxT[:, GT_ * th:GT_ * th + GT_], start=True, stop=True))

            def dt_rows():
                pe.wait_ge(s_u, 2)
                for th in range(NG):
                    k = ("xdbl", th)
                    o = fill(k)
                    for et in range(2):
                        mm = pe.matmul(o[0:104, :], xproj[:, et, :], u[:, et, GT_ * th:GT_ * th + GT_],
                                       start=(et == 0), stop=(et == 1))
                    filled(k, mm)
                pe.wait_ge(s_dtlo, NG)
                for et in range(2):
                    for th in range(NG):
                        k = ("dt", et, th)
                        filled(k, pe.matmul(fill(k)[:, :], dtproj[96:96 + DR, P * et:P * et + P],
                                            dtlo[96:96 + DR, GT_ * th:GT_ * th + GT_], start=True, stop=True))

            def broadcast_b(i):
                th, n = divmod(i, DS)
                if i:
                    pe.wait_ge(s_bcopy, i)
                pe.matmul(bank_b[:, :], eye3[:, n:n + 1].broadcast_to([96, P]), stk[:, GT_ * th:GT_ * th + GT_],
                          start=True, stop=True).then_inc(s_bb, 1)

            def broadcast_c(i):
                th, n = divmod(i, DS)
                if i:
                    pe.wait_ge(s_hc, i)
                pe.matmul(bank_c[:, :], eye3[:, DS + n:DS + n + 1].broadcast_to([96, P]), stk[:, GT_ * th:GT_ * th + GT_],
                          start=True, stop=True).then_inc(s_cc, 1)

            def blocks(x, k, half, c):
                return bd_all[:, x, k, :, NC * half + c]

            def step(name, b):
                x, n = b % 2, b // 2
                cols = slice(L * b, L * b + L)
                if name in ("v", "b", "k", "q"):
                    if (name, b) == ("v", 0):
                        pe.wait_ge(s_ld_c, LD_C)
                    if (name, b) == ("b", 0):
                        pe.wait_ge(s_wb, 1)
                    k = (name, b)
                    o = fill(k)
                    for half in range(2):
                        to = o[:, :].rearrange("p (c w j) -> p w c j", c=NC, w=2)[:, half, :, :] if name == "v" \
                            else o[:, L * half:L * half + L]
                        for kt in range(KT):
                            if name == "b":
                                w = wb16[:, kt, P * half:P * half + P]
                            else:
                                at = {"q": 0, "k": D, "v": 2 * D}[name] + P * half
                                w = wqkvb[:, kt, at:at + P]
                            mm = pe.matmul(to, w, xT[:, kt, cols], start=(kt == 0), stop=(kt == KT - 1))
                    filled(k, mm)
                if name in ("ssk", "ssq"):
                    k = (name, b)
                    o = fill(k)
                    pe.wait_ge(s_sq[x], 2 * n + (name == "ssq") + 1)
                    filled(k, pe.matmul(o[:, :], blk, sq[x][:, :], start=True, stop=True))
                if name[0] == "P":
                    half, ch = divmod(int(name[1]), 2)
                    if name == "P0":
                        pe.wait_ge(s_exp[x][1], 128 * (4 * n + 1))
                        pe.wait_ge(s_qk[x], n + 1)
                    k = (name, b)
                    o = fill(k)
                    for j in range(CH):
                        c = CH * ch + j
                        mm = pe.matmul(o[:, W3 * j:W3 * j + W3], blocks(x, 1, half, c), qke[x][:, half, c, :], start=True, stop=True)
                    filled(k, mm)
                if name[:2] == "UW":
                    pe.wait_ge(s_exp[x][1], 128 * (4 * n + 2))
                    pe.wait_ge(s_kc[x], 4 * (n + 1))
                    pe.wait_ge(s_vc[x], n + 1)
                    half = int(name[2])
                    k = (name, b)
                    o = fill(k)
                    for c in range(NC):
                        mm = pe.matmul(o[:, 2 * C * c:2 * C * c + 2 * C], blocks(x, 1, half, c), vkp[x][:, half, c, 0:2 * C], start=True, stop=True)
                    filled(k, mm)
                if name == "H":
                    pe.wait_ge(s_exp[x][0], 128 * (3 * n + 1))
                    pe.wait_ge(s_uv[x], 2 * (n + 1))
                    k = (name, b)
                    o = fill(k)
                    for half in range(2):
                        for c in range(NC):
                            at = L * half + C * c
                            mm = pe.matmul(o[:, at:at + C], blocks(x, 0, half, c), nhc(k_uv[x][:, :])[:, half, c, :], start=True, stop=True)
                    filled(k, mm)
                if name[:2] == "GQ":
                    pe.wait_ge(s_exp[x][1], 128 * (4 * n + 3))
                    half = int(name[2])
                    k = (name, b)
                    o = fill(k)
                    for c in range(NC):
                        mm = pe.matmul(o[:, 2 * C * c:2 * C * c + 2 * C], blocks(x, 1, half, c), vkp[x][:, half, c, C:W3], start=True, stop=True)
                    filled(k, mm)
                if name[0] == "S":
                    c = int(name[1:])
                    if c == 1:
                        pe.wait_ge(s_exp[x][0], 128 * (3 * n + 2))
                    k = (name, b)
                    o = fill(k)
                    pe.wait_ge(s_s[x], (NC - 1) * n + c)
                    for half in range(2):
                        mm = pe.matmul(o[:, C * half:C * half + C], blocks(x, 0, half, c), nhc(tt_s[x][:, :])[:, half, c, :],
                                       start=True, stop=True)
                    filled(k, mm)
                if name[0] == "O":
                    half = int(name[1])
                    if half == 0:
                        pe.wait_ge(s_exp[x][1], 128 * (4 * n + 4))
                        pe.wait_ge(s_exp[x][0], 128 * (3 * n + 3))
                        fill(("O", b))
                    o = bank[turns[("O", b)][0]]
                    for c in range(NC):
                        at = L * half + C * c
                        mm = pe.matmul(o[:, at:at + C], blocks(x, 1, half, c), vkp[x][:, half, c, 2 * C:W3], start=True, stop=(c == 0))
                        if c:
                            mm = pe.matmul(o[:, at:at + C], blocks(x, 0, half, c), qke[x][:, half, c, 0:C], start=False, stop=True)
                    if half == 1:
                        filled(("O", b), mm)
                if name == "ms":
                    k = (name, b)
                    o = fill(k)
                    pe.wait_ge(s_osq[x], n + 1)
                    filled(k, pe.matmul(o[:, :], blk, sq[x][:, :], start=True, stop=True))
                if name == "wo":
                    pe.wait_ge(s_on[x], n + 1)
                    if b == 0:
                        pe.wait_ge(s_ld_att, LD_ATT)
                    k = (name, b)
                    o = fill(k)
                    for tt in range(2):
                        for half in range(2):
                            at = L * half + P * tt
                            mm = pe.matmul(o[:, D * tt:D * tt + D], tmp_o[x][:, at:at + P], wo[:, half, :], start=(half == 0), stop=(half == 1))
                    filled(k, mm)

            def y_rows(th):
                for n in range(4):
                    bb, lt = divmod(n, 2)
                    k = ("yT", th, n)
                    o = fill(k)
                    pe.wait_ge(s_ys, GB * th + bb + 1)
                    for et in range(2):
                        at = GT_ * th + L * bb + P * lt
                        mm = pe.transpose(o[:, P * et:P * et + P], u[:, et, at:at + P], ident)
                    filled(k, mm)

            def x3_columns(th):
                for n in range(4):
                    k = ("x3T", th, n)
                    o = fill(k)
                    pe.wait_ge(s_x3, 4 * th + n + 1)
                    for kt in range(KT):
                        mm = pe.transpose(o[:, P * kt:P * kt + P], xres[:, 4 * th + n, P * kt:P * kt + P], ident)
                    filled(k, mm)

            def gates(th, part):
                if part == 0:
                    if th == 0:
                        pe.wait_ge(s_ld_small, 80)
                    pe.wait_ge(s_x3T, 4 * (th + 1))
                    k = ("score", th)
                    o = fill(k)
                    for tt in range(4):
                        for kt in range(KT):
                            mm = pe.matmul(o[:, NE * tt:NE * tt + NE], xT[:, kt, GT_ * th + P * tt:GT_ * th + P * tt + P],
                                           cent[:, kt, :], start=(kt == 0), stop=(kt == KT - 1))
                    filled(k, mm)
                if part == GATE_PARTS - 2:
                    k = ("gT", th)
                    o = fill(k)
                    pe.wait_ge(s_g96, th + 1)
                    for tt in range(4):
                        mm = pe.transpose(o[0:96, P * tt:P * tt + P], g96[:, tt, :], ident)
                    filled(k, mm)

            def experts(th):
                def hidden(ft):
                    k = ("h", th, ft)
                    o = fill(k)
                    if ft == 0:
                        pe.wait_ge(s_xlo, th + 1)
                    if (th, ft) == (0, 0):
                        pe.wait_ge(s_w1lo, KT)
                    for kt in range(KT):
                        w_hi, w_lo = (w[:, kt, P * ft:P * ft + P] for w in (w1_hi, w1_lo))
                        pe.matmul(o[:, :], w_hi, x_hl[th][:, 0, kt, :], start=(kt == 0), stop=False)
                        pe.matmul(o[:, :], w_hi, x_hl[th][:, 1, kt, :], start=False, stop=False)
                        mm = pe.matmul(o[:, :], w_lo, x_hl[th][:, 0, kt, :], start=False, stop=(kt == KT - 1))
                    filled(k, mm)
                    k = ("G", th, ft)
                    o = fill(k)
                    if ft == 0:
                        pe.wait_ge(s_gstk, th + 1)
                    filled(k, pe.matmul(o[:, :], sel[:, P * ft:P * ft + P], gstk[th], start=True, stop=True))

                def outputs(ft):
                    if th == 0:
                        pe.wait_ge(s_w2lo, sum(ft >= at for at, _ in w2_runs))
                    pe.wait_ge(s_hg, FT * th + ft + 1)
                    w_hi, w_lo = w2_hi(ft), w2_lo[:, ft, :]
                    for tt in range(4):
                        o = bank_y[tt // 2][:, D * (tt % 2):D * (tt % 2) + D]
                        h_hi, h_lo = (t[(FT * th + ft) % 2][:, P * tt:P * tt + P] for t in (hg_hi, hg_lo))
                        pe.matmul(o, h_hi, w_hi, start=(ft == 0 and tt % 2 == 0), stop=False, skip_group_check=True)
                        pe.matmul(o, h_hi, w_lo, start=False, stop=False, skip_group_check=True)
                        mm = pe.matmul(o, h_lo, w_hi, start=False, stop=False, skip_group_check=True)
                    mm.then_inc(s_hguse, 1)

                hidden(0)
                for ft in range(FT):
                    if ft + 1 < FT:
                        hidden(ft + 1)
                    if ft == 0:
                        pe.wait_ge(s_yfree, 2 * NG)
                        if th:
                            pe.wait_ge(s_yaccfree, 4 * th)
                    outputs(ft)
                    if th == 0 and ft in GATE_AT:
                        gates(1, GATE_AT.index(ft))
                for tt in range(4):
                    o = bank_y[tt // 2][:, D * (tt % 2):D * (tt % 2) + D]
                    pe.matmul(o, gT[th][0:NX, P * tt:P * tt + P], b2[:, :], start=False, stop=True,
                              skip_group_check=True).then_inc(s_yacc, 1)

            conv_input()
            for name, _, _ in ATTENTION[:PRELUDE]:
                step(name, 0)
            dt_rows()
            pe.wait_ge(s_stk, NG)
            pe.wait_ge(s_ld_att, LD_ATT)
            broadcast_b(0)
            for name, which in STEPS:
                if name == "pre":
                    if which + 1 < NITER:
                        broadcast_b(which + 1)
                elif name == "run":
                    broadcast_c(which)
                elif name == "yT":
                    y_rows(which)
                elif name == "x3T":
                    x3_columns(which)
                elif name not in ("gate", "y_out"):
                    step(name, which)
            y_rows(1)
            x3_columns(1)
            for part in range(GATE_PARTS):
                gates(0, part)
            for th in range(NG):
                experts(th)

        @block.scalar
        def _(act):
            chain = [0]

            def link(ins):
                chain[0] += 1
                ins.then_inc(s_act, 1)
                act.wait_ge(s_act, chain[0])

            def take(key):
                b_, n = turns[key]
                act.wait_ge(s_full[b_], n + 1)
                return bank[b_]

            def free(key):
                act.nop().then_inc(s_free[turns[key][0]], 1)

            def prelude():
                for et in range(2):
                    for th in range(NG):
                        k = ("xe", et, th)
                        o = take(k)
                        link(act.activation(xpad[:, et, GB * th:GB * th + GB, DC - 1:LP],
                                            o[:, :].rearrange("p (b l) -> p b l", b=GB), ACT.Copy))
                        free(k)
                        act.nop().then_inc(s_xpad, 1)
                for et in range(2):
                    act.wait_ge(s_conv, et + 1)
                    act.activation(u[:, et, :], u[:, et, :], ACT.Silu).then_inc(s_u, 1)
                for name, _, _ in ATTENTION[:PRELUDE]:
                    step(name, 0)
                link(act.activation(negA[:, :, :], alog[:, :, :], ACT.Exp))
                link(act.activation(negA[:, :, :], negA[:, :, :], ACT.Copy, scale=-1.0))
                for th in range(NG):
                    o = take(("xdbl", th))
                    act.activation(dtlo[96:96 + DR, GT_ * th:GT_ * th + GT_], o[96:96 + DR, :], ACT.Copy).then_inc(s_dtlo, 1)
                for et in range(2):
                    if et:
                        act.wait_ge(s_spf, et)
                    for th in range(NG):
                        k = ("dt", et, th)
                        o = take(k)
                        c_ = slice(GT_ * th, GT_ * th + GT_)
                        act.activation(delta[:, et, c_], o[:, :], ACT.Identity, bias=dtb[:, et:et + 1])
                        link(act.activation(sp_l[:, c_], o[:, :], ACT.Abs, bias=dtb[:, et:et + 1]))
                        free(k)
                    if et == 0:
                        take(("dt", 1, 0))
                        take(("dt", 1, 1))
                    link(act.activation(sp_z, sp_l, ACT.Exp, scale=-1.0))
                    link(act.activation(sp_w, sp_z, ACT.Identity, bias=bias_col(BI_ONE)))
                    act.activation(sp_l, sp_w, ACT.Ln).then_inc(s_sp, 1)

            def copy_b(i):
                act.wait_ge(s_bb, i + 1)
                if i >= 2:
                    act.wait_ge(s_dbu, i - 1)
                act.activation(bsb[:, i % 2, :], bank_b[:, :], ACT.Copy).then_inc(s_bcopy, 1)

            def decays(i):
                th, n = divmod(i, DS)
                if i >= 2:
                    act.wait_ge(s_scan, i - 1)
                for et in range(2):
                    o = dA[:, i % 2, GT_ * et:GT_ * et + GT_].rearrange("p (b l) -> p b l", b=GB)[:, :, 1:L]
                    src = delta[:, et, GT_ * th:GT_ * th + GT_].rearrange("p (b l) -> p b l", b=GB)[:, :, 1:L]
                    act.activation(o, src, ACT.Exp, scale=negA[:, et, n:n + 1]).then_inc(s_dA, 1)

            def step(name, b):
                x, n = b % 2, b // 2
                k = (name, b)
                if name == "v":
                    if n:
                        act.wait_ge(s_on[x], n)
                    link(act.activation(v_w[x][:, :], take(k)[:, :], ACT.Silu))
                    free(k)
                    act.nop().then_inc(s_v[x], 1)
                if name == "b":
                    link(act.activation(beta_kc[x][:, :], take(k)[:, :], ACT.Sigmoid))
                    free(k)
                    act.nop().then_inc(s_beta[x], 1)
                    nc.scalar.preload_act_table_set(LN_EXP)
                if name in ("k", "q"):
                    o = take(k)
                    if name == "q":
                        act.wait_ge(s_clamp[x], 2 * n + 1)
                    act.activation(sq[x][:, :], o[:, :], ACT.Square).then_inc(s_sq[x], 1)
                if name in ("ssk", "ssq"):
                    act.wait_ge(s_clamp[x], 2 * n + 1 + (name == "ssq"))
                    r = tmp_o[x][:, :]
                    link(act.activation(r, r, ACT.Ln, scale=float(2 ** SCALE_LOG2)))
                    act.activation(r, r, ACT.Exp, scale=-0.5,
                                   bias=bias_col(BI_Q if name == "ssq" else BI_K)).then_inc(s_rs[x], 1)
                if name[0] == "P":
                    w = int(name[1])
                    half, ch = divmod(w, 2)
                    o = take(k)[:, 0:CH * W3].rearrange("p (c n) -> p c n", c=CH)[:, :, 2 * C:W3]
                    act.wait_ge(s_at[x], 4 * n + w + 1)
                    if w == 0:
                        act.wait_ge(s_bdram[x], 16 * (n + 1))
                    cs = slice(CH * ch, CH * ch + CH)
                    act.activation(vkp[x][:, half, cs, C:2 * C], o, ACT.Copy)
                    link(act.activation(nhc(beta_kc[x][:, :])[:, half, cs, :], o, ACT.Copy))
                    free(k)
                    act.nop().then_inc(s_kc[x], 1)
                if name == "turn_t":
                    act.wait_ge(s_tcp[x], 128 * (n + 1))
                    act.activation(nhc(tt_s[x][:, :]), hcn(at_g[x][:, :]), ACT.Copy).then_inc(s_tperm[x], 1)
                if name[:2] == "UW":
                    half = int(name[2])
                    o = take(k)[:, :].rearrange("p (c n) -> p c n", c=NC)[:, :, 0:C]
                    act.wait_ge(s_w[x], 2 * n + half + 1)
                    link(act.activation(nhc(k_uv[x][:, :])[:, half, :, :], o, ACT.Copy))
                    free(k)
                    act.nop().then_inc(s_uv[x], 1)
                if name == "H":
                    link(act.activation(hh[x][:, :], take(k)[:, :], ACT.Copy))
                    free(k)
                    act.wait_ge(s_exp[x][1], 128 * (4 * n + 2))
                    act.activation(nhc(tt_s[x][:, :])[:, :, 1, :], hcn(hh[x][:, :])[:, :, 0, :], ACT.Copy).then_inc(s_s[x], 1)
                if name == "O1":
                    k = ("O", b)
                    o = take(k)
                    link(act.activation(tmp_o[x][:, :], o[:, :], ACT.Copy))
                    free(k)
                    act.activation(sq[x][:, :], tmp_o[x][:, :], ACT.Square).then_inc(s_osq[x], 1)
                if name == "ms":
                    r = v_w[x][:, :]
                    link(act.activation(r, take(k)[:, :], ACT.Ln, scale=1.0 / DH, bias=bias_col(BI_EPS)))
                    free(k)
                    act.activation(r, r, ACT.Exp, scale=-0.5).then_inc(s_or[x], 1)
                if name == "ln":
                    rstd()

            norms = [0]

            def rstd():
                norms[0] += 1
                act.wait_ge(s_var, norms[0])
                link(act.activation(ln_r[:, :], ln_mv[:, :, 1], ACT.Ln, bias=bias_col(BI_EPS)))
                act.activation(ln_r[:, :], ln_r[:, :], ACT.Exp, scale=-0.5).then_inc(s_rstd, 1)

            def gate(th):
                act.wait_ge(s_yfree, 2 * (th + 1))
                for bb in range(GB):
                    b = GB * th + bb
                    act.wait_ge(s_x2[b], 2)
                    act.activation(delta[:, :, L * b:L * b + L], xres[:, 2 * b:2 * b + 2, :], ACT.Silu).then_inc(s_z, 1)
                nc.scalar.preload_act_table_set(LN_EXP)

            def x3_columns(th):
                for n in range(4):
                    k = ("x3T", th, n)
                    o = take(k)[:, 0:D].rearrange("p (k t) -> p k t", k=KT)
                    at = GT_ * th + P * n
                    link(act.activation(xT[:, :, at:at + P], o, ACT.Copy))
                    free(k)
                    act.nop().then_inc(s_x3T, 1)

            def split_x3(th):
                if th == 0:
                    act.wait_ge(s_ys, B)
                act.activation(x_hl[th][:, 0, :, :], xT[:, :, GT_ * th:GT_ * th + GT_], ACT.Copy).then_inc(s_xhi, 1)

            def gates(th, part):
                if part == 0:
                    if th == 0:
                        act.wait_ge(s_ld_small, 80)
                    k = ("score", th)
                    o = take(k)
                    link(act.activation(sig[:, :, :], o[:, 0:4 * NE].rearrange("p (t e) -> p t e", t=4), ACT.Sigmoid))
                    free(k)
                    act.nop().then_inc(s_sige, 1)
                    nc.scalar.preload_act_table_set(LN_EXP)
                if part == GATE_PARTS - 2:
                    act.activation(gT[th], take(("gT", th))[0:32, :], ACT.Copy).then_inc(s_gT, 1)

            def experts(th):
                for ft in range(FT):
                    k = ("h", th, ft)
                    i = FT * th + ft
                    o = take(k)
                    if i >= 2:
                        act.wait_ge(s_hg, i - 1)
                    link(act.activation(hrel[:, i % 2, :], o[:, :], ACT.Relu, bias=b1[:, ft:ft + 1]))
                    free(k)
                    act.nop().then_inc(s_rel, 1)
                    if th == 0 and ft in GATE_AT:
                        gates(1, GATE_AT.index(ft))
                    if th and ft == LAST_NORM_AT:
                        rstd()
                if th:
                    rstd()

            prelude()
            act.wait_ge(s_delta, 2)
            act.wait_ge(s_dA0, 2)
            copy_b(0)
            decays(0)
            for name, which in STEPS:
                if name == "pre":
                    if which + 1 < NITER:
                        copy_b(which + 1)
                        decays(which + 1)
                elif name == "gate":
                    gate(which)
                elif name == "yT":
                    rstd()
                elif name == "x3T":
                    x3_columns(which)
                elif name not in ("run", "y_out"):
                    step(name, which)
            gate(1)
            split_x3(0)
            rstd()
            x3_columns(1)
            split_x3(1)
            for part in range(GATE_PARTS):
                gates(0, part)
            for th in range(NG):
                experts(th)

        @block.vector
        def _(dve):
            chain = [0]

            def link(ins):
                chain[0] += 1
                ins.then_inc(s_dve, 1)
                dve.wait_ge(s_dve, chain[0])

            def take(key):
                b_, n = turns[key]
                dve.wait_ge(s_full[b_], n + 1)
                return bank[b_]

            def free(key):
                dve.nop().then_inc(s_free[turns[key][0]], 1)

            norms = [0]

            def layer_norm(first, tiles, done):
                for tt in range(tiles):
                    dve.bn_stats(ln_st[:, tt, :], xres[:, first + tt, :]).then_inc(s_dve, 1)
                chain[0] += tiles
                dve.wait_ge(s_dve, chain[0])
                if norms[0]:
                    dve.wait_ge(s_rstd, norms[0])
                else:
                    link(dve.memset(ln_mv[:, :, :], 1.0))
                for tt in range(tiles):
                    dve.bn_aggr(ln_mv[:, tt, :], ln_st[:, tt, :]).then_inc(s_dve, 1)
                chain[0] += tiles
                dve.wait_ge(s_dve, chain[0])
                norms[0] += 1
                dve.nop().then_inc(s_var, 1)
                dve.wait_ge(s_rstd, norms[0])
                for tt in range(tiles):
                    dve.tensor_scalar(xres[:, first + tt, :], xres[:, first + tt, :], ln_mv[:, tt, 0:1],
                                      ln_r[:, tt:tt + 1], ALU.subtract, ALU.mult).then_inc(done, 1)
                return done

            def prelude():
                dve.wait_ge(s_ld_ssm, LD_SSM)
                dve.wait_ge(s_pad, 1)
                for et in range(2):
                    dve.wait_ge(s_xpad, 2 * et + 2)
                    v = u[:, et, :].rearrange("p (b l) -> p b l", b=B)
                    link(dve.tensor_scalar(v, xpad[:, et, :, 0:L], convw[:, et, 0:1], convb[:, et:et + 1], ALU.mult, ALU.add))
                    for k in range(1, DC):
                        ins = dve.scalar_tensor_tensor(out=v, in0=xpad[:, et, :, k:k + L], scalar=convw[:, et, k:k + 1],
                                                       in1=v, op0=ALU.mult, op1=ALU.add)
                        if k < DC - 1:
                            link(ins)
                    ins.then_inc(s_conv, 1)
                    if et == 0:
                        dve.wait_ge(s_ld_c, LD_C)
                        for kt in range(KT):
                            ins = dve.tensor_copy(wb16[:, kt, :].rearrange("p (h r) -> p h r", h=H),
                                                  wqkvb[:, kt, 3 * D:3 * D + H].unsqueeze(2).broadcast_to([P, H, DH]))
                            if kt < KT - 1:
                                link(ins)
                        link(ins)
                        dve.nop().then_inc(s_wb, 1)
                for x in range(2):
                    dve.tensor_copy(qke[x][:, :, :, 2 * C:W3].rearrange("p h c n -> p (h c) n"),
                                    eye16.unsqueeze(1).broadcast_to([P, 2 * NC, C])).then_inc(s_eye, 1)
                for name, _, _ in ATTENTION[:PRELUDE]:
                    step(name, 0)
                dve.wait_ge(s_u, 2)
                hi, r1, mid16 = gm16, gr1, gstk[0]
                for th in range(NG):
                    k = ("xdbl", th)
                    o = take(k)
                    c_ = slice(GT_ * th, GT_ * th + GT_)
                    dve.wait_ge(s_dtlo, th + 1)
                    link(dve.tensor_copy(hi, o[0:96, :]))
                    link(dve.tensor_tensor(r1, o[0:96, :], hi, ALU.subtract))
                    free(k)
                    dve.tensor_copy(stk[0:32, c_], hi[0:32, :])
                    link(dve.tensor_copy(mid16, r1))
                    dve.tensor_copy(stk[32:64, c_], mid16[32:64, :])
                    link(dve.tensor_tensor(r1[64:96, :], r1[64:96, :], mid16[64:96, :], ALU.subtract))
                    link(dve.tensor_copy(stk[64:96, c_], r1[64:96, :]))
                    dve.nop().then_inc(s_stk, 1)
                for et in range(2):
                    dve.wait_ge(s_sp, et + 1)
                    link(dve.scalar_tensor_tensor(out=sp_w, in0=sp_w, scalar=1.0, in1=sp_z, op0=ALU.subtract, op1=ALU.subtract))
                    link(dve.tensor_tensor(sp_l, sp_l, sp_w, ALU.subtract))
                    link(dve.scalar_tensor_tensor(out=delta[:, et, :], in0=delta[:, et, :], scalar=0.0, in1=sp_l,
                                                  op0=ALU.max, op1=ALU.add))
                    dve.nop().then_inc(s_spf, 1)
                    dve.nop().then_inc(s_delta, 1)
                    dve.tensor_tensor(du[:, et, :], delta[:, et, :], u[:, et, :], ALU.mult).then_inc(s_du, 1)
                for k in range(2):
                    v = dA[:, k, :].rearrange("p (n l) -> p n l", l=L)[:, :, 0:1]
                    dve.memset(v, 0.0).then_inc(s_dA0, 1)
                dve.wait_ge(s_dA0, 2)

            def scan(i):
                dve.wait_ge(s_dA, 2 * (i + 1))
                dve.wait_ge(s_dbu, i + 1)
                link(dve.tensor_tensor_scan(hst, dA[:, i % 2, :], dBu[:, i % 2, :], 0.0, ALU.mult, ALU.add))
                dve.nop().then_inc(s_scan, 1)

            def add_states(i):
                n = i % DS
                dve.wait_ge(s_cc, i + 1)
                h_c = hC[:, :].rearrange("p (e t) -> p e t", e=2)
                link(dve.tensor_tensor(h_c, hst.rearrange("p (e t) -> p e t", e=2),
                                       bank_c[:, :].unsqueeze(1).broadcast_to([P, 2, GT_]), ALU.mult))
                dve.nop().then_inc(s_hc, 1)
                for et in range(2):
                    if n == 0:
                        ins = dve.tensor_copy(bank_y[et][:, :], h_c[:, et, :])
                    else:
                        ins = dve.tensor_tensor(bank_y[et][:, :], bank_y[et][:, :], h_c[:, et, :], ALU.add)
                    if et == 0:
                        ins.then_inc(s_dve, 1)
                        chain[0] += 1
                    else:
                        link(ins)

            def y_out(th):
                if th == 0:
                    dve.wait_ge(s_ld_small, 80)
                c_ = slice(GT_ * th, GT_ * th + GT_)
                for et in range(2):
                    dve.scalar_tensor_tensor(out=u[:, et, c_], in0=u[:, et, c_], scalar=dskip[:, et:et + 1],
                                             in1=bank_y[et][:, :], op0=ALU.mult, op1=ALU.add).then_inc(s_yfree, 1)

            def solve(b, rows):
                x, n = b % 2, b // 2
                a_t = at_g[x][:, :].rearrange("p (s c t) -> p s c t", s=C, c=CLO)
                t_t = tt_s[x][:, :].rearrange("p (j c t) -> p j c t", j=C, c=CLO)
                for t in rows:
                    if t == 0:
                        if n:
                            dve.wait_ge(s_exp[x][0], 128 * 3 * n)
                        link(dve.memset(tt_s[x][:, :], 0.0))
                        for c in range(CLO):
                            ins = dve.memset(tt_s[x][:, C * c:C * c + (CLO * C + 1) * (C - 1) + 1:CLO * C + 1], 1.0)
                            if c < CLO - 1:
                                link(ins)
                        link(ins)
                        dve.wait_ge(s_ain[x], 128 * (n + 1))
                        continue
                    prod = tmp_o[x][:, 0:CLO * t * t].rearrange("p (c j s) -> p c j s", c=CLO, j=t)
                    a = a_t[:, 0:t, :, t].rearrange("p s c -> p c s").unsqueeze(2).broadcast_to([P, CLO, t, t])
                    link(dve.tensor_tensor(prod, a, t_t[:, 0:t, :, 0:t].rearrange("p j c s -> p c j s"), ALU.mult))
                    link(dve.tensor_reduce(t_t[:, 0:t, :, t].rearrange("p j c -> p c j"), prod, AX_X, ALU.add, negate=True))
                    if t == C - 1:
                        dve.wait_ge(s_binst[x], 16 * (n + 1))
                        bt = binst[x][:, :].rearrange("p (c j) -> p j c", c=CLO).unsqueeze(3).broadcast_to([P, C, CLO, C])
                        link(dve.tensor_tensor(t_t, t_t, bt, ALU.mult))
                        dve.nop().then_inc(s_tt[x], 1)

            def step(name, b):
                x, n = b % 2, b // 2
                k = (name, b)
                if name == "v":
                    dve.wait_ge(s_v[x], n + 1)
                    dve.transpose(vkp[x][:, :, :, 0:C].rearrange("p h c n -> p c h n"),
                                  v_w[x][:, :].rearrange("p (c h n) -> p c h n", c=NC, h=2)).then_inc(s_vc[x], 1)
                if name in ("ssk", "ssq"):
                    w = 2 * n + (name == "ssq")
                    o = take(k)
                    r = tmp_o[x][:, :]
                    link(dve.tensor_scalar(r, o[:, :], 1e-24, None, ALU.max))
                    free(k)
                    dve.nop().then_inc(s_clamp[x], 1)
                    dve.wait_ge(s_rs[x], w + 1)
                    k = (name[2], b)
                    o = take(k)
                    if name == "ssq":
                        link(dve.tensor_tensor(qke[x][:, :, :, 0:C], hcn(o[:, :]), hcn(r), ALU.mult))
                        free(k)
                        dve.nop().then_inc(s_qk[x], 1)
                    else:
                        link(dve.tensor_tensor(nhc(k_uv[x][:, :]), hcn(o[:, :]), hcn(r), ALU.mult))
                        free(k)
                        dve.nop().then_inc(s_k[x], 1)
                        dve.wait_ge(s_beta[x], n + 1)
                        dve.wait_ge(s_eye, 2)
                        link(dve.tensor_tensor(qke[x][:, :, :, C:2 * C], nhc(k_uv[x][:, :]), hcn(beta_kc[x][:, :]), ALU.mult))
                if name[0] == "P":
                    half, ch = divmod(int(name[1]), 2)
                    o = take(k)[:, 0:CH * W3].rearrange("p (c n) -> p c n", c=CH)
                    cs = slice(CH * ch, CH * ch + CH)
                    dve.tensor_tensor(vkp[x][:, half, cs, 2 * C:W3], o[:, :, 0:C],
                                      mask_p.unsqueeze(1).broadcast_to([P, CH, C]), ALU.mult).then_inc(s_dve, 1)
                    chain[0] += 1
                    dve.tensor_tensor(hcn(at_g[x][:, :])[:, half, cs, :], o[:, :, C:2 * C],
                                      mask_a.unsqueeze(1).broadcast_to([P, CH, C]), ALU.mult).then_inc(s_at[x], 1)
                if name[:5] == "solve":
                    solve(b, [range(0, 8), range(8, 12), range(12, 16)][int(name[5])])
                if name[:2] == "UW":
                    half = int(name[2])
                    o = take(k)[:, :].rearrange("p (c n) -> p c n", c=NC)[:, :, C:2 * C]
                    dve.tensor_copy(nhc(v_w[x][:, :])[:, half, :, :], o).then_inc(s_w[x], 1)
                if name[:2] == "GQ":
                    half = int(name[2])
                    o = take(k)[:, :].rearrange("p (c n) -> p c n", c=NC)
                    dve.tensor_tensor(nhc(at_g[x][:, :])[:, half, :, :], eye16.unsqueeze(1).broadcast_to([P, NC, C]),
                                      o[:, :, 0:C], ALU.subtract).then_inc(s_gq[x], 1)
                    link(dve.tensor_tensor(qke[x][:, half, :, 0:C], qke[x][:, half, :, 0:C], o[:, :, C:2 * C], ALU.subtract))
                    free(k)
                    dve.nop().then_inc(s_gq[x], 1)
                if name[0] == "S":
                    c = int(name[1:])
                    o = take(k)[:, 0:2 * C].rearrange("p (h n) -> p h n", h=2)
                    if c == 1:
                        dve.wait_ge(s_s[x], (NC - 1) * n + 1)
                    link(dve.tensor_tensor(nhc(tt_s[x][:, :])[:, :, c + 1, :], o, hcn(hh[x][:, :])[:, :, c, :], ALU.add))
                    free(k)
                    dve.nop().then_inc(s_s[x], 1)
                if name == "ms":
                    dve.wait_ge(s_or[x], n + 1)
                    if b == 0:
                        dve.wait_ge(s_ld_small, 80)
                        dve.wait_ge(s_ld_att, LD_ATT)
                    v = tmp_o[x][:, :]
                    dve.scalar_tensor_tensor(out=v, in0=v, scalar=onorm[:, 0:1], in1=v_w[x][:, :],
                                             op0=ALU.mult, op1=ALU.mult).then_inc(s_on[x], 1)
                if name == "ln":
                    k = ("wo", b)
                    xr = xres[:, 2 * b:2 * b + 2, :]
                    link(dve.tensor_tensor(xr, xr, take(k)[:, :].rearrange("p (t d) -> p t d", t=2), ALU.add))
                    free(k)
                    layer_norm(2 * b, 2, s_x2[b])

            def gate(th):
                dve.wait_ge(s_yfree, 2 * (th + 1))
                for bb in range(GB):
                    b = GB * th + bb
                    dve.wait_ge(s_x2[b], 2)
                    dve.wait_ge(s_z, b + 1)
                    yv = u[:, :, L * b:L * b + L]
                    dve.tensor_tensor(yv, yv, delta[:, :, L * b:L * b + L], ALU.mult).then_inc(s_ys, 1)

            def y_rows(th):
                for n in range(4):
                    k = ("yT", th, n)
                    link(dve.tensor_tensor(xres[:, 4 * th + n, :], xres[:, 4 * th + n, :], take(k)[:, 0:D], ALU.add))
                    free(k)
                layer_norm(4 * th, 4, s_x3)

            def split_x3(th):
                dve.wait_ge(s_xhi, th + 1)
                dve.tensor_tensor(x_hl[th][:, 1, :, :], xT[:, :, GT_ * th:GT_ * th + GT_], x_hl[th][:, 0, :, :],
                                  ALU.subtract).then_inc(s_xlo, 1)

            def gates(th, part):
                ge = rk0.rearrange("p (t e j) -> p t e j", t=4, e=NE)
                gt = rk1.rearrange("p (t e j) -> p t e j", t=4, e=NE)
                s_j = sc[:, :, :].unsqueeze(2).broadcast_to([P, 4, NE, NE])
                s_e = sc[:, :, :].unsqueeze(3).broadcast_to([P, 4, NE, NE])
                lm = lmask[:, :].unsqueeze(1).broadcast_to([P, 4, NE * NE])
                if part == 0:
                    dve.wait_ge(s_sige, th + 1)
                    link(dve.tensor_tensor(sc[:, :, :], sig[:, :, :], ebias[:, :].unsqueeze(1).broadcast_to([P, 4, NE]), ALU.add))
                    link(dve.tensor_tensor(gt, s_j, s_e, ALU.is_gt))
                if part == 1:
                    link(dve.tensor_tensor(ge, s_j, s_e, ALU.is_ge))
                if part == 2:
                    if th == 0:
                        dve.wait_ge(s_ld_w2, LD_W2)
                    link(dve.tensor_tensor(rk0.rearrange("p (t n) -> p t n", t=4), rk0.rearrange("p (t n) -> p t n", t=4), lm, ALU.mult))
                if part == 3:
                    link(dve.tensor_tensor(rk0, rk0, rk1, ALU.max))
                if part == 4:
                    link(dve.tensor_reduce(rank[:, :, :], ge, AX_X, ALU.add))
                if part == 5:
                    link(dve.scalar_tensor_tensor(out=sc[:, :, :], in0=rank[:, :, :], scalar=float(KR) - 0.5, in1=sc[:, :, :],
                                                  op0=ALU.is_lt, op1=ALU.mult))
                    link(dve.tensor_reduce(gsum[:, :], sc[:, :, :], AX_X, ALU.add))
                    link(dve.tensor_scalar(gsum[:, :], gsum[:, :], 1e-8, None, ALU.max))
                    link(dve.reciprocal(gsum[:, :], gsum[:, :]))
                    if th == 0:
                        link(dve.memset(g96[:, :, :], 0.0))
                    for r in range(3):
                        dve.memset(g96[:, :, 32 * r:32 * r + NSH], 1.0)
                        link(dve.tensor_tensor(g96[:, :, 32 * r + NSH:32 * r + NX], sc[:, :, :],
                                               gsum[:, :].unsqueeze(2).broadcast_to([P, 4, NE]), ALU.mult))
                    dve.nop().then_inc(s_g96, 1)
                k = ("gT", th)
                stack = gstk[th]
                if part == 6:
                    o = take(k)
                    hi = gm16
                    dve.wait_ge(s_gT, th + 1)
                    link(dve.tensor_copy(hi, o[0:96, :]))
                    link(dve.tensor_copy(stack[0:32, :], hi[0:32, :]))
                    link(dve.tensor_tensor(gr1, o[0:96, :], hi, ALU.subtract))
                    free(k)
                if part == 7:
                    mid16 = gm16
                    link(dve.tensor_copy(mid16, gr1))
                    link(dve.tensor_copy(stack[32:64, :], mid16[32:64, :]))
                    link(dve.tensor_tensor(gr1[64:96, :], gr1[64:96, :], mid16[64:96, :], ALU.subtract))
                    link(dve.tensor_copy(stack[64:96, :], gr1[64:96, :]))
                    dve.nop().then_inc(s_gstk, 1)

            def experts(th):
                for ft in range(FT):
                    i = FT * th + ft
                    k = ("G", th, ft)
                    o = take(k)
                    dve.wait_ge(s_rel, i + 1)
                    h = hrel[:, i % 2, :]
                    link(dve.tensor_tensor(h, h, o[:, :], ALU.mult))
                    free(k)
                    if i >= 2:
                        dve.wait_ge(s_hguse, i - 1)
                    link(dve.tensor_copy(hg_hi[i % 2][:, :], h))
                    link(dve.tensor_tensor(hg_lo[i % 2][:, :], h, hg_hi[i % 2][:, :], ALU.subtract))
                    dve.nop().then_inc(s_hg, 1)
                    if th == 0 and ft in GATE_AT:
                        gates(1, GATE_AT.index(ft))
                    if th and ft == LAST_NORM_AT:
                        layer_norm(0, 4, s_last)
                for tt in range(4):
                    dve.wait_ge(s_yacc, 4 * th + 2 * (tt // 2) + 2)
                    o = bank_y[tt // 2][:, D * (tt % 2):D * (tt % 2) + D]
                    link(dve.scalar_tensor_tensor(out=xres[:, 4 * th + tt, :], in0=xres[:, 4 * th + tt, :], scalar=2.0,
                                                  in1=o, op0=ALU.mult, op1=ALU.add))
                    dve.nop().then_inc(s_yaccfree, 1)
                if th:
                    layer_norm(4, 4, s_last)

            prelude()
            for name, which in STEPS:
                if name == "run":
                    scan(which)
                    add_states(which)
                elif name == "y_out":
                    y_out(which)
                elif name == "gate":
                    gate(which)
                elif name == "yT":
                    y_rows(which)
                elif name not in ("pre", "x3T"):
                    step(name, which)
            gate(1)
            split_x3(0)
            y_rows(1)
            split_x3(1)
            for part in range(GATE_PARTS):
                gates(0, part)
            for th in range(NG):
                experts(th)


_OUTS = [((4, 256, 256), "float32")]


def kernel(**inputs):
    import numpy as np
    import ml_dtypes
    import concourse.bacc as bacc
    from concourse.bass_utils import run_bass_kernel_spmd

    v = {k: np.asarray(a) for k, a in inputs.items()}
    wide = np.zeros((D, 104), np.float32)
    xp = v["L0_xattn_x_proj_w"]
    for r in range(3):
        wide[:, 32 * r:32 * r + 2 * DS] = xp[DR:].T
    wide[:, 96:96 + DR] = xp[:DR].T

    def side_by_side(shared, routed):
        return np.concatenate([shared, routed], axis=0)

    wv = v["L0_attn_Wv"].reshape(D, 2, HH // 2, 2, DH).transpose(0, 3, 2, 1, 4).reshape(D, D)
    w1 = np.zeros((D, FP), np.float32)
    w1[:, :NX * DFF] = side_by_side(v["L0_ffn_shared_w1"], v["L0_ffn_routed_w1"]).transpose(1, 0, 2).reshape(D, NX * DFF)
    b1 = np.zeros((FP,), np.float32)
    b1[:NX * DFF] = side_by_side(v["L0_ffn_shared_b1"], v["L0_ffn_routed_b1"]).reshape(-1)
    w2 = np.zeros((FP, D), np.float32)
    w2[:NX * DFF] = side_by_side(v["L0_ffn_shared_w2"], v["L0_ffn_routed_w2"]).reshape(NX * DFF, D)
    b2 = side_by_side(v["L0_ffn_shared_b2"], v["L0_ffn_routed_b2"])

    const = np.zeros((P, C_ALL), np.float32)
    row, col = np.arange(P)[:, None], np.arange(P)[None, :]
    c16 = np.arange(C)[None, :]
    const[:, C_ID:C_ID + P] = row == col
    const[:, C_BLK:C_BLK + P] = row // DH == col // DH
    const[:, C_E:C_E + C] = row % C == c16
    const[:, C_MA:C_MA + C] = c16 > row % C
    const[:, C_MP:C_MP + C] = c16 >= row % C
    const[:, C_BIAS + BI_ONE] = 1.0
    const[:, C_BIAS + BI_EPS] = EPS
    const[:, C_BIAS + BI_K] = 0.5 * SCALE_LOG2 * LN2
    const[:, C_BIAS + BI_Q] = 0.5 * SCALE_LOG2 * LN2 - 2 * LN2
    lmask = np.tile((np.arange(NE)[None, :] < np.arange(NE)[:, None]).reshape(1, -1), (P, 1)).astype(np.float32)
    eye3 = (np.arange(96)[:, None] % 32 == np.arange(2 * DS)[None, :]).astype(ml_dtypes.bfloat16)
    sel = (np.arange(96)[:, None] % 32 == np.arange(FP)[None, :] // DFF).astype(ml_dtypes.bfloat16)

    arrays = {
        "x_tok": v["x"].reshape(T, D),
        "x_t": v["x"].reshape(T, D).T,
        "ctx_t": v["ctx_1024"].reshape(T, DM).T,
        "wqkvb": np.concatenate([v["L0_attn_Wq"], v["L0_attn_Wk"], wv, v["L0_attn_Wb"]], axis=1),
        "onorm": np.tile(v["L0_attn_o_norm_weight"], HH).reshape(P, 1),
        "wo": v["L0_attn_Wo"],
        "inproj": v["L0_xattn_in_proj_w"].T,
        "convw": v["L0_xattn_conv_w"],
        "convb": v["L0_xattn_conv_b"].reshape(2, P).T,
        "xproj": wide,
        "dtproj": v["L0_xattn_dt_proj_w"].T,
        "dtb": v["L0_xattn_dt_proj_b"].reshape(2, P).T,
        "alog": v["L0_xattn_A_log"],
        "dskip": v["L0_xattn_D"].reshape(2, P).T,
        "w1": w1,
        "b1": b1.reshape(FT, P).T,
        "w2": w2,
        "b2": b2,
        "cent": v["L0_ffn_centroids"].T,
        "ebias": v["L0_ffn_bias"],
        "const": const,
        "eye3": eye3,
        "sel": sel,
        "lmask": lmask,
    }
    arrays = {f"in_{k}": np.ascontiguousarray(a) for k, a in arrays.items()}
    nc = bacc.Bacc("TRN2", target_bir_lowering=False, num_devices=1)
    args = [nc.dram_tensor(k, a.shape, mybir.dt.from_np(a.dtype), kind="ExternalInput").ap() for k, a in arrays.items()]
    out = nc.dram_tensor("out_0", (T, D), F32, kind="ExternalOutput").ap()
    decoder_layer(nc, *args, out)
    r = run_bass_kernel_spmd(nc, [arrays], core_ids=[0])
    return r.results[0]["out_0"].reshape(B, L, D)
```

```python
from contextlib import ExitStack

import concourse.bass as bass
from concourse import mybir

F32 = mybir.dt.float32
BF16 = mybir.dt.bfloat16
F32R = mybir.dt.float32r
ALU = mybir.AluOpType
ACT = mybir.ActivationFunctionType
AX_X = mybir.AxisListType.X

P = 128
B, L, D = 4, 256, 256
T = B * L
KT = D // P
H, DH = 16, 16
HH = P // DH
C = 16
NC = L // C
W3 = 3 * C
CH = NC // 2
CLO = 2
BL = 2 * L
GB = 2
GT_ = GB * L
NG = B // GB
DM, DS, DC, DR = 128, 16, 4, 8
DI = 2 * DM
LP = L + DC - 1
NE, NSH, KR, DFF = 16, 2, 4, 176
NX = NE + NSH
FT = -(-NX * DFF // P)
FP = FT * P
EPS = 1e-5
LN2 = 0.6931471805599453
SCALE_LOG2 = 20
LN_EXP = "natural_log_exp_and_others"

C_ID, C_BLK, C_E, C_MA, C_MP, C_BIAS = 0, 128, 256, 272, 288, 304
BI_ONE, BI_EPS, BI_K, BI_Q = range(4)
C_ALL = C_BIAS + 4

NREC = NC - 2
ATTENTION = [("k", 2.7, 0), ("v", 1.2, 1.5), ("b", 1.7, 0.5), ("ssk", 0.9, 0), ("q", 1.7, 1), ("ssq", 0.4, 2),
             ("move_k", 0, 4),
             ("P0", 1.7, 0), ("P1", 1.7, 0), ("P2", 1.7, 1), ("P3", 1.7, 3), ("move_a", 0, 4),
             ("solve0", 0, 4), ("solve1", 0, 1), ("solve2", 0, 4), ("move_t", 0, 8), ("turn_t", 0, 2), ("expand_t", 0, 6),
             ("UW0", 3.4, 4), ("UW1", 3.4, 1), ("expand_w", 0, 0.5), ("H", 8.8, 4.5),
             ("GQ0", 3.4, 1), ("GQ1", 2.9, 2), ("expand_gu", 1.5, 7)]
ATTENTION += [(f"S{c}", 1, 1) for c in range(1, NREC + 1)]
ATTENTION += [("expand_s", 0, 12.5), ("O0", 3.4, 0), ("O1", 3.4, 0.5), ("ms", 0.9, 3.5), ("wo", 1.7, 0), ("ln", 0, 3), ("lnorm", 0, 1)]
PU_FROM = 4


def pu_chunks(c):
    steps = NREC + 1 - PU_FROM
    return range((c - PU_FROM) * NC // steps, (c + 1 - PU_FROM) * NC // steps)


NITER = NG * DS
MID = 2
GATE_PARTS = 8
SSM_START = [("stack", 0, 3.5), ("dt0", 0.9, 8), ("dt1", 0.9, 12), ("begin", 0.5, 0.5)]
MIDDLE = [("gate", 0, 4), ("yT", 2, 3), ("ynorm", 0, 1), ("x3T", 2, 2)] + [(f"gates{i}", .2, 2) for i in range(GATE_PARTS)] + [("split", 0, 0)]
NEEDS = {"gate": {("lnorm", 0), ("lnorm", 1), ("y_out", 0)}, "gates0": {("y_out", NG - 1)}}
SIDE = dict(zip([1, 3, 4, 6, 8, 10, 11, 12, 13, 14, 15, 17, 18],
                ["gate", "yT", "ynorm", "x3T", "split"] + [f"gates{i}" for i in range(GATE_PARTS)]))
W2_SPLITS = {-1: [0, 1], 3: [2], 7: [3], 11: [4], 15: [5]}
LAST_NORM_AT = 3


def order():
    chains = {x: [(n, b, pe, late) for b in range(x, B, 2) for n, pe, late in ATTENTION] for x in range(2)}
    chains[0] = chains[0][PRELUDE:]
    chains["ssm"] = [(n, 0, pe, late) for n, pe, late in SSM_START] + [s for i in range(NITER) for s in
                     [("pre", i, .5, 0), ("scan", i, .5, 0), ("add", i, 0, SSM_PERIOD)] + [("y_out", i // DS, 0, 4)] * (i % DS == DS - 1)]
    chains["mid"] = [(n, 0, pe, late) for n, pe, late in MIDDLE]
    ready = {0: 0, 1: SECOND, "ssm": 0, "mid": 0}
    done, steps, now = set(), [], 0
    while any(chains.values()):
        open_ = [c for c in chains if chains[c] and (c != "mid" or NEEDS.get(chains[c][0][0], set()) <= done)]
        c = min(open_, key=lambda c: (max(ready[c], now), ["mid", "ssm", 0, 1].index(c)))
        name, which, pe, late = chains[c].pop(0)
        now = max(now, ready[c]) + pe
        ready[c] = now + late
        steps.append((name, which))
        done.add((name, which))
    return steps


PRELUDE = 6
SECOND = 15
SSM_PERIOD = 3.5
STEPS = order()
MID_NAMES = [n for n, _, _ in MIDDLE]
SSM_NAMES = [n for n, _, _ in SSM_START] + ["pre", "scan", "add", "y_out"]


def bank_turns():
    used = [0] * 8
    turns = {}
    ring = [0]
    held = set()

    def take(key, bank=None):
        if bank is None:
            while (bank := 2 + ring[0] % 6) in held:
                ring[0] += 1
            ring[0] += 1
        turns[key] = (bank, used[bank])
        used[bank] += 1

    def step(name, b):
        if name in ("v", "b", "k", "q", "ssk", "ssq", "H", "ms") or name[0] in "PUG":
            take((name, b))
        if name in ("k", "q"):
            held.add(turns[(name, b)][0])
        if name in ("ssk", "ssq"):
            held.remove(turns[(name[2], b)][0])
        if name == "H":
            held.add(turns[("H", b)][0])
        if name == f"S{NREC}":
            held.remove(turns[("H", b)][0])
        if name == f"S{PU_FROM}":
            take(("O", b))
            held.add(turns[("O", b)][0])
        if name == "O1":
            held.remove(turns[("O", b)][0])
        if name == "wo":
            take((name, b))
            held.add(turns[("wo", b)][0])
        if name == "ln":
            held.remove(turns[("wo", b)][0])

    def mid(name, th, banks=(None, None)):
        if name in ("yT", "x3T"):
            for n in range(2):
                take((name, th, n), banks[n])
        if name == "gates0":
            take(("score", th), banks[0])
        if name == f"gates{GATE_PARTS - 2}":
            take(("gT", th), banks[1])

    for et in range(2):
        for th in range(NG):
            take(("xe", et, th), 1 + 2 * et + th)
    for n, _, _ in ATTENTION[:PRELUDE]:
        step(n, 0)
    for th in range(NG):
        take(("xdbl", th), 1 + th)
    for name, b in STEPS:
        if name in ("dt0", "dt1"):
            for th in range(NG):
                take(("dt", int(name[2]), th), 3 + th)
        if name in MID_NAMES:
            mid(name, b)
        elif name not in SSM_NAMES:
            step(name, b)
    for n in range(2):
        take(("out", n), 3 + n)
    for th in range(NG):
        for ft in range(FT):
            take(("h", th, ft), 5 + ft % 2)
            take(("G", th, ft), 1 + ft % 2)
    for name in SIDE.values():
        mid(name, 1, (7, 0))
    return turns


def decoder_layer(nc, x_tok_d, x_t_d, ctx_t_d, wqkvb_d, onorm_d, wo_d, inproj_d, convw_d, convb_d, xproj_d,
                  dtproj_d, dtb_d, alog_d, dskip_d, w1_d, b1_d, w2_d, b2_d, cent_d, ebias_d, const_d, eye3_d,
                  sel_d, lmask_d, out_d):
    turns = bank_turns()
    scr_a = nc.dram_tensor("scr_a", (B, P, BL), F32).ap()
    scr_t = nc.dram_tensor("scr_t", (B, P, C * CLO * C), F32).ap()
    scr_b = nc.dram_tensor("scr_b", (B, HH, BL), F32).ap()

    with ExitStack() as ctx:
        def sb(name, shape, dt=F32):
            return ctx.enter_context(nc.sbuf_tensor(name, shape, dt))

        def sem(name):
            return ctx.enter_context(nc.semaphore(name))

        def sems(name, n=2):
            return [sem(f"{name}{i}") for i in range(n)]

        bank = [ctx.enter_context(nc.psum_tensor(f"bank{i}", [P, 512], F32)) for i in range(8)]
        bank_b, bank_c, bank_y = bank[0], bank[1], bank[3:5]

        xT = sb("xT", [P, KT, T])
        xres = sb("xres", [P, 8, D])
        wb16 = sb("wb16", [P, KT, D])
        wo = sb("wo", [P, 2, D])
        onorm = sb("onorm", [P, 1])
        const = sb("const", [P, C_ALL])
        eye3 = sb("eye3", [96, 2 * DS], BF16)
        convw = sb("convw", [P, 2, DC])
        convb = sb("convb", [P, 2])
        dtproj = sb("dtproj", [P, DI])
        dtb = sb("dtb", [P, 2])
        alog = sb("alog", [P, 2, DS])
        dskip = sb("dskip", [P, 2])
        stk = sb("stk", [96, T], BF16)
        negA = sb("negA", [P, 2, DS])
        qke = [sb(f"qke{x}", [P, 2, NC, W3]) for x in range(2)]
        vkp = [sb(f"vkp{x}", [P, 2, NC, W3]) for x in range(2)]
        beta_kc = [sb(f"beta_kc{x}", [P, BL]) for x in range(2)]
        at_g = [sb(f"at_g{x}", [P, BL]) for x in range(2)]
        tt_s = [sb(f"tt_s{x}", [P, BL]) for x in range(2)]
        tmp_o = [sb(f"tmp_o{x}", [P, BL]) for x in range(2)]
        sq = [sb(f"sq{x}", [P, BL]) for x in range(2)]
        binst = [sb(f"binst{x}", [P, CLO * C]) for x in range(2)]
        ln_st = [sb(f"ln_st{g}", [P, 4, 6]) for g in range(3)]
        ln_mv = [sb(f"ln_mv{g}", [P, 4, 2]) for g in range(3)]
        ln_r = [sb(f"ln_r{g}", [P, 4]) for g in range(3)]
        b1 = sb("b1", [P, FT])
        cent = sb("cent", [P, KT, NE])
        ebias = sb("ebias", [P, NE])
        sig = sb("sig", [P, 4, NE])
        sc = sb("sc", [P, 4, NE])
        rank = sb("rank", [P, 4, NE])
        gsum = sb("gsum", [P, 4])
        g96 = sb("g96", [P, 4, 96])
        lmask = sb("lmask", [P, NE * NE])

        layer = ctx.enter_context(ExitStack())

        def sb_of_layer(name, shape, dt=F32):
            return layer.enter_context(nc.sbuf_tensor(name, shape, dt))

        bd_all = sb_of_layer("bd_all", [P, 2, 2, P, 2 * NC])
        arena_s = sb_of_layer("arena_s", [P, 8 * GT_])
        arena_h = sb_of_layer("arena_h", [P, 6 * GT_])
        bsb = sb_of_layer("bsb", [P, 2, GT_])
        du = sb_of_layer("du", [P, 2, T])
        delta = sb_of_layer("delta", [P, 2, T])
        u = sb_of_layer("u", [P, 2, T])
        wqkvb = sb_of_layer("wqkvb", [P, KT, 3 * D + H])
        k_uv = [sb_of_layer(f"k_uv{x}", [P, BL]) for x in range(2)]
        v_w = [sb_of_layer(f"v_w{x}", [P, BL]) for x in range(2)]
        layer.close()
        half_blocks = 2 * P * 2 * NC
        w1 = sb_of_layer("w1", [P, KT, FP])
        sel = sb_of_layer("sel", [96, FP], BF16)
        sb_of_layer("pad_b0", [P, half_blocks - KT * FP - FP // 2])
        w2 = sb_of_layer("w2", [P, FT, D])
        b2 = sb_of_layer("b2", [NX, D])
        layer.close()
        spare = (half_blocks - FT * D - D) // D
        w1_lo = sb_of_layer("w1_lo", [P, KT, FP], F32R)
        sb_of_layer("pad_c0", [P, half_blocks - KT * FP])
        w2_lo = sb_of_layer("w2_lo", [P, FT, D], F32R)
        sb_of_layer("pad_c1", [P, half_blocks - FT * D - spare * D])
        w2_hi_a = sb_of_layer("w2_hi_a", [P, spare, D], F32R)
        w1_hi = sb_of_layer("w1_hi", [P, KT, FP], F32R)
        beside = (8 * GT_ + 6 * GT_ + 2 * GT_ - KT * FP) // D
        w2_hi_b = sb_of_layer("w2_hi_b", [P, beside, D], F32R)
        x_hl0 = sb_of_layer("x_hl0", [P, 2, KT, GT_], F32R)
        w2_hi_d = sb_of_layer("w2_hi_d", [P, 2 * T // D, D], F32R)
        x_hl1 = sb_of_layer("x_hl1", [P, 2, KT, GT_], F32R)
        left = FT - spare - beside - 2 * T // D
        w2_hi_c = sb_of_layer("w2_hi_c", [P, left, D], F32R)
        sb_of_layer("pad_c2", [P, KT * (3 * D + H) - left * D])
        hg_hi = [sb_of_layer(f"hg_hi{x}", [P, GT_], F32R) for x in range(2)]
        hg_lo = [sb_of_layer(f"hg_lo{x}", [P, GT_], F32R) for x in range(2)]
        x_hl = [x_hl0, x_hl1]
        w2_runs = [(0, w2_hi_b[:, 0:2, :]), (2, w2_hi_b[:, 2:beside, :]), (beside, w2_hi_a[:, :, :]),
                   (beside + spare, w2_hi_c[:, :, :]), (beside + spare + left, w2_hi_d[:, 0:T // D, :]),
                   (beside + spare + left + T // D, w2_hi_d[:, T // D:2 * T // D, :])]

        def w2_hi(ft):
            at, place = [r for r in w2_runs if r[0] <= ft][-1]
            return place[:, ft - at, :]

        ident = const[:, C_ID:C_ID + P]
        blk = const[:, C_BLK:C_BLK + P]
        eye16 = const[:, C_E:C_E + C]
        mask_a = const[:, C_MA:C_MA + C]
        mask_p = const[:, C_MP:C_MP + C]

        def bias_col(i):
            return const[:, C_BIAS + i:C_BIAS + i + 1]

        xpad = arena_s[:, 0:2 * B * LP].rearrange("p (e b l) -> p e b l", e=2, b=B)
        ctxT = arena_s[:, 2 * B * LP:2 * B * LP + T]
        dA = arena_s[:, 0:4 * GT_].rearrange("p (k n) -> p k n", k=2)
        dBu = arena_s[:, 4 * GT_:8 * GT_].rearrange("p (k n) -> p k n", k=2)
        sp_z = arena_h[:, 0:T]
        sp_w = arena_h[:, T:2 * T]
        sp_l = arena_h[:, 2 * T:3 * T]
        inproj = arena_h[:, 2 * T:2 * T + DI]
        xproj = arena_h[:, 2 * T + DI:2 * T + DI + 2 * 104].rearrange("p (e n) -> p e n", e=2)
        hst = arena_h[:, 0:2 * GT_]
        hC = arena_h[:, 2 * GT_:4 * GT_]
        ysum = arena_h[:, 4 * GT_:6 * GT_]

        dtlo = bsb[:, :, :].rearrange("p k t -> p (k t)")

        def hcn(t):
            return t.rearrange("p (h c n) -> p h c n", h=2, c=NC)

        def nhc(t):
            return t.rearrange("p (n h c) -> p h c n", n=C, h=2)

        def flat(t):
            return t[:, :, :, :].rearrange("p h c n -> p (h c n)")

        rk = [[du[:, e, :] for e in range(2)], [flat(qke[x])[:, 0:4 * NE * NE] for x in range(2)]]
        gr1 = [bsb[0:96, 0, :], sq[0][0:96, :]]
        gm16 = [stk[:, 0:GT_], at_g[0][0:96, 0:GT_ // 2].bitcast(BF16)]
        gstk = [stk[:, GT_:2 * GT_], at_g[1][0:96, 0:GT_ // 2].bitcast(BF16)]
        gT = [wb16[0:32, :, :].rearrange("p k n -> p (k n)"), tmp_o[1][0:32, :]]
        hrel = flat(vkp[0])[:, 0:2 * GT_].rearrange("p (k n) -> p k n", k=2)

        s_ld_ssm = sem("s_ld_ssm")
        s_ld_c = sem("s_ld_c")
        s_ld_att = sem("s_ld_att")
        s_ld_w1 = sem("s_ld_w1")
        s_ld_w2 = sems("s_ld_w2_", len(w2_runs))
        s_ld_b2 = sem("s_ld_b2")
        s_w1hi = sem("s_w1hi")
        s_w1lo = sem("s_w1lo")
        s_w2hi = sem("s_w2hi")
        s_w2lo = sem("s_w2lo")
        s_xhi = sem("s_xhi")
        s_xlo = sem("s_xlo")
        s_ld_small = sem("s_ld_small")
        s_full = sems("s_full", 8)
        s_free = sems("s_free", 8)
        s_pad = sem("s_pad")
        s_xpad = sem("s_xpad")
        s_conv = sem("s_conv")
        s_u = sem("s_u")
        s_dtlo = sem("s_dtlo")
        s_stk = sem("s_stk")
        s_sp = sem("s_sp")
        s_spf = sem("s_spf")
        s_delta = sem("s_delta")
        s_du = sem("s_du")
        s_act = sem("s_act")
        s_dve = sem("s_dve")
        s_dA0 = sem("s_dA0")
        s_dA = sem("s_dA")
        s_scan = sem("s_scan")
        s_bb = sem("s_bb")
        s_bcopy = sem("s_bcopy")
        s_dbu = sem("s_dbu")
        s_cc = sem("s_cc")
        s_hc = sem("s_hc")
        s_yout = sem("s_yout")
        s_rec = sems("s_rec")
        s_zero = sem("s_zero")
        s_wb = sem("s_wb")
        s_eye = sem("s_eye")
        s_beta = sems("s_beta")
        s_bdram = sems("s_bdram")
        s_binst = sems("s_binst")
        s_v = sems("s_v")
        s_sq = sems("s_sq")
        s_clamp = sems("s_clamp")
        s_rs = sems("s_rs")
        s_k = sems("s_k")
        s_qk = sems("s_qk")
        s_exp = [sems(f"s_exp{x}_") for x in range(2)]
        s_at = sems("s_at")
        s_adram = sems("s_adram")
        s_ain = sems("s_ain")
        s_kc = sems("s_kc")
        s_vc = sems("s_vc")
        s_tt = sems("s_tt")
        s_tdram = sems("s_tdram")
        s_tcp = sems("s_tcp")
        s_tperm = sems("s_tperm")
        s_uv = sems("s_uv")
        s_w = sems("s_w")
        s_gq = sems("s_gq")
        s_s = sems("s_s")
        s_osq = sems("s_osq")
        s_ocopy = sems("s_ocopy")
        s_or = sems("s_or")
        s_on = sems("s_on")
        s_var = sems("s_var", 3)
        s_rstd = sems("s_rstd", 3)
        s_x2 = sems("s_x2_", B)
        s_z = sem("s_z")
        s_ys = sem("s_ys")
        s_x3 = sem("s_x3")
        s_x3T = sem("s_x3T")
        s_sige = sem("s_sige")
        s_g96 = sem("s_g96")
        s_gT = sem("s_gT")
        s_gstk = sem("s_gstk")
        s_rel = sem("s_rel")
        s_hghi = sem("s_hghi")
        s_hglo = sem("s_hglo")
        s_hguse = sem("s_hguse")
        s_yacc = sem("s_yacc")
        s_yaccfree = sem("s_yaccfree")
        s_last = sem("s_last")
        s_out = sem("s_out")

        block = ctx.enter_context(nc.Block())

        LD_SSM, LD_C, LD_ATT, LD_W1 = 8 * 16, 3 * 16, 4 * 16, 2 * 16

        @block.sync
        def _(sp):
            def load(dst, src, s):
                sp.dma_start(dst, src).then_inc(s, 16)

            load(ctxT, ctx_t_d, s_ld_ssm)
            load(inproj, inproj_d, s_ld_ssm)
            load(convw[:, :, :], convw_d.rearrange("(e p) k -> p e k", p=P), s_ld_ssm)
            load(convb[:, :], convb_d, s_ld_ssm)
            load(xproj, xproj_d.rearrange("(e p) k -> p e k", p=P), s_ld_ssm)
            load(dtproj[96:96 + DR, :], dtproj_d, s_ld_ssm)
            load(dtb[:, :], dtb_d, s_ld_ssm)
            load(alog[:, :, :], alog_d.rearrange("(e p) n -> p e n", p=P), s_ld_ssm)
            load(const[:, :], const_d, s_ld_c)
            load(wqkvb[:, :, :], wqkvb_d.rearrange("(k p) n -> p k n", p=P), s_ld_c)
            load(xT[:, :, :], x_t_d.rearrange("(k p) t -> p k t", p=P), s_ld_c)
            load(eye3[:, :], eye3_d, s_ld_att)
            load(xres[:, :, :], x_tok_d.rearrange("(n p) d -> p n d", p=P), s_ld_att)
            load(lmask[:, :], lmask_d, s_ld_att)
            load(wo[:, :, :], wo_d.rearrange("(k p) n -> p k n", p=P), s_ld_att)

            def read(key):
                b_, n = turns[key]
                sp.wait_ge(s_full[b_], n + 1)

            def heads():
                for h in range(HH):
                    yield h, slice(DH * h, DH * h + DH)

            def expand(x, k, src):
                for h, r in heads():
                    sp.dma_start(bd_all[r, x, k, r, :].rearrange("p m n -> p (m n)"), src[r, :]).then_inc(s_exp[x][k], 16)

            def step(name, b):
                x, n = b % 2, b // 2
                if name == "move_k":
                    sp.wait_ge(s_zero, 2 * x + 2)
                    sp.wait_ge(s_k[x], n + 1)
                    if n:
                        read(("O", b - 2))
                    expand(x, 1, k_uv[x])
                    sp.wait_ge(s_beta[x], n + 1)
                    sp.dma_start(scr_b[b], beta_kc[x][0:P:DH, :]).then_inc(s_bdram[x], 16)
                    sp.wait_ge(s_bdram[x], 16 * (n + 1))
                    sp.dma_start(binst[x][:, :], scr_b[b].rearrange("h (i e) -> (h i) e", i=16)).then_inc(s_binst[x], 16)
                if name == "move_a":
                    sp.wait_ge(s_at[x], 4 * (n + 1))
                    sp.dma_start(scr_a[b], at_g[x][:, :]).then_inc(s_adram[x], 16)
                    sp.wait_ge(s_adram[x], 16 * (n + 1))
                    for h, r in heads():
                        sp.dma_start(at_g[x][r, :].rearrange("i (t e) -> i t e", t=C),
                                     scr_a[b, r, :].rearrange("t (i e) -> i t e", i=16)).then_inc(s_ain[x], 16)
                    sp.wait_ge(s_kc[x], 4 * (n + 1))
                    expand(x, 0, beta_kc[x])
                if name == "move_t":
                    sp.wait_ge(s_tt[x], n + 1)
                    sp.dma_start(scr_t[b], tt_s[x][:, :]).then_inc(s_tdram[x], 16)
                    sp.wait_ge(s_tdram[x], 16 * (n + 1))
                    for h, r in heads():
                        sp.dma_start(at_g[x][r, :].rearrange("p (i e) -> p i e", i=16),
                                     scr_t[b, r, :].rearrange("i (j e) -> j i e", j=C)).then_inc(s_tcp[x], 16)
                if name == "expand_t":
                    sp.wait_ge(s_tperm[x], n + 1)
                    expand(x, 1, tt_s[x])
                if name == "expand_w":
                    sp.wait_ge(s_w[x], 2 * (n + 1))
                    expand(x, 1, v_w[x])
                if name == "expand_gu":
                    sp.wait_ge(s_gq[x], 4 * (n + 1))
                    expand(x, 0, at_g[x])
                    expand(x, 1, k_uv[x])
                if name == "expand_s":
                    sp.wait_ge(s_s[x], (NC - 1) * (n + 1))
                    expand(x, 0, tt_s[x])
                if (name, b) == ("ln", B - 2):
                    read(("O", B - 2))
                    load(w1[:, :, :], w1_d.rearrange("(k p) f -> p k f", p=P), s_ld_w1)
                    load(sel[:, :], sel_d, s_ld_w1)

            for name, which in STEPS:
                step(name, which)
            read(("O", B - 1))
            for n, (at, place) in enumerate(w2_runs):
                tiles = slice(at, at + place.shape[1])
                load(w2[:, tiles, :], w2_d.rearrange("(f p) d -> p f d", p=P)[:, tiles, :], s_ld_w2[n])
            load(b2[:, :], b2_d, s_ld_b2)
            for n in range(8):
                sp.wait_ge(s_last, n + 1)
                sp.dma_start(out_d[P * n:P * (n + 1), :], xres[:, n, :]).then_inc(s_out, 16)
            sp.wait_ge(s_out, 16 * 8)

        @block.gpsimd
        def _(pool):
            pool.memset(xpad[:, :, :, 0:DC - 1], 0.0).then_inc(s_pad, 1)
            for x in range(2):
                for k in range(2):
                    pool.memset(bd_all[:, x, k, :, :], 0.0).then_inc(s_zero, 1)
            pool.dma_start(dskip[:, :], dskip_d).then_inc(s_ld_small, 16)
            pool.dma_start(onorm[:, :], onorm_d).then_inc(s_ld_small, 16)
            pool.dma_start(b1[:, :], b1_d).then_inc(s_ld_small, 16)
            pool.dma_start(cent[:, :, :], cent_d.rearrange("(k p) e -> p k e", p=P)).then_inc(s_ld_small, 16)
            pool.dma_start(ebias[:, :], ebias_d.rearrange("(a e) -> a e", a=1).partition_broadcast(P)).then_inc(s_ld_small, 16)
            pool.wait_ge(s_du, 2)
            for i in range(NITER):
                th = i // DS
                pool.wait_ge(s_bcopy, i + 1)
                if i >= 2:
                    pool.wait_ge(s_scan, i - 1)
                pool.tensor_tensor(dBu[:, i % 2, :].rearrange("p (e t) -> p e t", e=2), du[:, :, GT_ * th:GT_ * th + GT_],
                                   bsb[:, i % 2, :].unsqueeze(1).broadcast_to([P, 2, GT_]), ALU.mult).then_inc(s_dbu, 1)
            pool.wait_ge(s_yout, 2 * NG)
            pool.wait_ge(s_ld_w1, LD_W1)
            for kt in range(KT):
                pool.wait_ge(s_w1hi, kt + 1)
                pool.tensor_tensor(w1_lo[:, kt, :], w1[:, kt, :], w1_hi[:, kt, :], ALU.subtract).then_inc(s_w1lo, 1)

            def split_w2(runs):
                for n in runs:
                    at, place = w2_runs[n]
                    part = slice(at, at + place.shape[1])
                    pool.wait_ge(s_w2hi, n + 1)
                    pool.tensor_tensor(w2_lo[:, part, :], w2[:, part, :], place, ALU.subtract).then_inc(s_w2lo, 1)

            split_w2(W2_SPLITS[-1])
            for th in range(NG):
                for ft in range(FT):
                    i = FT * th + ft
                    pool.wait_ge(s_hghi, i + 1)
                    pool.tensor_tensor(hg_lo[i % 2][:, :], hrel[:, i % 2, :], hg_hi[i % 2][:, :], ALU.subtract).then_inc(s_hglo, 1)
                    if th == 0:
                        split_w2(W2_SPLITS.get(ft, []))

        @block.tensor
        def _(pe):
            def fill(key):
                b_, n = turns[key]
                if n:
                    pe.wait_ge(s_free[b_], n)
                return bank[b_]

            def filled(key, mm):
                mm.then_inc(s_full[turns[key][0]], 1)

            def conv_input():
                pe.wait_ge(s_ld_ssm, LD_SSM)
                for et in range(2):
                    for th in range(NG):
                        k = ("xe", et, th)
                        filled(k, pe.matmul(fill(k)[:, :], inproj[:, P * et:P * et + P],
                                            ctxT[:, GT_ * th:GT_ * th + GT_], start=True, stop=True))

            def dt_rows():
                pe.wait_ge(s_u, 2)
                for th in range(NG):
                    k = ("xdbl", th)
                    o = fill(k)
                    for et in range(2):
                        mm = pe.matmul(o[0:104, :], xproj[:, et, :], u[:, et, GT_ * th:GT_ * th + GT_],
                                       start=(et == 0), stop=(et == 1))
                    filled(k, mm)

            def dt_all(et):
                pe.wait_ge(s_dtlo, NG)
                for th in range(NG):
                    k = ("dt", et, th)
                    filled(k, pe.matmul(fill(k)[:, :], dtproj[96:96 + DR, P * et:P * et + P],
                                        dtlo[96:96 + DR, GT_ * th:GT_ * th + GT_], start=True, stop=True))

            def broadcast_b(i):
                th, n = divmod(i, DS)
                if i:
                    pe.wait_ge(s_bcopy, i)
                pe.matmul(bank_b[:, :], eye3[:, n:n + 1].broadcast_to([96, P]), stk[:, GT_ * th:GT_ * th + GT_],
                          start=True, stop=True).then_inc(s_bb, 1)

            def broadcast_c(i):
                th, n = divmod(i, DS)
                if i:
                    pe.wait_ge(s_hc, i)
                pe.matmul(bank_c[:, :], eye3[:, DS + n:DS + n + 1].broadcast_to([96, P]), stk[:, GT_ * th:GT_ * th + GT_],
                          start=True, stop=True).then_inc(s_cc, 1)

            def blocks(x, k, half, c):
                return bd_all[:, x, k, :, NC * half + c]

            def step(name, b):
                x, n = b % 2, b // 2
                cols = slice(L * b, L * b + L)
                if name in ("v", "b", "k", "q"):
                    if (name, b) == ("k", 0):
                        pe.wait_ge(s_ld_c, LD_C)
                    if (name, b) == ("b", 0):
                        pe.wait_ge(s_wb, 1)
                    k = (name, b)
                    o = fill(k)
                    for half in range(2):
                        to = o[:, :].rearrange("p (c w j) -> p w c j", c=NC, w=2)[:, half, :, :] if name == "v" \
                            else o[:, L * half:L * half + L]
                        for kt in range(KT):
                            if name == "b":
                                w = wb16[:, kt, P * half:P * half + P]
                            else:
                                at = {"q": 0, "k": D, "v": 2 * D}[name] + P * half
                                w = wqkvb[:, kt, at:at + P]
                            mm = pe.matmul(to, w, xT[:, kt, cols], start=(kt == 0), stop=(kt == KT - 1))
                    filled(k, mm)
                if name in ("ssk", "ssq"):
                    k = (name, b)
                    o = fill(k)
                    pe.wait_ge(s_sq[x], 2 * n + (name == "ssq") + 1)
                    filled(k, pe.matmul(o[:, :], blk, sq[x][:, :], start=True, stop=True))
                if name[0] == "P":
                    half, ch = divmod(int(name[1]), 2)
                    if name == "P0":
                        pe.wait_ge(s_exp[x][1], 128 * (4 * n + 1))
                        pe.wait_ge(s_qk[x], n + 1)
                    k = (name, b)
                    o = fill(k)
                    for j in range(CH):
                        c = CH * ch + j
                        mm = pe.matmul(o[:, W3 * j:W3 * j + W3], blocks(x, 1, half, c), qke[x][:, half, c, :], start=True, stop=True)
                    filled(k, mm)
                if name[:2] == "UW":
                    pe.wait_ge(s_exp[x][1], 128 * (4 * n + 2))
                    pe.wait_ge(s_kc[x], 4 * (n + 1))
                    pe.wait_ge(s_vc[x], n + 1)
                    half = int(name[2])
                    k = (name, b)
                    o = fill(k)
                    for c in range(NC):
                        mm = pe.matmul(o[:, 2 * C * c:2 * C * c + 2 * C], blocks(x, 1, half, c), vkp[x][:, half, c, 0:2 * C], start=True, stop=True)
                    filled(k, mm)
                if name == "H":
                    pe.wait_ge(s_exp[x][0], 128 * (3 * n + 1))
                    pe.wait_ge(s_uv[x], 2 * (n + 1))
                    k = (name, b)
                    o = fill(k)
                    for half in range(2):
                        for c in range(NC):
                            at = L * half + C * c
                            mm = pe.matmul(o[:, at:at + C], blocks(x, 0, half, c), nhc(k_uv[x][:, :])[:, half, c, :],
                                           start=(half == 0 and c == 0), stop=False, skip_group_check=True)
                    filled(k, mm)
                if name[:2] == "GQ":
                    pe.wait_ge(s_exp[x][1], 128 * (4 * n + 3))
                    half = int(name[2])
                    k = (name, b)
                    o = fill(k)
                    for c in range(NC):
                        mm = pe.matmul(o[:, 2 * C * c:2 * C * c + 2 * C], blocks(x, 1, half, c), vkp[x][:, half, c, C:W3], start=True, stop=True)
                    filled(k, mm)
                if name[0] == "S":
                    c = int(name[1:])
                    if c == 1:
                        pe.wait_ge(s_exp[x][0], 128 * (3 * n + 2))
                    o = bank[turns[("H", b)][0]]
                    pe.wait_ge(s_s[x], (NC - 1) * n + c)
                    for half in range(2):
                        at = L * half + C * c
                        mm = pe.matmul(o[:, at:at + C], blocks(x, 0, half, c), nhc(tt_s[x][:, :])[:, half, c, :],
                                       start=False, stop=True, skip_group_check=True)
                    mm.then_inc(s_rec[x], 1)
                    if c >= PU_FROM:
                        if c == PU_FROM:
                            pe.wait_ge(s_exp[x][1], 128 * (4 * n + 4))
                            fill(("O", b))
                        o = bank[turns[("O", b)][0]]
                        for own in pu_chunks(c):
                            for half in range(2):
                                at = L * half + C * own
                                pe.matmul(o[:, at:at + C], blocks(x, 1, half, own), vkp[x][:, half, own, 2 * C:W3],
                                          start=(own == 0 and half == 0), stop=False, skip_group_check=True)
                if name[0] == "O":
                    half = int(name[1])
                    if half == 0:
                        pe.wait_ge(s_exp[x][0], 128 * (3 * n + 3))
                    o = bank[turns[("O", b)][0]]
                    for c in range(1, NC):
                        at = L * half + C * c
                        mm = pe.matmul(o[:, at:at + C], blocks(x, 0, half, c), qke[x][:, half, c, 0:C],
                                       start=False, stop=True, skip_group_check=True)
                    if half == 1:
                        filled(("O", b), mm)
                if name == "ms":
                    k = (name, b)
                    o = fill(k)
                    pe.wait_ge(s_osq[x], n + 1)
                    filled(k, pe.matmul(o[:, :], blk, sq[x][:, :], start=True, stop=True))
                if name == "wo":
                    pe.wait_ge(s_on[x], n + 1)
                    if b == 0:
                        pe.wait_ge(s_ld_att, LD_ATT)
                    k = (name, b)
                    o = fill(k)
                    for tt in range(2):
                        for half in range(2):
                            at = L * half + P * tt
                            mm = pe.matmul(o[:, D * tt:D * tt + D], tmp_o[x][:, at:at + P], wo[:, half, :], start=(half == 0), stop=(half == 1))
                    filled(k, mm)

            def y_rows(th):
                for bb in range(GB):
                    k = ("yT", th, bb)
                    o = fill(k)
                    pe.wait_ge(s_ys, GB * th + bb + 1)
                    for lt in range(2):
                        for et in range(2):
                            at = GT_ * th + L * bb + P * lt
                            mm = pe.transpose(o[:, D * lt + P * et:D * lt + P * et + P], u[:, et, at:at + P], ident)
                    filled(k, mm)

            def x3_columns(th):
                for n in range(2):
                    k = ("x3T", th, n)
                    o = fill(k)
                    pe.wait_ge(s_x3, 4 * th + 2 * n + 2)
                    for kt in range(KT):
                        for lt in range(2):
                            at = L * kt + P * lt
                            mm = pe.transpose(o[:, at:at + P], xres[:, 4 * th + 2 * n + lt, P * kt:P * kt + P], ident)
                    filled(k, mm)

            def gates(th, part):
                if part == 0:
                    if th == 0:
                        pe.wait_ge(s_ld_small, 80)
                    pe.wait_ge(s_x3T, 2 * (th + 1))
                    k = ("score", th)
                    o = fill(k)
                    for tt in range(4):
                        for kt in range(KT):
                            mm = pe.matmul(o[:, NE * tt:NE * tt + NE], xT[:, kt, GT_ * th + P * tt:GT_ * th + P * tt + P],
                                           cent[:, kt, :], start=(kt == 0), stop=(kt == KT - 1))
                    filled(k, mm)
                if part == GATE_PARTS - 2:
                    k = ("gT", th)
                    o = fill(k)
                    pe.wait_ge(s_g96, th + 1)
                    for tt in range(4):
                        mm = pe.transpose(o[0:96, P * tt:P * tt + P], g96[:, tt, :], ident)
                    filled(k, mm)

            def experts(th):
                def hidden(ft):
                    k = ("h", th, ft)
                    o = fill(k)
                    if ft == 0:
                        pe.wait_ge(s_xlo, th + 1)
                    if (th, ft) == (0, 0):
                        pe.wait_ge(s_w1lo, KT)
                    for kt in range(KT):
                        w_hi, w_lo = (w[:, kt, P * ft:P * ft + P] for w in (w1_hi, w1_lo))
                        pe.matmul(o[:, :], w_hi, x_hl[th][:, 0, kt, :], start=(kt == 0), stop=False)
                        pe.matmul(o[:, :], w_hi, x_hl[th][:, 1, kt, :], start=False, stop=False)
                        mm = pe.matmul(o[:, :], w_lo, x_hl[th][:, 0, kt, :], start=False, stop=(kt == KT - 1))
                    filled(k, mm)
                    k = ("G", th, ft)
                    o = fill(k)
                    if ft == 0:
                        pe.wait_ge(s_gstk, th + 1)
                    filled(k, pe.matmul(o[:, :], sel[:, P * ft:P * ft + P], gstk[th], start=True, stop=True))

                def outputs(ft):
                    if th == 0:
                        pe.wait_ge(s_w2lo, sum(ft >= at for at, _ in w2_runs))
                    i = FT * th + ft
                    w_hi, w_lo = w2_hi(ft), w2_lo[:, ft, :]
                    pe.wait_ge(s_hghi, i + 1)
                    for tt in range(4):
                        o = bank_y[tt // 2][:, D * (tt % 2):D * (tt % 2) + D]
                        h_hi = hg_hi[i % 2][:, P * tt:P * tt + P]
                        pe.matmul(o, h_hi, w_hi, start=(ft == 0 and tt % 2 == 0), stop=False, skip_group_check=True)
                        pe.matmul(o, h_hi, w_lo, start=False, stop=False, skip_group_check=True)
                    pe.wait_ge(s_hglo, i + 1)
                    for tt in range(4):
                        o = bank_y[tt // 2][:, D * (tt % 2):D * (tt % 2) + D]
                        mm = pe.matmul(o, hg_lo[i % 2][:, P * tt:P * tt + P], w_hi, start=False, stop=False, skip_group_check=True)
                    mm.then_inc(s_hguse, 1)

                hidden(0)
                for ft in range(FT):
                    if ft + 1 < FT:
                        hidden(ft + 1)
                    if ft == 0:
                        for n in range(2):
                            fill(("out", n))
                        if th:
                            pe.wait_ge(s_yaccfree, 4 * th)
                    outputs(ft)
                    if th == 0 and ft in SIDE:
                        middle(SIDE[ft], 1)
                if th == 0:
                    pe.wait_ge(s_ld_b2, 16)
                for tt in range(4):
                    o = bank_y[tt // 2][:, D * (tt % 2):D * (tt % 2) + D]
                    pe.matmul(o, gT[th][0:NX, P * tt:P * tt + P], b2[:, :], start=False, stop=True,
                              skip_group_check=True).then_inc(s_yacc, 1)

            def middle(name, th):
                if name == "yT":
                    y_rows(th)
                if name == "x3T":
                    x3_columns(th)
                if name[:5] == "gates":
                    gates(th, int(name[5:]))

            conv_input()
            for name, _, _ in ATTENTION[:PRELUDE]:
                step(name, 0)
            dt_rows()
            for name, which in STEPS:
                if name in ("dt0", "dt1"):
                    dt_all(int(name[2]))
                elif name == "begin":
                    pe.wait_ge(s_stk, NG)
                    pe.wait_ge(s_ld_att, LD_ATT)
                    broadcast_b(0)
                elif name == "pre":
                    if which + 1 < NITER:
                        broadcast_b(which + 1)
                elif name == "scan":
                    broadcast_c(which)
                elif name in MID_NAMES:
                    middle(name, which)
                elif name not in SSM_NAMES:
                    step(name, which)
            for th in range(NG):
                experts(th)

        @block.scalar
        def _(act):
            chain = [0]

            def link(ins):
                chain[0] += 1
                ins.then_inc(s_act, 1)
                act.wait_ge(s_act, chain[0])

            def take(key):
                b_, n = turns[key]
                act.wait_ge(s_full[b_], n + 1)
                return bank[b_]

            def free(key):
                act.nop().then_inc(s_free[turns[key][0]], 1)

            def signal(ins, s, count, key):
                ins.then_inc(s, 1)
                act.wait_ge(s, count)
                free(key)

            def prelude():
                for et in range(2):
                    for th in range(NG):
                        k = ("xe", et, th)
                        o = take(k)
                        link(act.activation(xpad[:, et, GB * th:GB * th + GB, DC - 1:LP],
                                            o[:, :].rearrange("p (b l) -> p b l", b=GB), ACT.Copy))
                        free(k)
                        act.nop().then_inc(s_xpad, 1)
                for et in range(2):
                    act.wait_ge(s_conv, et + 1)
                    act.activation(u[:, et, :], u[:, et, :], ACT.Silu).then_inc(s_u, 1)
                for name, _, _ in ATTENTION[:PRELUDE]:
                    step(name, 0)
                link(act.activation(negA[:, :, :], alog[:, :, :], ACT.Exp))
                link(act.activation(negA[:, :, :], negA[:, :, :], ACT.Copy, scale=-1.0))
                for th in range(NG):
                    o = take(("xdbl", th))
                    act.activation(dtlo[96:96 + DR, GT_ * th:GT_ * th + GT_], o[96:96 + DR, :], ACT.Copy).then_inc(s_dtlo, 1)

            def softplus(et):
                if et:
                    act.wait_ge(s_spf, et)
                for th in range(NG):
                    k = ("dt", et, th)
                    o = take(k)
                    c_ = slice(GT_ * th, GT_ * th + GT_)
                    act.activation(delta[:, et, c_], o[:, :], ACT.Identity, bias=dtb[:, et:et + 1])
                    link(act.activation(sp_l[:, c_], o[:, :], ACT.Abs, bias=dtb[:, et:et + 1]))
                    free(k)
                link(act.activation(sp_z, sp_l, ACT.Exp, scale=-1.0))
                link(act.activation(sp_w, sp_z, ACT.Identity, bias=bias_col(BI_ONE)))
                act.activation(sp_l, sp_w, ACT.Ln).then_inc(s_sp, 1)

            def copy_b(i):
                act.wait_ge(s_bb, i + 1)
                if i >= 2:
                    act.wait_ge(s_dbu, i - 1)
                act.activation(bsb[:, i % 2, :], bank_b[:, :], ACT.Copy).then_inc(s_bcopy, 1)

            def decays(i):
                th, n = divmod(i, DS)
                if i >= 2:
                    act.wait_ge(s_scan, i - 1)
                for et in range(2):
                    o = dA[:, i % 2, GT_ * et:GT_ * et + GT_].rearrange("p (b l) -> p b l", b=GB)[:, :, 1:L]
                    src = delta[:, et, GT_ * th:GT_ * th + GT_].rearrange("p (b l) -> p b l", b=GB)[:, :, 1:L]
                    act.activation(o, src, ACT.Exp, scale=negA[:, et, n:n + 1]).then_inc(s_dA, 1)

            def step(name, b):
                x, n = b % 2, b // 2
                k = (name, b)
                if name == "v":
                    if n:
                        act.wait_ge(s_on[x], n)
                    signal(act.activation(v_w[x][:, :], take(k)[:, :], ACT.Silu),
                           s_v[x], n + 1, k)
                if name == "b":
                    signal(act.activation(beta_kc[x][:, :], take(k)[:, :], ACT.Sigmoid),
                           s_beta[x], n + 1, k)
                    nc.scalar.preload_act_table_set(LN_EXP)
                if name in ("k", "q"):
                    o = take(k)
                    if name == "q":
                        act.wait_ge(s_clamp[x], 2 * n + 1)
                    act.activation(sq[x][:, :], o[:, :], ACT.Square).then_inc(s_sq[x], 1)
                if name in ("ssk", "ssq"):
                    act.wait_ge(s_clamp[x], 2 * n + 1 + (name == "ssq"))
                    r = tmp_o[x][:, :]
                    link(act.activation(r, r, ACT.Ln, scale=float(2 ** SCALE_LOG2)))
                    act.activation(r, r, ACT.Exp, scale=-0.5,
                                   bias=bias_col(BI_Q if name == "ssq" else BI_K)).then_inc(s_rs[x], 1)
                if name[0] == "P":
                    w = int(name[1])
                    half, ch = divmod(w, 2)
                    o = take(k)[:, 0:CH * W3].rearrange("p (c n) -> p c n", c=CH)[:, :, 2 * C:W3]
                    act.wait_ge(s_at[x], 4 * n + w + 1)
                    if w == 0:
                        act.wait_ge(s_bdram[x], 16 * (n + 1))
                    cs = slice(CH * ch, CH * ch + CH)
                    act.activation(vkp[x][:, half, cs, C:2 * C], o, ACT.Copy)
                    signal(act.activation(nhc(beta_kc[x][:, :])[:, half, cs, :], o, ACT.Copy),
                           s_kc[x], 4 * n + w + 1, k)
                if name == "turn_t":
                    act.wait_ge(s_tcp[x], 128 * (n + 1))
                    act.activation(nhc(tt_s[x][:, :]), hcn(at_g[x][:, :]), ACT.Copy).then_inc(s_tperm[x], 1)
                if name[:2] == "UW":
                    half = int(name[2])
                    o = take(k)[:, :].rearrange("p (c n) -> p c n", c=NC)[:, :, 0:C]
                    act.wait_ge(s_w[x], 2 * n + half + 1)
                    signal(act.activation(nhc(k_uv[x][:, :])[:, half, :, :], o, ACT.Copy),
                           s_uv[x], 2 * n + half + 1, k)
                if name == "H":
                    o = take(k)
                    act.wait_ge(s_exp[x][1], 128 * (4 * n + 2))
                    act.activation(nhc(tt_s[x][:, :])[:, :, 1, :], hcn(o[:, :])[:, :, 0, :], ACT.Copy).then_inc(s_s[x], 1)
                if name[0] == "S":
                    c = int(name[1:])
                    k = ("H", b)
                    act.wait_ge(s_rec[x], NREC * n + c)
                    o = hcn(bank[turns[k][0]][:, :])[:, :, c, :]
                    act.activation(nhc(tt_s[x][:, :])[:, :, c + 1, :], o, ACT.Copy).then_inc(s_s[x], 1)
                    if c == NREC:
                        act.wait_ge(s_s[x], (NC - 1) * (n + 1))
                        free(k)
                if name == "O1":
                    k = ("O", b)
                    o = take(k)
                    act.activation(sq[x][:, :], o[:, :], ACT.Square).then_inc(s_osq[x], 1)
                    link(act.activation(tmp_o[x][:, :], o[:, :], ACT.Copy))
                    act.nop().then_inc(s_ocopy[x], 1)
                    free(k)
                if name == "ms":
                    r = v_w[x][:, :]
                    link(act.activation(r, take(k)[:, :], ACT.Ln, scale=1.0 / DH, bias=bias_col(BI_EPS)))
                    free(k)
                    act.activation(r, r, ACT.Exp, scale=-0.5).then_inc(s_or[x], 1)
                if name == "ln":
                    rstd(x)
                if (name, b) == ("expand_s", B - 1):
                    act.wait_ge(s_yout, 2 * NG)
                    act.wait_ge(s_ld_w1, LD_W1)
                    for kt in range(KT):
                        act.activation(w1_hi[:, kt, :], w1[:, kt, :], ACT.Copy).then_inc(s_w1hi, 1)

            norms = [0] * 3

            def rstd(g):
                norms[g] += 1
                act.wait_ge(s_var[g], norms[g])
                link(act.activation(ln_r[g][:, :], ln_mv[g][:, :, 1], ACT.Ln, bias=bias_col(BI_EPS)))
                act.activation(ln_r[g][:, :], ln_r[g][:, :], ACT.Exp, scale=-0.5).then_inc(s_rstd[g], 1)

            def gate(th):
                act.wait_ge(s_yout, 2 * (th + 1))
                for bb in range(GB):
                    b = GB * th + bb
                    act.wait_ge(s_x2[b], 2)
                    act.activation(delta[:, :, L * b:L * b + L], xres[:, 2 * b:2 * b + 2, :], ACT.Silu).then_inc(s_z, 1)
                nc.scalar.preload_act_table_set(LN_EXP)

            def x3_columns(th):
                for n in range(2):
                    k = ("x3T", th, n)
                    o = take(k)[:, :].rearrange("p (k t) -> p k t", k=KT)
                    at = GT_ * th + L * n
                    signal(act.activation(xT[:, :, at:at + L], o, ACT.Copy),
                           s_x3T, 2 * th + n + 1, k)

            def split_x3(th):
                if th == 0:
                    act.wait_ge(s_gstk, 1)
                act.activation(x_hl[th][:, 0, :, :], xT[:, :, GT_ * th:GT_ * th + GT_], ACT.Copy).then_inc(s_xhi, 1)

            def gates(th, part):
                if part == 0:
                    if th == 0:
                        act.wait_ge(s_ld_small, 80)
                    k = ("score", th)
                    o = take(k)
                    signal(act.activation(sig[:, :, :], o[:, 0:4 * NE].rearrange("p (t e) -> p t e", t=4), ACT.Sigmoid),
                           s_sige, th + 1, k)
                    nc.scalar.preload_act_table_set(LN_EXP)
                if part == GATE_PARTS - 2:
                    act.activation(gT[th], take(("gT", th))[0:32, :], ACT.Copy).then_inc(s_gT, 1)

            def split_w2(runs):
                for n in runs:
                    at, place = w2_runs[n]
                    act.wait_ge(s_ld_w2[n], 16)
                    act.activation(place, w2[:, at:at + place.shape[1], :], ACT.Copy).then_inc(s_w2hi, 1)

            def experts(th):
                if th == 0:
                    split_w2(W2_SPLITS[-1])
                for ft in range(FT):
                    k = ("h", th, ft)
                    i = FT * th + ft
                    o = take(k)
                    if i >= 2:
                        act.wait_ge(s_hglo, i - 1)
                    signal(act.activation(hrel[:, i % 2, :], o[:, :], ACT.Relu, bias=b1[:, ft:ft + 1]),
                           s_rel, i + 1, k)
                    if th == 0 and ft - 1 in SIDE:
                        middle(SIDE[ft - 1], 1)
                    if th == 0:
                        split_w2(W2_SPLITS.get(ft, []))
                    if th and ft == LAST_NORM_AT:
                        rstd(MID)
                if th:
                    rstd(MID)

            def middle(name, th):
                if name == "gate":
                    gate(th)
                if name == "yT":
                    rstd(MID)
                if name == "x3T":
                    x3_columns(th)
                if name == "split":
                    split_x3(th)
                if name[:5] == "gates":
                    gates(th, int(name[5:]))

            prelude()
            for name, which in STEPS:
                if name in ("dt0", "dt1"):
                    softplus(int(name[2]))
                elif name == "begin":
                    act.wait_ge(s_delta, 2)
                    act.wait_ge(s_dA0, 2)
                    copy_b(0)
                    decays(0)
                elif name == "pre":
                    if which + 1 < NITER:
                        copy_b(which + 1)
                        decays(which + 1)
                elif name in MID_NAMES:
                    middle(name, which)
                elif name not in SSM_NAMES:
                    step(name, which)
            for th in range(NG):
                experts(th)

        @block.vector
        def _(dve):
            chain = [0]

            def link(ins):
                chain[0] += 1
                ins.then_inc(s_dve, 1)
                dve.wait_ge(s_dve, chain[0])

            def take(key):
                b_, n = turns[key]
                dve.wait_ge(s_full[b_], n + 1)
                return bank[b_]

            def free(key):
                dve.nop().then_inc(s_free[turns[key][0]], 1)

            def signal(ins, s, count, key):
                ins.then_inc(s, 1)
                dve.wait_ge(s, count)
                free(key)

            norms = [0] * 3

            def norm_stats(g, first, tiles):
                st, mv = ln_st[g], ln_mv[g]
                if norms[g] == 0:
                    link(dve.memset(mv[:, :, :], 1.0))
                for tt in range(tiles):
                    dve.bn_stats(st[:, tt, :], xres[:, first + tt, :]).then_inc(s_dve, 1)
                chain[0] += tiles
                dve.wait_ge(s_dve, chain[0])
                for tt in range(tiles):
                    dve.bn_aggr(mv[:, tt, :], st[:, tt, :]).then_inc(s_dve, 1)
                chain[0] += tiles
                dve.wait_ge(s_dve, chain[0])
                norms[g] += 1
                dve.nop().then_inc(s_var[g], 1)

            def norm_apply(g, first, tiles, done):
                dve.wait_ge(s_rstd[g], norms[g])
                for tt in range(tiles):
                    dve.tensor_scalar(xres[:, first + tt, :], xres[:, first + tt, :], ln_mv[g][:, tt, 0:1],
                                      ln_r[g][:, tt:tt + 1], ALU.subtract, ALU.mult).then_inc(done, 1)

            def prelude():
                dve.wait_ge(s_ld_ssm, LD_SSM)
                dve.wait_ge(s_pad, 1)
                for et in range(2):
                    dve.wait_ge(s_xpad, 2 * et + 2)
                    v = u[:, et, :].rearrange("p (b l) -> p b l", b=B)
                    link(dve.tensor_scalar(v, xpad[:, et, :, 0:L], convw[:, et, 0:1], convb[:, et:et + 1], ALU.mult, ALU.add))
                    for k in range(1, DC):
                        ins = dve.scalar_tensor_tensor(out=v, in0=xpad[:, et, :, k:k + L], scalar=convw[:, et, k:k + 1],
                                                       in1=v, op0=ALU.mult, op1=ALU.add)
                        if k < DC - 1:
                            link(ins)
                    ins.then_inc(s_conv, 1)
                    if et == 0:
                        dve.wait_ge(s_ld_c, LD_C)
                        for kt in range(KT):
                            ins = dve.tensor_copy(wb16[:, kt, :].rearrange("p (h r) -> p h r", h=H),
                                                  wqkvb[:, kt, 3 * D:3 * D + H].unsqueeze(2).broadcast_to([P, H, DH]))
                            if kt < KT - 1:
                                link(ins)
                        link(ins)
                        dve.nop().then_inc(s_wb, 1)
                for x in range(2):
                    dve.tensor_copy(qke[x][:, :, :, 2 * C:W3].rearrange("p h c n -> p (h c) n"),
                                    eye16.unsqueeze(1).broadcast_to([P, 2 * NC, C])).then_inc(s_eye, 1)
                for name, _, _ in ATTENTION[:PRELUDE]:
                    step(name, 0)
            def stack():
                dve.wait_ge(s_u, 2)
                hi, r1, mid16 = gm16[1], gr1[1], gstk[1]
                for th in range(NG):
                    k = ("xdbl", th)
                    o = take(k)
                    c_ = slice(GT_ * th, GT_ * th + GT_)
                    dve.wait_ge(s_dtlo, th + 1)
                    link(dve.tensor_copy(hi, o[0:96, :]))
                    link(dve.tensor_tensor(r1, o[0:96, :], hi, ALU.subtract))
                    free(k)
                    dve.tensor_copy(stk[0:32, c_], hi[0:32, :])
                    link(dve.tensor_copy(mid16, r1))
                    dve.tensor_copy(stk[32:64, c_], mid16[32:64, :])
                    link(dve.tensor_tensor(r1[64:96, :], r1[64:96, :], mid16[64:96, :], ALU.subtract))
                    link(dve.tensor_copy(stk[64:96, c_], r1[64:96, :]))
                    dve.nop().then_inc(s_stk, 1)
            def softplus(et):
                dve.wait_ge(s_sp, et + 1)
                link(dve.scalar_tensor_tensor(out=sp_w, in0=sp_w, scalar=1.0, in1=sp_z, op0=ALU.subtract, op1=ALU.subtract))
                link(dve.tensor_tensor(sp_l, sp_l, sp_w, ALU.subtract))
                link(dve.scalar_tensor_tensor(out=delta[:, et, :], in0=delta[:, et, :], scalar=0.0, in1=sp_l,
                                              op0=ALU.max, op1=ALU.add))
                dve.nop().then_inc(s_spf, 1)
                dve.nop().then_inc(s_delta, 1)
                dve.tensor_tensor(du[:, et, :], delta[:, et, :], u[:, et, :], ALU.mult).then_inc(s_du, 1)

            def begin():
                for k in range(2):
                    v = dA[:, k, :].rearrange("p (n l) -> p n l", l=L)[:, :, 0:1]
                    dve.memset(v, 0.0).then_inc(s_dA0, 1)
                dve.wait_ge(s_dA0, 2)

            def scan(i):
                dve.wait_ge(s_dA, 2 * (i + 1))
                dve.wait_ge(s_dbu, i + 1)
                link(dve.tensor_tensor_scan(hst, dA[:, i % 2, :], dBu[:, i % 2, :], 0.0, ALU.mult, ALU.add))
                dve.nop().then_inc(s_scan, 1)

            def add_states(i):
                n = i % DS
                dve.wait_ge(s_cc, i + 1)
                h_c = hC[:, :].rearrange("p (e t) -> p e t", e=2)
                link(dve.tensor_tensor(h_c, hst.rearrange("p (e t) -> p e t", e=2),
                                       bank_c[:, :].unsqueeze(1).broadcast_to([P, 2, GT_]), ALU.mult))
                dve.nop().then_inc(s_hc, 1)
                if n == 0:
                    link(dve.tensor_copy(ysum, hC))
                else:
                    link(dve.tensor_tensor(ysum, ysum, hC, ALU.add))

            def y_out(th):
                if th == 0:
                    dve.wait_ge(s_ld_small, 80)
                c_ = slice(GT_ * th, GT_ * th + GT_)
                for et in range(2):
                    dve.scalar_tensor_tensor(out=u[:, et, c_], in0=u[:, et, c_], scalar=dskip[:, et:et + 1],
                                             in1=ysum[:, GT_ * et:GT_ * et + GT_], op0=ALU.mult, op1=ALU.add).then_inc(s_yout, 1)

            def solve(b, rows):
                x, n = b % 2, b // 2
                a_t = at_g[x][:, :].rearrange("p (s c t) -> p s c t", s=C, c=CLO)
                t_t = tt_s[x][:, :].rearrange("p (j c t) -> p j c t", j=C, c=CLO)
                for t in rows:
                    if t == 0:
                        if n:
                            dve.wait_ge(s_exp[x][0], 128 * 3 * n)
                        link(dve.memset(tt_s[x][:, :], 0.0))
                        for c in range(CLO):
                            ins = dve.memset(tt_s[x][:, C * c:C * c + (CLO * C + 1) * (C - 1) + 1:CLO * C + 1], 1.0)
                            if c < CLO - 1:
                                link(ins)
                        link(ins)
                        dve.wait_ge(s_ain[x], 128 * (n + 1))
                        continue
                    prod = tmp_o[x][:, 0:CLO * t * t].rearrange("p (c j s) -> p c j s", c=CLO, j=t)
                    a = a_t[:, 0:t, :, t].rearrange("p s c -> p c s").unsqueeze(2).broadcast_to([P, CLO, t, t])
                    link(dve.tensor_tensor(prod, a, t_t[:, 0:t, :, 0:t].rearrange("p j c s -> p c j s"), ALU.mult))
                    link(dve.tensor_reduce(t_t[:, 0:t, :, t].rearrange("p j c -> p c j"), prod, AX_X, ALU.add, negate=True))
                    if t == C - 1:
                        dve.wait_ge(s_binst[x], 16 * (n + 1))
                        bt = binst[x][:, :].rearrange("p (c j) -> p j c", c=CLO).unsqueeze(3).broadcast_to([P, C, CLO, C])
                        link(dve.tensor_tensor(t_t, t_t, bt, ALU.mult))
                        dve.nop().then_inc(s_tt[x], 1)

            def step(name, b):
                x, n = b % 2, b // 2
                k = (name, b)
                if name == "v":
                    dve.wait_ge(s_v[x], n + 1)
                    dve.transpose(vkp[x][:, :, :, 0:C].rearrange("p h c n -> p c h n"),
                                  v_w[x][:, :].rearrange("p (c h n) -> p c h n", c=NC, h=2)).then_inc(s_vc[x], 1)
                if name in ("ssk", "ssq"):
                    w = 2 * n + (name == "ssq")
                    o = take(k)
                    r = tmp_o[x][:, :]
                    signal(dve.tensor_scalar(r, o[:, :], 1e-24, None, ALU.max),
                           s_clamp[x], w + 1, k)
                    dve.wait_ge(s_rs[x], w + 1)
                    k = (name[2], b)
                    o = take(k)
                    if name == "ssq":
                        signal(dve.tensor_tensor(qke[x][:, :, :, 0:C], hcn(o[:, :]), hcn(r), ALU.mult),
                               s_qk[x], n + 1, k)
                    else:
                        signal(dve.tensor_tensor(nhc(k_uv[x][:, :]), hcn(o[:, :]), hcn(r), ALU.mult),
                               s_k[x], n + 1, k)
                        dve.wait_ge(s_beta[x], n + 1)
                        dve.wait_ge(s_eye, 2)
                        link(dve.tensor_tensor(qke[x][:, :, :, C:2 * C], nhc(k_uv[x][:, :]), hcn(beta_kc[x][:, :]), ALU.mult))
                if name[0] == "P":
                    half, ch = divmod(int(name[1]), 2)
                    o = take(k)[:, 0:CH * W3].rearrange("p (c n) -> p c n", c=CH)
                    cs = slice(CH * ch, CH * ch + CH)
                    dve.tensor_tensor(vkp[x][:, half, cs, 2 * C:W3], o[:, :, 0:C],
                                      mask_p.unsqueeze(1).broadcast_to([P, CH, C]), ALU.mult).then_inc(s_dve, 1)
                    chain[0] += 1
                    dve.tensor_tensor(hcn(at_g[x][:, :])[:, half, cs, :], o[:, :, C:2 * C],
                                      mask_a.unsqueeze(1).broadcast_to([P, CH, C]), ALU.mult).then_inc(s_at[x], 1)
                if name[:5] == "solve":
                    solve(b, [range(0, 8), range(8, 12), range(12, 16)][int(name[5])])
                if name[:2] == "UW":
                    half = int(name[2])
                    o = take(k)[:, :].rearrange("p (c n) -> p c n", c=NC)[:, :, C:2 * C]
                    dve.tensor_copy(nhc(v_w[x][:, :])[:, half, :, :], o).then_inc(s_w[x], 1)
                if name[:2] == "GQ":
                    half = int(name[2])
                    o = take(k)[:, :].rearrange("p (c n) -> p c n", c=NC)
                    dve.tensor_tensor(nhc(at_g[x][:, :])[:, half, :, :], eye16.unsqueeze(1).broadcast_to([P, NC, C]),
                                      o[:, :, 0:C], ALU.subtract).then_inc(s_gq[x], 1)
                    signal(dve.tensor_tensor(qke[x][:, half, :, 0:C], qke[x][:, half, :, 0:C], o[:, :, C:2 * C], ALU.subtract),
                           s_gq[x], 2 * (2 * n + half + 1), k)
                if name == "ms":
                    dve.wait_ge(s_or[x], n + 1)
                    dve.wait_ge(s_ocopy[x], n + 1)
                    if b == 0:
                        dve.wait_ge(s_ld_small, 80)
                        dve.wait_ge(s_ld_att, LD_ATT)
                    v = tmp_o[x][:, :]
                    dve.scalar_tensor_tensor(out=v, in0=v, scalar=onorm[:, 0:1], in1=v_w[x][:, :],
                                             op0=ALU.mult, op1=ALU.mult).then_inc(s_on[x], 1)
                if name == "ln":
                    k = ("wo", b)
                    xr = xres[:, 2 * b:2 * b + 2, :]
                    link(dve.tensor_tensor(xr, xr, take(k)[:, :].rearrange("p (t d) -> p t d", t=2), ALU.add))
                    free(k)
                    norm_stats(x, 2 * b, 2)
                if name == "lnorm":
                    norm_apply(x, 2 * b, 2, s_x2[b])

            def gate(th):
                dve.wait_ge(s_yout, 2 * (th + 1))
                for bb in range(GB):
                    b = GB * th + bb
                    dve.wait_ge(s_x2[b], 2)
                    dve.wait_ge(s_z, b + 1)
                    yv = u[:, :, L * b:L * b + L]
                    dve.tensor_tensor(yv, yv, delta[:, :, L * b:L * b + L], ALU.mult).then_inc(s_ys, 1)

            def y_rows(th):
                for n in range(2):
                    k = ("yT", th, n)
                    x = xres[:, 4 * th + 2 * n:4 * th + 2 * n + 2, :]
                    link(dve.tensor_tensor(x, x, take(k)[:, :].rearrange("p (t d) -> p t d", t=2), ALU.add))
                    free(k)
                norm_stats(MID, 4 * th, 4)

            def split_x3(th):
                dve.wait_ge(s_xhi, th + 1)
                dve.tensor_tensor(x_hl[th][:, 1, :, :], xT[:, :, GT_ * th:GT_ * th + GT_], x_hl[th][:, 0, :, :],
                                  ALU.subtract).then_inc(s_xlo, 1)

            def gates(th, part):
                rk0, rk1 = rk[th]
                ge = rk0.rearrange("p (t e j) -> p t e j", t=4, e=NE)
                gt = rk1.rearrange("p (t e j) -> p t e j", t=4, e=NE)
                s_j = sc[:, :, :].unsqueeze(2).broadcast_to([P, 4, NE, NE])
                s_e = sc[:, :, :].unsqueeze(3).broadcast_to([P, 4, NE, NE])
                lm = lmask[:, :].unsqueeze(1).broadcast_to([P, 4, NE * NE])
                if part == 0:
                    dve.wait_ge(s_sige, th + 1)
                    link(dve.tensor_tensor(sc[:, :, :], sig[:, :, :], ebias[:, :].unsqueeze(1).broadcast_to([P, 4, NE]), ALU.add))
                    link(dve.tensor_tensor(gt, s_j, s_e, ALU.is_gt))
                if part == 1:
                    link(dve.tensor_tensor(ge, s_j, s_e, ALU.is_ge))
                if part == 2:
                    link(dve.tensor_tensor(rk0.rearrange("p (t n) -> p t n", t=4), rk0.rearrange("p (t n) -> p t n", t=4), lm, ALU.mult))
                if part == 3:
                    link(dve.tensor_tensor(rk0, rk0, rk1, ALU.max))
                if part == 4:
                    link(dve.tensor_reduce(rank[:, :, :], ge, AX_X, ALU.add))
                if part == 5:
                    link(dve.scalar_tensor_tensor(out=sc[:, :, :], in0=rank[:, :, :], scalar=float(KR) - 0.5, in1=sc[:, :, :],
                                                  op0=ALU.is_lt, op1=ALU.mult))
                    link(dve.tensor_reduce(gsum[:, :], sc[:, :, :], AX_X, ALU.add))
                    link(dve.tensor_scalar(gsum[:, :], gsum[:, :], 1e-8, None, ALU.max))
                    link(dve.reciprocal(gsum[:, :], gsum[:, :]))
                    if th == 0:
                        link(dve.memset(g96[:, :, :], 0.0))
                    for r in range(3):
                        dve.memset(g96[:, :, 32 * r:32 * r + NSH], 1.0)
                        link(dve.tensor_tensor(g96[:, :, 32 * r + NSH:32 * r + NX], sc[:, :, :],
                                               gsum[:, :].unsqueeze(2).broadcast_to([P, 4, NE]), ALU.mult))
                    dve.nop().then_inc(s_g96, 1)
                k = ("gT", th)
                stack = gstk[th]
                if part == 6:
                    o = take(k)
                    hi = gm16[th]
                    dve.wait_ge(s_gT, th + 1)
                    link(dve.tensor_copy(hi, o[0:96, :]))
                    link(dve.tensor_copy(stack[0:32, :], hi[0:32, :]))
                    link(dve.tensor_tensor(gr1[th], o[0:96, :], hi, ALU.subtract))
                    free(k)
                if part == 7:
                    mid16, r1 = gm16[th], gr1[th]
                    link(dve.tensor_copy(mid16, r1))
                    link(dve.tensor_copy(stack[32:64, :], mid16[32:64, :]))
                    link(dve.tensor_tensor(r1[64:96, :], r1[64:96, :], mid16[64:96, :], ALU.subtract))
                    link(dve.tensor_copy(stack[64:96, :], r1[64:96, :]))
                    dve.nop().then_inc(s_gstk, 1)

            def experts(th):
                for ft in range(FT):
                    i = FT * th + ft
                    k = ("G", th, ft)
                    o = take(k)
                    dve.wait_ge(s_rel, i + 1)
                    h = hrel[:, i % 2, :]
                    link(dve.tensor_tensor(h, h, o[:, :], ALU.mult))
                    free(k)
                    if i >= 2:
                        dve.wait_ge(s_hguse, i - 1)
                    dve.tensor_copy(hg_hi[i % 2][:, :], h).then_inc(s_hghi, 1)
                    if th == 0 and ft - 1 in SIDE:
                        middle(SIDE[ft - 1], 1)
                    if th and ft == LAST_NORM_AT:
                        norm_stats(MID, 0, 4)
                    if th and ft == LAST_NORM_AT + 1:
                        norm_apply(MID, 0, 4, s_last)
                for tt in range(4):
                    dve.wait_ge(s_yacc, 4 * th + 2 * (tt // 2) + 2)
                    o = bank_y[tt // 2][:, D * (tt % 2):D * (tt % 2) + D]
                    link(dve.scalar_tensor_tensor(out=xres[:, 4 * th + tt, :], in0=xres[:, 4 * th + tt, :], scalar=2.0,
                                                  in1=o, op0=ALU.mult, op1=ALU.add))
                    dve.nop().then_inc(s_yaccfree, 1)
                if th:
                    norm_stats(MID, 4, 4)
                    norm_apply(MID, 4, 4, s_last)

            def middle(name, th):
                if name == "gate":
                    gate(th)
                if name == "yT":
                    y_rows(th)
                if name == "ynorm":
                    norm_apply(MID, 4 * th, 4, s_x3)
                if name == "split":
                    split_x3(th)
                if name[:5] == "gates":
                    gates(th, int(name[5:]))

            prelude()
            for name, which in STEPS:
                if name == "stack":
                    stack()
                elif name in ("dt0", "dt1"):
                    softplus(int(name[2]))
                elif name == "begin":
                    begin()
                elif name == "scan":
                    scan(which)
                elif name == "add":
                    add_states(which)
                elif name == "y_out":
                    y_out(which)
                elif name in MID_NAMES:
                    middle(name, which)
                elif name != "pre":
                    step(name, which)
            for th in range(NG):
                experts(th)


_OUTS = [((4, 256, 256), "float32")]


def kernel(**inputs):
    import numpy as np
    import ml_dtypes
    import concourse.bacc as bacc
    from concourse.bass_utils import run_bass_kernel_spmd

    v = {k: np.asarray(a) for k, a in inputs.items()}
    wide = np.zeros((D, 104), np.float32)
    xp = v["L0_xattn_x_proj_w"]
    for r in range(3):
        wide[:, 32 * r:32 * r + 2 * DS] = xp[DR:].T
    wide[:, 96:96 + DR] = xp[:DR].T

    def side_by_side(shared, routed):
        return np.concatenate([shared, routed], axis=0)

    wv = v["L0_attn_Wv"].reshape(D, 2, HH // 2, 2, DH).transpose(0, 3, 2, 1, 4).reshape(D, D)
    w1 = np.zeros((D, FP), np.float32)
    w1[:, :NX * DFF] = side_by_side(v["L0_ffn_shared_w1"], v["L0_ffn_routed_w1"]).transpose(1, 0, 2).reshape(D, NX * DFF)
    b1 = np.zeros((FP,), np.float32)
    b1[:NX * DFF] = side_by_side(v["L0_ffn_shared_b1"], v["L0_ffn_routed_b1"]).reshape(-1)
    w2 = np.zeros((FP, D), np.float32)
    w2[:NX * DFF] = side_by_side(v["L0_ffn_shared_w2"], v["L0_ffn_routed_w2"]).reshape(NX * DFF, D)
    b2 = side_by_side(v["L0_ffn_shared_b2"], v["L0_ffn_routed_b2"])

    const = np.zeros((P, C_ALL), np.float32)
    row, col = np.arange(P)[:, None], np.arange(P)[None, :]
    c16 = np.arange(C)[None, :]
    const[:, C_ID:C_ID + P] = row == col
    const[:, C_BLK:C_BLK + P] = row // DH == col // DH
    const[:, C_E:C_E + C] = row % C == c16
    const[:, C_MA:C_MA + C] = c16 > row % C
    const[:, C_MP:C_MP + C] = c16 >= row % C
    const[:, C_BIAS + BI_ONE] = 1.0
    const[:, C_BIAS + BI_EPS] = EPS
    const[:, C_BIAS + BI_K] = 0.5 * SCALE_LOG2 * LN2
    const[:, C_BIAS + BI_Q] = 0.5 * SCALE_LOG2 * LN2 - 2 * LN2
    lmask = np.tile((np.arange(NE)[None, :] < np.arange(NE)[:, None]).reshape(1, -1), (P, 1)).astype(np.float32)
    eye3 = (np.arange(96)[:, None] % 32 == np.arange(2 * DS)[None, :]).astype(ml_dtypes.bfloat16)
    sel = (np.arange(96)[:, None] % 32 == np.arange(FP)[None, :] // DFF).astype(ml_dtypes.bfloat16)

    arrays = {
        "x_tok": v["x"].reshape(T, D),
        "x_t": v["x"].reshape(T, D).T,
        "ctx_t": v["ctx_1024"].reshape(T, DM).T,
        "wqkvb": np.concatenate([v["L0_attn_Wq"], v["L0_attn_Wk"], wv, v["L0_attn_Wb"]], axis=1),
        "onorm": np.tile(v["L0_attn_o_norm_weight"], HH).reshape(P, 1),
        "wo": v["L0_attn_Wo"],
        "inproj": v["L0_xattn_in_proj_w"].T,
        "convw": v["L0_xattn_conv_w"],
        "convb": v["L0_xattn_conv_b"].reshape(2, P).T,
        "xproj": wide,
        "dtproj": v["L0_xattn_dt_proj_w"].T,
        "dtb": v["L0_xattn_dt_proj_b"].reshape(2, P).T,
        "alog": v["L0_xattn_A_log"],
        "dskip": v["L0_xattn_D"].reshape(2, P).T,
        "w1": w1,
        "b1": b1.reshape(FT, P).T,
        "w2": w2,
        "b2": b2,
        "cent": v["L0_ffn_centroids"].T,
        "ebias": v["L0_ffn_bias"],
        "const": const,
        "eye3": eye3,
        "sel": sel,
        "lmask": lmask,
    }
    arrays = {f"in_{k}": np.ascontiguousarray(a) for k, a in arrays.items()}
    nc = bacc.Bacc("TRN2", target_bir_lowering=False, num_devices=1)
    args = [nc.dram_tensor(k, a.shape, mybir.dt.from_np(a.dtype), kind="ExternalInput").ap() for k, a in arrays.items()]
    out = nc.dram_tensor("out_0", (T, D), F32, kind="ExternalOutput").ap()
    decoder_layer(nc, *args, out)
    r = run_bass_kernel_spmd(nc, [arrays], core_ids=[0])
    return r.results[0]["out_0"].reshape(B, L, D)
```
